# Optimizing a Trainium2 kernel written in Bass

```python
import numpy as np
import jax
import jax.numpy as jnp

def _softmax(x, axis=-1):
    return jax.nn.softmax(x, axis=axis)

def _gelu(x):
    return jax.nn.gelu(x, approximate=True)

def _silu(x):
    return jax.nn.silu(x)

def _sigmoid(x):
    return jax.nn.sigmoid(x)

def _layernorm(x, axis=-1, eps=1e-05):
    m = jnp.mean(x, axis=axis, keepdims=True)
    v = jnp.var(x, axis=axis, keepdims=True)
    return (x - m) / jnp.sqrt(v + eps)

def _scatter_add(tgt, idx, src, axis=0):
    return tgt.at[idx].add(src)

def _segment_sum(src, seg, n):
    return jax.ops.segment_sum(src, seg, n)
kernel_name = 'mk_perceiver_d1_seqx_r4_5b818a'

def setup_inputs(seed: int=0):
    np.random.seed(seed)
    _w = jnp.asarray

    def _rec_inputs():
        import jax
        import jax.numpy as jnp
        _rk = jax.random.key(seed)
        x = -0.0002928 + 1 * jax.random.normal(jax.random.fold_in(_rk, 1), (2, 256, 256), jnp.float32)
        _lenS = 256 - jax.random.randint(jax.random.fold_in(_rk, 7), (2,), 0, max(1, 256 // 4) + 1, jnp.int32)
        _lenS2 = 4096 - jax.random.randint(jax.random.fold_in(_rk, 8), (2,), 0, max(1, 4096 // 4) + 1, jnp.int32)
        _ctx_1024P = jax.random.normal(jax.random.fold_in(_rk, 11), (2, 16, 256), jnp.float32)
        _ctx_1024c = jax.random.dirichlet(jax.random.fold_in(_rk, 511), 0.3 * jnp.ones((16,), jnp.float32), (2, 4096))
        _ctx_1024t = jnp.einsum('bsk,bkd->bsd', _ctx_1024c, _ctx_1024P)
        _ctx_1024t = _ctx_1024t * jax.lax.rsqrt(jnp.mean(jnp.square(_ctx_1024t)) + 1e-12) * 0.953939
        ctx_1024 = 4.13588e-05 + 0.999923 * (_ctx_1024t + 0.3 * jax.random.normal(jax.random.fold_in(_rk, 611), (2, 4096, 256), jnp.float32))
        return (x, ctx_1024)
    x, ctx_1024 = _rec_inputs()

    def _L0_xattn_setup():
        import jax, jax.numpy as jnp
        import numpy as np
        HIDDEN = 256
        HEADS = 16
        HEAD_DIM = 64
        key = jax.random.key(seed)
        ks = jax.random.split(key, 7)
        B, Q, K = (2, 512, 1024)
        s = 1.0 / np.sqrt(HIDDEN)
        return {'query': jax.random.normal(ks[0], (B, Q, HIDDEN), dtype=jnp.float32), 'key': jax.random.normal(ks[1], (B, K, HIDDEN), dtype=jnp.float32), 'value': jax.random.normal(ks[2], (B, K, HIDDEN), dtype=jnp.float32), 'w_q': jax.random.normal(ks[3], (HIDDEN, HEADS * HEAD_DIM), dtype=jnp.float32) * s, 'w_k': jax.random.normal(ks[4], (HIDDEN, HEADS * HEAD_DIM), dtype=jnp.float32) * s, 'w_v': jax.random.normal(ks[5], (HIDDEN, HEADS * HEAD_DIM), dtype=jnp.float32) * s, 'w_o': jax.random.normal(ks[6], (HEADS * HEAD_DIM, HIDDEN), dtype=jnp.float32) * s}
    _L0_xattn_all = _L0_xattn_setup()
    _L0_xattn_in = {k: v for k, v in _L0_xattn_all.items() if k in ('w_q', 'w_k', 'w_v', 'w_o')}
    del _L0_xattn_all

    def _L0_attn_setup():
        import jax, jax.numpy as jnp
        import numpy as np
        D_MODEL = 256
        NUM_HEADS = 16
        HEAD_DIM = D_MODEL // NUM_HEADS
        CURVATURE = 1.0

        def _hyperbolic_distance(q, k, c):
            q_norm_sq = jnp.sum(q * q, axis=-1, keepdims=True)
            k_norm_sq = jnp.sum(k * k, axis=-1)[..., None, :]
            qk = jnp.einsum('bhnd,bhmd->bhnm', q, k)
            diff_sq = q_norm_sq + k_norm_sq - 2.0 * qk
            denom = (1.0 - c * q_norm_sq) * (1.0 - c * k_norm_sq)
            denom = jnp.maximum(denom, 1e-06)
            cosh_arg = 1.0 + 2.0 * c * diff_sq / denom
            cosh_arg = jnp.maximum(cosh_arg, 1.0)
            return jnp.arccosh(cosh_arg)
        key = jax.random.key(seed)
        kx, kq, kk, kv, ko = jax.random.split(key, 5)
        B, N = (2, 512)
        s = 1.0 / np.sqrt(D_MODEL)
        return {'x': jax.random.normal(kx, (B, N, D_MODEL), dtype=jnp.float32), 'wq': jax.random.normal(kq, (D_MODEL, D_MODEL), dtype=jnp.float32) * s, 'wk': jax.random.normal(kk, (D_MODEL, D_MODEL), dtype=jnp.float32) * s, 'wv': jax.random.normal(kv, (D_MODEL, D_MODEL), dtype=jnp.float32) * s, 'wo': jax.random.normal(ko, (D_MODEL, D_MODEL), dtype=jnp.float32) * s}
    _L0_attn_all = _L0_attn_setup()
    _L0_attn_in = {k: v for k, v in _L0_attn_all.items() if k in ('wq', 'wk', 'wv', 'wo')}
    del _L0_attn_all

    def _L0_ffn_setup():
        import jax, jax.numpy as jnp
        import numpy as np
        H = 256
        I = 256
        E = 8
        key = jax.random.key(seed)
        ks = jax.random.split(key, 8)
        s = 0.02
        x = jax.random.normal(ks[0], (4, 512, H), dtype=jnp.float32)
        Wg = jax.random.normal(ks[1], (H, E), dtype=jnp.float32) * s
        bg = jnp.zeros((E,), dtype=jnp.float32)
        W1 = jax.random.normal(ks[2], (E, H, I), dtype=jnp.float32) * s
        b1 = jnp.zeros((E, I), dtype=jnp.float32)
        W2 = jax.random.normal(ks[3], (E, I, H), dtype=jnp.float32) * s
        b2 = jnp.zeros((E, H), dtype=jnp.float32)
        return {'x': x, 'Wg': Wg, 'bg': bg, 'W1': W1, 'b1': b1, 'W2': W2, 'b2': b2}
    _L0_ffn_all = _L0_ffn_setup()
    _L0_ffn_in = {k: v for k, v in _L0_ffn_all.items() if k in ('Wg', 'bg', 'W1', 'b1', 'W2', 'b2')}
    del _L0_ffn_all
    return {'x': x, 'ctx_1024': ctx_1024, 'L0_xattn_w_q': _L0_xattn_in['w_q'], 'L0_xattn_w_k': _L0_xattn_in['w_k'], 'L0_xattn_w_v': _L0_xattn_in['w_v'], 'L0_xattn_w_o': _L0_xattn_in['w_o'], 'L0_attn_wq': _L0_attn_in['wq'], 'L0_attn_wk': _L0_attn_in['wk'], 'L0_attn_wv': _L0_attn_in['wv'], 'L0_attn_wo': _L0_attn_in['wo'], 'L0_ffn_Wg': _L0_ffn_in['Wg'], 'L0_ffn_bg': _L0_ffn_in['bg'], 'L0_ffn_W1': _L0_ffn_in['W1'], 'L0_ffn_b1': _L0_ffn_in['b1'], 'L0_ffn_W2': _L0_ffn_in['W2'], 'L0_ffn_b2': _L0_ffn_in['b2']}

def reference(x, ctx_1024, L0_xattn_w_q, L0_xattn_w_k, L0_xattn_w_v, L0_xattn_w_o, L0_attn_wq, L0_attn_wk, L0_attn_wv, L0_attn_wo, L0_ffn_Wg, L0_ffn_bg, L0_ffn_W1, L0_ffn_b1, L0_ffn_W2, L0_ffn_b2):
    import jax
    import jax.numpy as jnp

    def _L0_xattn_ref(query, key, value, w_q, w_k, w_v, w_o):
        import jax, jax.numpy as jnp
        import numpy as np
        HIDDEN = 256
        HEADS = 16
        HEAD_DIM = 64
        B, Q, _ = query.shape
        Kl = key.shape[1]
        scale = HEAD_DIM ** (-0.5)
        q = (query @ w_q).reshape(B, Q, HEADS, HEAD_DIM).transpose(0, 2, 1, 3)
        k = (key @ w_k).reshape(B, Kl, HEADS, HEAD_DIM).transpose(0, 2, 1, 3)
        v = (value @ w_v).reshape(B, Kl, HEADS, HEAD_DIM).transpose(0, 2, 1, 3)
        scores = jnp.einsum('bhqd,bhkd->bhqk', q, k) * scale
        attn = jax.nn.softmax(scores, axis=-1)
        out = jnp.einsum('bhqk,bhkd->bhqd', attn, v)
        out = out.transpose(0, 2, 1, 3).reshape(B, Q, HEADS * HEAD_DIM)
        return out @ w_o

    def _L0_attn_ref(x, wq, wk, wv, wo):
        import jax, jax.numpy as jnp
        import numpy as np
        D_MODEL = 256
        NUM_HEADS = 16
        HEAD_DIM = D_MODEL // NUM_HEADS
        CURVATURE = 1.0

        def _hyperbolic_distance(q, k, c):
            q_norm_sq = jnp.sum(q * q, axis=-1, keepdims=True)
            k_norm_sq = jnp.sum(k * k, axis=-1)[..., None, :]
            qk = jnp.einsum('bhnd,bhmd->bhnm', q, k)
            diff_sq = q_norm_sq + k_norm_sq - 2.0 * qk
            denom = (1.0 - c * q_norm_sq) * (1.0 - c * k_norm_sq)
            denom = jnp.maximum(denom, 1e-06)
            cosh_arg = 1.0 + 2.0 * c * diff_sq / denom
            cosh_arg = jnp.maximum(cosh_arg, 1.0)
            return jnp.arccosh(cosh_arg)
        B, N, D = x.shape
        H, Dh = (NUM_HEADS, HEAD_DIM)
        q = (x @ wq.T).reshape(B, N, H, Dh).transpose(0, 2, 1, 3)
        k = (x @ wk.T).reshape(B, N, H, Dh).transpose(0, 2, 1, 3)
        v = (x @ wv.T).reshape(B, N, H, Dh).transpose(0, 2, 1, 3)
        dist = _hyperbolic_distance(q, k, CURVATURE)
        attn = jax.nn.softmax(-dist, axis=-1)
        out = jnp.einsum('bhnm,bhmd->bhnd', attn, v)
        out = out.transpose(0, 2, 1, 3).reshape(B, N, D)
        return out @ wo.T

    def _L0_ffn_ref(x, Wg, bg, W1, b1, W2, b2):
        import jax, jax.numpy as jnp
        import numpy as np
        H = 256
        I = 256
        E = 8
        B, S, Hd = x.shape
        xf = x.reshape(-1, Hd)
        logits = xf @ Wg + bg
        gates = jax.nn.softmax(logits, axis=-1)
        idx = jnp.argmax(gates, axis=-1)
        h = jax.nn.gelu(jnp.einsum('th,ehi->tei', xf, W1) + b1, approximate=False)
        y = jnp.einsum('tei,eih->teh', h, W2) + b2
        out = jnp.take_along_axis(y, idx[:, None, None], axis=1)[:, 0, :]
        return out.reshape(B, S, Hd)
    x = x + _L0_xattn_ref(_layernorm(x, axis=-1), ctx_1024, ctx_1024, L0_xattn_w_q, L0_xattn_w_k, L0_xattn_w_v, L0_xattn_w_o)
    x = x + _L0_attn_ref(_layernorm(x, axis=-1), L0_attn_wq, L0_attn_wk, L0_attn_wv, L0_attn_wo)
    x = x + _L0_ffn_ref(_layernorm(x, axis=-1), L0_ffn_Wg, L0_ffn_bg, L0_ffn_W1, L0_ffn_b1, L0_ffn_W2, L0_ffn_b2)
    return x

_drawn_inputs = setup_inputs


def setup_inputs(seed=0):
    import zlib

    import numpy as np

    out = dict(_drawn_inputs(seed))
    spreads = {'L0_ffn_bg': (0.0, 0.1), 'L0_ffn_b1': (0.0, 0.709), 'L0_ffn_b2': (0.0, 0.1)}
    factors = {'L0_attn_wq': 7.882, 'L0_attn_wk': 6.671}
    for name, (base, spread) in spreads.items():
        noise = np.random.default_rng([zlib.crc32(name.encode()), seed]).standard_normal(out[name].shape)
        drawn = base * np.exp(spread * noise) if base else spread * noise
        out[name] = jnp.asarray(drawn.astype(out[name].dtype))
    for name, factor in factors.items():
        out[name] = (out[name] * factor).astype(out[name].dtype)
    return out
```

```python
from contextlib import ExitStack

import concourse.bass as bass
from concourse import mybir

FP32 = mybir.dt.float32
FP16 = mybir.dt.float16
BF16 = mybir.dt.bfloat16
ALU = mybir.AluOpType
ACT = mybir.ActivationFunctionType
AX = mybir.AxisListType

P = 128
B, TQ, TK, D = 2, 256, 4096, 256
T = B * TQ
NT = T // P
NC = D // P
XH, XD = 16, 64
HP = XH // 2
STEPS = HP * B
SLOTS = TK // (2 * P)
KCH = TK // 512
WS = 16.0
XSCALE = XD ** -0.5 / WS
SH, SD = 16, 16
E, F = 8, 256
EPS = 1e-5
LN = 9

SC = (0, 2)
ACC = 4
MX = 5
PJ = 7

EARLY = {0: ("q", 0), 2: ("sum", 0), 14: ("m", 0)}
LATE = {0: ("k", 0), 1: ("k", 1), 2: ("k", 2), 3: ("k", 3), 4: ("v", 0), 5: ("k", 4), 6: ("v", 1),
        7: ("k", 5), 8: ("v", 2), 9: ("k", 6), 10: ("v", 3), 11: ("k", 7), 12: ("v", 4),
        13: ("v", 5), 14: ("v", 6), 15: ("v", 7)}
MAX_A = {1: 0, 2: 2, 3: 4, 4: 6, 5: 7, 6: 8, 7: 9, 8: 10, 9: 11, 10: 12, 11: 13, 12: 14}
MAX_B = {1: 1, 2: 3, 3: 5, 12: 15}
NU = 2 * KCH
SPLIT_SLOT = 8
NP = 4


def perceiver(nc, x, ctx, wq, wk, wv, wo, aq, ak, av, ao, gw, gb, w1, b1, w2, b2, out):
    stack = ExitStack()

    def sb(name, shape, dt=FP32):
        return stack.enter_context(nc.sbuf_tensor(name, shape, dt))

    def sem(name):
        return stack.enter_context(nc.semaphore(name))

    with stack:
        ps = stack.enter_context(nc.psum_tensor("ps", [P, 8, 512], FP32))
        ctx_hi = sb("ctx_hi", [P, NC, B, TK], FP16)
        ctx_lo = sb("ctx_lo", [P, NC, B, TK], FP16)
        k_hi = sb("k_hi", [P, B, TK], FP16)
        k_lo = sb("k_lo", [P, B, TK], FP16)
        v_sb = sb("v_sb", [P, B, TK // P, P])
        probs = sb("probs", [P, NP, 2, 2, TQ])
        psums = sb("psums", [P, B, 2, 2, TQ])
        o_all = sb("o_all", [P, HP, T])
        o_raw = sb("o_raw", [P, TQ])
        o_rec = sb("o_rec", [P, TQ])
        x_sb = sb("x_sb", [P, NT, D])
        xn = sb("xn", [P, NT, D])
        xnT = sb("xnT", [P, NC, T])
        w_raw = sb("w_raw", [P, B, 3, NC, P])
        w_hi = sb("w_hi", [P, B, 2, NC, P], FP16)
        w_lo = sb("w_lo", [P, B, 2, NC, P], FP16)
        q_hi = sb("q_hi", [P, B, TQ], FP16)
        q_lo = sb("q_lo", [P, B, TQ], FP16)
        m_part = sb("m_part", [P, KCH, 2, 2])
        m_neg = sb("m_neg", [P, 2, P], BF16)
        m_row = sb("m_row", [P, B, TQ], BF16)
        ident = sb("ident", [P, P])
        ident_b = sb("ident_b", [P, P], BF16)
        ones_b = sb("ones_b", [P, P], BF16)
        sixteen = sb("sixteen", [P, XD])
        stats = sb("stats", [P, NT, 6])
        mv = sb("mv", [P, NT, 2])
        rstd = sb("rstd", [P, NT])
        var = sb("var", [P, NT])
        newton = sb("newton", [P, NT])

        stage = probs[:, :, :, :, :].rearrange("p (n a) h k q -> p n (a h k q)", n=2) \
            .rearrange("p n (t c) -> p n t c", c=D)

        hi32 = ctx_hi[:, :, :, :].rearrange("p c b k -> p (c b k)").bitcast(FP32)
        lo32 = ctx_lo[:, :, :, :].rearrange("p c b k -> p (c b k)").bitcast(FP32)
        w1_sb = hi32[:, 0:4096].rearrange("p (e c n) -> p e c n", e=E, c=NC)
        w2_sb = hi32[:, 4096:8192].rearrange("p (e c n) -> p e c n", e=E, c=NC)
        wo_sb = lo32[:, 0:2048].rearrange("p (h n) -> p h n", h=HP)
        a_raw = lo32[:, 2048:4096].rearrange("p (w t n) -> p w t n", w=4, t=NC)
        aqk_T = lo32[:, 4096:6144].rearrange("p (w c h d) -> p w c h d", w=2, c=NC, h=SH)
        avo_T = lo32[:, 6144:7168].rearrange("p (w c n) -> p w c n", w=2, c=NC)
        k32 = k_hi[:, :, :].rearrange("p b k -> p (b k)").bitcast(FP32)
        d32 = k_lo[:, :, :].rearrange("p b k -> p (b k)").bitcast(FP32)
        qx = k32[:, 0:2048].rearrange("p (g t) -> p g t", g=4)
        kx = k32[:, 2048:4096].rearrange("p (g t) -> p g t", g=4)
        dq = d32[:, 0:2048].rearrange("p (g t) -> p g t", g=4)
        dk = d32[:, 2048:4096].rearrange("p (g t) -> p g t", g=4)
        v32 = v_sb[:, :, :, :].rearrange("p b k n -> p (b k n)")
        ratio = v32[:, 0:2048].rearrange("p (n h q) -> p n h q", n=2, h=4)
        root0 = v32[:, 2048:4096].rearrange("p (n h q) -> p n h q", n=2, h=4)
        root2 = v32[:, 4096:6144].rearrange("p (n h q) -> p n h q", n=2, h=4)
        square = v32[:, 6144:7168].rearrange("p (n t) -> p n t", n=2)
        p32 = probs[:, :, :, :, :].rearrange("p n h k q -> p (n h k q)")
        weight = p32[:, 0:4096].rearrange("p (n k h q) -> p n k h q", n=2, k=2, h=4)
        hid = v32[:, 0:1024].rearrange("p (n t) -> p n t", n=2)
        hid_m = v32[:, 1024:2048].rearrange("p (n t) -> p n t", n=2)
        s32 = psums[:, :, :, :, :].rearrange("p b h k q -> p (b h k q)")
        vx = s32[:, 0:NT * SH * (SD + 1)].rearrange("p (t h d) -> p t h d", t=NT, h=SH)
        orec = s32[:, 1536:1600].rearrange("p (b t h) -> p b t h", b=B, t=2)
        sel = sb("sel", [P, 3, P])
        vecs = sb("vecs", [P, 6])
        sel_e = sb("sel_e", [E, E, P])
        ones1 = sb("ones1", [1, P])
        rank = sb("rank", [P, NT, E])
        gw_sb = sb("gw_sb", [P, NC, E])
        gb_sb = sb("gb_sb", [1, E])
        b1_raw = sb("b1_raw", [E * NC, P])
        b1_T = sb("b1_T", [P, E * NC])
        b2_sb = sb("b2_sb", [E, D])
        lg = sb("lg", [P, NT, E])
        ge = sb("ge", [P, NT, E])
        best = sb("best", [P, NT, E])
        gs = sb("gs", [P, 4, NT])
        best_T = sb("best_T", [E, T])


        s_const = sem("s_const")
        s_x = sem("s_x")
        s_ctx = [sem("s_ctx0"), sem("s_ctx1")]
        s_w = [sem("s_w0"), sem("s_w1")]
        s_ln = sem("s_ln")
        s_sd = sem("s_sd")
        s_xt = sem("s_xt")
        s_xc = sem("s_xc")
        s_tp = sem("s_tp")
        s_th = sem("s_th")
        s_tl = sem("s_tl")
        s_wh = sem("s_wh")
        s_wl = sem("s_wl")
        s_q = sem("s_q")
        s_k = sem("s_k")
        s_v = sem("s_v")
        s_mx = sem("s_mx")
        s_mt = sem("s_mt")
        s_sc = sem("s_sc")
        s_pv = sem("s_pv")
        s_sum = sem("s_sum")
        s_qh = sem("s_qh")
        s_kh = sem("s_kh")
        s_vc = sem("s_vc")
        s_mr = sem("s_mr")
        s_exp = sem("s_exp")
        s_ql = sem("s_ql")
        s_kl = sem("s_kl")
        s_red = sem("s_red")
        s_mf = sem("s_mf")
        s_mn = sem("s_mn")
        s_or = sem("s_or")
        s_rs = sem("s_rs")
        s_on = sem("s_on")
        s_ps = sem("s_ps")
        s_aw = sem("s_aw")
        s_ew = sem("s_ew")
        s_small = sem("s_small")
        s_out = sem("s_out")
        s_tc = sem("s_tc")
        s_vec = sem("s_vec")
        s_vone = sem("s_vone")
        s_at = sem("s_at")
        s_ac = sem("s_ac")
        s_y = sem("s_y")
        s_x1 = sem("s_x1")
        s_qk = sem("s_qk")
        s_sq = sem("s_sq")
        s_nm = sem("s_nm")
        s_qx = sem("s_qx")
        s_dx = sem("s_dx")
        s_vp = sem("s_vp")
        s_vx = sem("s_vx")
        s_dd = sem("s_dd")
        s_rt = sem("s_rt")
        s_r2 = sem("s_r2")
        s_ra = sem("s_ra")
        s_iv = sem("s_iv")
        s_wt = sem("s_wt")
        s_o = sem("s_o")
        s_on2 = sem("s_on2")
        s_gl = sem("s_gl")
        s_g = sem("s_g")
        s_ge = sem("s_ge")
        s_bt = sem("s_bt")
        s_bc = sem("s_bc")
        s_h = sem("s_h")
        s_hg = sem("s_hg")
        s_hm = sem("s_hm")
        s_dv = sem("s_dv")

        def at_least(eng, semaphore, count):
            if not (isinstance(count, int) and count <= 0):
                eng.wait_ge(semaphore, count)

        def slot_of(hp, b, s):
            return hp * (B * SLOTS) + (b * SLOTS + s)

        def step_of(hp, b):
            return hp * B + b

        def summed(n, s):
            if s < 0:
                return n * (SLOTS - 1) + s + 1
            return n * (SLOTS - 1) + max(s, 1)

        def first_step(hp, b):
            return isinstance(hp, int) and hp == 0 and b == 0

        def prepares(hp, b):
            return not (isinstance(hp, int) and hp == HP - 1 and b == B - 1)

        def attn_units():
            return [((b * 4 + g) * 2 + kt, b, g, kt) for b in range(B) for g in range(4)
                    for kt in range(2)]

        def tail_sp(sp):
            sp.dma_start(gw_sb[:, :, :], gw.rearrange("(c p) e -> p c e", p=P)).then_inc(s_small, 16)
            sp.dma_start(gb_sb[:, :], gb.rearrange("(a e) -> a e", a=1)).then_inc(s_small, 16)
            sp.dma_start(b1_raw[:, :], b1.rearrange("e (i p) -> (e i) p", p=P)).then_inc(s_small, 16)
            sp.dma_start(b2_sb[:, :], b2).then_inc(s_small, 16)
            sp.wait_ge(s_v, STEPS * KCH)
            for i, w in enumerate((aq, ak, av, ao)):
                sp.dma_start(a_raw[:, i, :, :], w.rearrange("(t p) n -> p t n", p=P)).then_inc(s_aw, 16)
            sp.dma_start(wo_sb, wo.rearrange("(h p) n -> p h n", p=P)).then_inc(s_aw, 16)
            for w, w_sb in ((w1, w1_sb), (w2, w2_sb)):
                sp.dma_start(w_sb.rearrange("p e c n -> p (e c) n"),
                             w.rearrange("e (c p) n -> p (e c) n", p=P)).then_inc(s_ew, 16)
            sp.wait_ge(s_x1, 3 * NT)
            sp.dma_start(out.rearrange("b (t p) c -> p (b t) c", p=P), x_sb[:, :, :]).then_inc(s_out, 16)
            sp.wait_ge(s_out, 16)

        def tail_pool(pool):
            nc.gpsimd.memset(sel[:, :, :], 0.0).then_inc(s_tc, 1)
            nc.gpsimd.memset(sel_e[:, :, :], 0.0).then_inc(s_tc, 1)
            nc.gpsimd.memset(ones1[:, :], 1.0).then_inc(s_tc, 1)
            pool.wait_ge(s_tc, 3)
            for i, r in enumerate((16, 17, 0)):
                nc.gpsimd.memset(sel[:, i, r:P:32], 1.0).then_inc(s_tc, 1)
                pool.wait_ge(s_tc, 4 + 3 * i)
                nc.gpsimd.affine_select(out=sel[:, i, r:P:32], in_=sel[:, i, r:P:32],
                                        compare_op=ALU.is_ge, fill=0.0, base=0, pattern=[[-32, 4]],
                                        channel_multiplier=1).then_inc(s_tc, 1)
                pool.wait_ge(s_tc, 5 + 3 * i)
                nc.gpsimd.affine_select(out=sel[:, i, r:P:32], in_=sel[:, i, r:P:32],
                                        compare_op=ALU.is_ge, fill=0.0, base=15, pattern=[[32, 4]],
                                        channel_multiplier=-1).then_inc(s_tc, 1)
                pool.wait_ge(s_tc, 6 + 3 * i)
            nc.gpsimd.affine_select(out=sel_e[:, :, :], in_=sel_e[:, :, :], compare_op=ALU.not_equal,
                                    fill=1.0, base=0, pattern=[[-1, E], [0, P]],
                                    channel_multiplier=1).then_inc(s_tc, 1)
            for e in range(E):
                i = nc.gpsimd.memset(rank[:, :, e], float(E - e))
            i.then_inc(s_tc, 1)
            pool.wait_ge(s_v, STEPS * KCH)
            for w in range(2):
                for c in range(NC):
                    i = nc.gpsimd.memset(aqk_T[:, w, c, :, SD:32], 0.0)
            i.then_inc(s_vone, 1)
            pool.wait_ge(s_sum, STEPS)
            for t in range(NT):
                i = nc.gpsimd.memset(vx[:, t, :, SD:SD + 1], 1.0)
            i.then_inc(s_vone, 1)
            for i in range(len(attn_units())):
                pool.wait_ge(s_r2, i + 1)
                nc.gpsimd.tensor_tensor(root2[:, i % 2, :, :], root0[:, i % 2, :, :],
                                        root2[:, i % 2, :, :], ALU.add).then_inc(s_ra, 1)

        def tail_pe(pe):
            def transposes(src, bank):
                for c in range(NC):
                    for t in range(NT):
                        mm = pe.transpose(ps[:, bank + c, t * P:(t + 1) * P],
                                          src[:, t, c * P:(c + 1) * P], ident[:, :])
                    mm.then_inc(s_xt, 1)

            pe.wait_ge(s_aw, 5 * 16)
            pe.wait_ge(s_exp, STEPS * SLOTS)
            for w in range(4):
                for c in range(NC):
                    for t in range(NC):
                        mm = pe.transpose(ps[:, w, (NC * c + t) * P:(NC * c + t + 1) * P],
                                          a_raw[:, w, t, c * P:(c + 1) * P], ident[:, :])
                mm.then_inc(s_at, 1)
            pe.wait_ge(s_on, STEPS)
            pe.wait_ge(s_ac, 4)
            for t in range(NT):
                for h in range(HP):
                    mm = pe.matmul(ps[:, t, 0:D], o_all[:, h, t * P:(t + 1) * P], wo_sb[:, h, :],
                                   start=(h == 0), stop=(h == HP - 1))
                mm.then_inc(s_y, 1)
            pe.wait_ge(s_ln, 2 * LN)
            transposes(xn, 4)
            pe.wait_ge(s_xc, 2 * NC)
            pe.wait_ge(s_x1, NT)
            for t in range(NT):
                for c in range(NC):
                    mm = pe.matmul(ps[:, t, 0:D], xnT[:, c, t * P:(t + 1) * P], avo_T[:, 0, c, :],
                                   start=(c == 0), stop=(c == NC - 1))
                mm.then_inc(s_vp, 1)
            pe.wait_ge(s_tc, 14)
            pe.wait_ge(s_vone, 1)

            def qk(i):
                w, g = divmod(i, 4)
                bank = 4 + i % 2
                if i >= 2:
                    pe.wait_ge(s_qx, i - 1)
                for c in range(NC):
                    mm = pe.matmul(ps[:, bank, :],
                                   aqk_T[:, w, c, 4 * g:4 * g + 4, :].rearrange("p h d -> p (h d)"),
                                   xnT[:, c, :], start=(c == 0), stop=(c == NC - 1))
                mm.then_inc(s_qk, 1)

            def lengths(i):
                w, g = divmod(i, 4)
                pe.wait_ge(s_sq, i + 1)
                pe.matmul(ps[:, 4 + i % 2, :], sel[:, w, :], square[:, i % 2, :],
                          start=False, stop=True, skip_group_check=True)
                if i >= 2:
                    pe.wait_ge(s_dx, i - 1)
                pe.matmul(ps[:, 6 + i % 2, :], sel[:, 2, :], square[:, i % 2, :],
                          start=True, stop=True).then_inc(s_nm, 1)

            for i in range(9):
                if i < 8:
                    qk(i)
                if i >= 1:
                    lengths(i - 1)
            pe.wait_ge(s_vx, NT)

            def distances(i, b, g, kt):
                if i == 0:
                    pe.wait_ge(s_qx, 8)
                    pe.wait_ge(s_dx, 8)
                else:
                    pe.wait_ge(s_rt, 3 * i)
                keys = slice((2 * b + kt) * P, (2 * b + kt + 1) * P)
                for half, left, right in ((0, kx, qx), (1, dk, dq)):
                    for j in range(4):
                        mm = pe.matmul(ps[:, j, half * TQ:(half + 1) * TQ],
                                       left[32 * j:32 * j + 32, g, keys],
                                       right[32 * j:32 * j + 32, g, b * TQ:(b + 1) * TQ],
                                       start=True, stop=True)
                mm.then_inc(s_dd, 1)

            def average(i, b, g):
                pe.wait_ge(s_wt, i + 1)
                for j in range(4):
                    for t in range(2):
                        for kt in range(2):
                            col = (4 * g + j) * (SD + 1)
                            mm = pe.matmul(ps[:, 4 + 2 * b + t, col:col + SD + 1],
                                           weight[:, g % 2, kt, j, t * P:(t + 1) * P],
                                           vx[:, 2 * b + kt, 4 * g + j, :],
                                           start=(kt == 0), stop=(kt == 1))
                mm.then_inc(s_o, 1)

            units = attn_units()
            for n, (i, b, g, kt) in enumerate(units):
                distances(i, b, g, kt)
                if i >= 2 and kt == 0:
                    average(i - 1, *units[n - 1][1:3])
            average(15, B - 1, 3)
            pe.wait_ge(s_on2, B)
            transposes(xn, 0)
            pe.wait_ge(s_xc, 3 * NC)
            for t in range(NT):
                for c in range(NC):
                    mm = pe.matmul(ps[:, t, 0:D], xnT[:, c, t * P:(t + 1) * P], avo_T[:, 1, c, :],
                                   start=(c == 0), stop=(c == NC - 1))
                mm.then_inc(s_y, 1)

            pe.wait_ge(s_small, 64)
            pe.transpose(ps[:, 7, 0:E * NC], b1_raw[:, :], ident[0:E * NC, 0:E * NC]).then_inc(s_bt, 1)
            pe.wait_ge(s_ln, 3 * LN)
            transposes(xn, 4)
            pe.wait_ge(s_xc, 4 * NC)
            for t in range(NT):
                for c in range(NC):
                    pe.matmul(ps[:, 6, t * E:(t + 1) * E], xnT[:, c, t * P:(t + 1) * P],
                              gw_sb[:, c, :], start=(c == 0), stop=False)
                mm = pe.matmul(ps[:, 6, t * E:(t + 1) * E], ones1[:, :], gb_sb[:, :],
                               start=False, stop=True)
            mm.then_inc(s_gl, 1)
            pe.wait_ge(s_ew, 32)
            pe.wait_ge(s_x1, 2 * NT)
            pe.wait_ge(s_bc, 1)

            def hidden(i):
                e, it = divmod(i, NC)
                if i >= 2:
                    pe.wait_ge(s_hg, i - 1)
                for c in range(NC):
                    mm = pe.matmul(ps[:, 4 + i % 2, :], w1_sb[:, e, c, it * P:(it + 1) * P],
                                   xnT[:, c, :], start=(c == 0), stop=(c == NC - 1))
                mm.then_inc(s_h, 1)
                if it == 0:
                    if e >= 2:
                        pe.wait_ge(s_hm, NC * (e - 1))
                    pe.matmul(ps[:, 6 + e % 2, :], sel_e[:, e, :], best_T[:, :],
                              start=True, stop=True).then_inc(s_bt, 1)

            def outer(i):
                e, it = divmod(i, NC)
                pe.wait_ge(s_hm, i + 1)
                for t in range(NT):
                    mm = pe.matmul(ps[:, t, 0:D], hid_m[:, i % 2, t * P:(t + 1) * P],
                                   w2_sb[:, e, it, :], start=False, stop=(i == E * NC - 1))
                mm.then_inc(s_y, 1)

            pe.wait_ge(s_g, 10)
            for t in range(NT):
                mm = pe.transpose(ps[0:E, 7, t * P:(t + 1) * P], best[:, t, :], ident[:, :])
            mm.then_inc(s_bt, 1)
            pe.wait_ge(s_bc, 2)
            for t in range(NT):
                pe.matmul(ps[:, t, 0:D], best_T[:, t * P:(t + 1) * P], b2_sb[:, :],
                          start=True, stop=False)
            for i in range(E * NC + 1):
                if i < E * NC:
                    hidden(i)
                if i >= 1:
                    outer(i - 1)

        def root_of_variance(act, part):
            act.wait_ge(s_ln, LN * part + 3)
            nc.scalar.activation(rstd[:, :], var[:, :], ACT.Sqrt).then_inc(s_sd, 1)

        def tail_act(act):
            act.wait_ge(s_at, 2)
            act.wait_ge(s_vone, 1)
            for w in range(2):
                nc.scalar.activation(
                    aqk_T[:, w, :, :, 0:SD].rearrange("p c h d -> p (c h) d"),
                    ps[:, w, :].rearrange("p (h d) -> p h d", d=SD), ACT.Copy).then_inc(s_ac, 1)
            act.wait_ge(s_at, 4)
            for w in range(2):
                nc.scalar.activation(avo_T[:, w, :, :].rearrange("p c n -> p (c n)"), ps[:, 2 + w, :],
                                     ACT.Copy).then_inc(s_ac, 1)

            def take_xnT(base, bank):
                act.wait_ge(s_xt, base + NC)
                for c in range(NC):
                    nc.scalar.activation(xnT[:, c, :], ps[:, bank + c, :], ACT.Copy).then_inc(s_xc, 1)

            root_of_variance(act, 1)
            take_xnT(NC, 4)
            act.wait_ge(s_vp, NT)
            act.wait_ge(s_vone, 2)
            for t in range(NT):
                nc.scalar.activation(vx[:, t, :, 0:SD],
                                     ps[:, t, 0:D].rearrange("p (h d) -> p h d", d=SD),
                                     ACT.Copy).then_inc(s_vx, 1)
            act.wait_ge(s_vec, 1)

            def squares(i):
                act.wait_ge(s_qk, i + 1)
                if i >= 2:
                    act.wait_ge(s_nm, i - 1)
                nc.scalar.activation(square[:, i % 2, :], ps[:, 4 + i % 2, :], ACT.Square) \
                    .then_inc(s_sq, 1)

            def rows(i):
                w, g = divmod(i, 4)
                act.wait_ge(s_nm, i + 1)
                if w == 0:
                    nc.scalar.activation(qx[:, g, :], ps[:, 4 + i % 2, :], ACT.Identity,
                                         bias=vecs[:, 1:2]).then_inc(s_qx, 1)
                else:
                    nc.scalar.activation(kx[:, g, :], ps[:, 4 + i % 2, :], ACT.Identity,
                                         bias=vecs[:, 0:1], scale=vecs[:, 4:5]).then_inc(s_qx, 1)

            for i in range(9):
                if i < 8:
                    squares(i)
                if i >= 1:
                    rows(i - 1)

            def roots(i):
                act.wait_ge(s_rt, 3 * i + 3)
                if i >= 2:
                    act.wait_ge(s_wt, i - 1)
                nc.scalar.activation(root0[:, i % 2, :, :], ratio[:, i % 2, :, :], ACT.Sqrt, scale=2.0)
                nc.scalar.activation(root2[:, i % 2, :, :], ratio[:, i % 2, :, :], ACT.Sqrt, scale=2.0,
                                     bias=vecs[:, 5:6]).then_inc(s_r2, 1)

            def weights(i, g, kt):
                act.wait_ge(s_iv, i + 1)
                if i >= 4 and kt == 0:
                    act.wait_ge(s_o, i // 2 - 1)
                nc.scalar.activation(weight[:, g % 2, kt, :, :], root0[:, i % 2, :, :], ACT.Square) \
                    .then_inc(s_wt, 1)

            units = attn_units()
            for n, (i, b, g, kt) in enumerate(units):
                roots(i)
                weights(i, g, kt)
            take_xnT(2 * NC, 0)
            root_of_variance(act, 2)

            act.wait_ge(s_bt, 1)
            nc.scalar.activation(b1_T[:, :], ps[:, 7, 0:E * NC], ACT.Copy).then_inc(s_bc, 1)
            take_xnT(3 * NC, 4)
            act.wait_ge(s_g, 2)
            nc.scalar.activation(ge[:, :, :], lg[:, :, :], ACT.Exp).then_inc(s_ge, 1)
            act.wait_ge(s_bt, 2)
            nc.scalar.activation(best_T[:, :], ps[0:E, 7, :], ACT.Copy).then_inc(s_bc, 1)
            act.wait_ge(s_bc, 1)
            for i in range(E * NC):
                act.wait_ge(s_h, i + 1)
                if i >= 2:
                    act.wait_ge(s_hm, i - 1)
                nc.scalar.activation(hid[:, i % 2, :], ps[:, 4 + i % 2, :], ACT.Gelu,
                                     bias=b1_T[:, i:i + 1]).then_inc(s_hg, 1)

        def tail_dve(dve, layernorm):
            def residual(part, count):
                for t in range(NT):
                    dve.wait_ge(s_y, count(t))
                    nc.vector.tensor_tensor(x_sb[:, t, :], x_sb[:, t, :], ps[:, t, 0:D], ALU.add) \
                        .then_inc(s_x1, 1)
                dve.wait_ge(s_x1, NT * (part + 1))

            dve.wait_ge(s_const, 5)
            for i, r in enumerate((16, 17, 0)):
                nc.vector.tensor_reduce(vecs[:, i:i + 1], ident[:, r:P:32], AX.X, ALU.add)
            nc.vector.tensor_reduce(vecs[:, 3:4], ident[:, :].rearrange("p (j d) -> p j d", d=32)
                                    [:, :, 0:SD], AX.XY, ALU.add).then_inc(s_dv, 1)
            nc.vector.memset(vecs[:, 5:6], 2.0)
            dve.wait_ge(s_dv, 1)
            nc.vector.tensor_scalar(vecs[:, 4:5], vecs[:, 3:4], -3.0, 1.0, ALU.mult, ALU.add) \
                .then_inc(s_vec, 1)
            residual(0, lambda t: t + 1)
            layernorm(1)
            for i in range(8):
                w, g = divmod(i, 4)
                dve.wait_ge(s_nm, i + 1)
                if i == 0:
                    dve.wait_ge(s_vec, 1)
                nc.vector.tensor_scalar((dq, dk)[w][:, g, :], ps[:, 6 + i % 2, :], -1.0,
                                        vecs[:, 2:3], ALU.mult, ALU.add).then_inc(s_dx, 1)

            def ratios(i):
                dve.wait_ge(s_dd, i + 1)
                if i >= 2:
                    dve.wait_ge(s_r2, i - 1)
                nc.vector.tensor_scalar(ratio[:, i % 2, :, :], ps[:, 0:4, TQ:2 * TQ], 1e-6, None,
                                        ALU.max).then_inc(s_rt, 1)
                dve.wait_ge(s_rt, 3 * i + 1)
                nc.vector.reciprocal(ratio[:, i % 2, :, :], ratio[:, i % 2, :, :]).then_inc(s_rt, 1)
                dve.wait_ge(s_rt, 3 * i + 2)
                nc.vector.scalar_tensor_tensor(ratio[:, i % 2, :, :], ps[:, 0:4, 0:TQ], 0.0,
                                               ratio[:, i % 2, :, :], ALU.max, ALU.mult) \
                    .then_inc(s_rt, 1)

            def inverses(i):
                dve.wait_ge(s_ra, i + 1)
                nc.vector.reciprocal(root0[:, i % 2, :, :], root2[:, i % 2, :, :]).then_inc(s_iv, 1)

            def normalise(b, base):
                dve.wait_ge(s_o, 4 * (b + 1))
                o = ps[:, 4 + 2 * b:6 + 2 * b, 0:SH * (SD + 1)].rearrange("p t (h d) -> p t h d", h=SH)
                for t in range(2):
                    i = nc.vector.reciprocal(orec[:, b, t, :], o[:, t, :, SD])
                i.then_inc(s_dv, 1)
                dve.wait_ge(s_dv, base + 1)
                for t in range(2):
                    i = nc.vector.tensor_tensor(
                        xn[:, 2 * b + t, :].rearrange("p (h d) -> p h d", h=SH), o[:, t, :, 0:SD],
                        orec[:, b, t, :].unsqueeze(2).to_broadcast([P, SH, SD]), ALU.mult)
                i.then_inc(s_on2, 1)

            ratios(0)
            for i in range(16):
                if i + 1 < 16:
                    ratios(i + 1)
                inverses(i)
                if i == 9:
                    normalise(0, 1)
            normalise(1, 2)
            residual(1, lambda t: NT + t + 1)
            layernorm(2)

            def per_token(v):
                return v.unsqueeze(2).to_broadcast([P, NT, E])

            dve.wait_ge(s_gl, 1)
            logits = ps[:, 6, 0:NT * E].rearrange("p (t e) -> p t e", e=E)
            nc.vector.tensor_reduce(gs[:, 0, :], logits, AX.X, ALU.max).then_inc(s_g, 1)
            dve.wait_ge(s_g, 1)
            nc.vector.tensor_tensor(lg[:, :, :], logits, per_token(gs[:, 0, :]), ALU.subtract) \
                .then_inc(s_g, 1)
            dve.wait_ge(s_ge, 1)
            nc.vector.tensor_reduce(gs[:, 1, :], ge[:, :, :], AX.X, ALU.add).then_inc(s_g, 1)
            dve.wait_ge(s_g, 3)
            nc.vector.reciprocal(gs[:, 1, :], gs[:, 1, :]).then_inc(s_g, 1)
            dve.wait_ge(s_g, 4)
            nc.vector.tensor_tensor(lg[:, :, :], ge[:, :, :], per_token(gs[:, 1, :]), ALU.mult) \
                .then_inc(s_g, 1)
            dve.wait_ge(s_g, 5)
            nc.vector.tensor_reduce(gs[:, 2, :], lg[:, :, :], AX.X, ALU.max).then_inc(s_g, 1)
            dve.wait_ge(s_g, 6)
            nc.vector.tensor_tensor(best[:, :, :], lg[:, :, :], per_token(gs[:, 2, :]), ALU.is_equal) \
                .then_inc(s_g, 1)
            dve.wait_ge(s_g, 7)
            dve.wait_ge(s_tc, 14)
            nc.vector.tensor_tensor(best[:, :, :], best[:, :, :], rank[:, :, :], ALU.mult) \
                .then_inc(s_g, 1)
            dve.wait_ge(s_g, 8)
            nc.vector.tensor_reduce(gs[:, 3, :], best[:, :, :], AX.X, ALU.max).then_inc(s_g, 1)
            dve.wait_ge(s_g, 9)
            nc.vector.tensor_tensor(best[:, :, :], best[:, :, :], per_token(gs[:, 3, :]),
                                    ALU.is_equal).then_inc(s_g, 1)
            for i in range(E * NC):
                e, it = divmod(i, NC)
                dve.wait_ge(s_hg, i + 1)
                dve.wait_ge(s_bt, 3 + e)
                if i >= 2:
                    dve.wait_ge(s_y, 2 * NT + i - 1)
                nc.vector.tensor_tensor(hid_m[:, i % 2, :], hid[:, i % 2, :], ps[:, 6 + e % 2, :],
                                        ALU.mult).then_inc(s_hm, 1)
            residual(2, lambda t: 2 * NT + E * NC)

        block = stack.enter_context(nc.Block())

        @block.sync
        def _(sp):
            wcols = [w.rearrange("(c p) n -> p c n", p=P) for w in (wq, wk, wv)]

            def load_weights(par, hp):
                for i, w in enumerate(wcols):
                    sp.dma_start(w_raw[:, par, i, :, :], w[:, :, bass.ds(hp * P, P)]) \
                        .then_inc(s_w[par], 16)

            sp.dma_start(x_sb[:, :, :], x.rearrange("b (t p) c -> p (b t) c", p=P)).then_inc(s_x, 16)
            chunks = ctx.rearrange("b (n p t) c -> (b n) p t c", p=P, t=8)
            load_weights(0, 0)
            for n in range(8):
                if n >= 2:
                    sp.wait_ge(s_tp, 4 * (n - 1))
                sp.dma_start(stage[:, n % 2, :, :], chunks[n, :, :, :]).then_inc(s_ctx[n % 2], 16)
                if n == 3:
                    load_weights(1, 0)

            def step(hp, b):
                n = step_of(hp, b)
                sp.wait_ge(s_q, n + 1)
                sp.wait_ge(s_wl, n + 1)
                load_weights(b, hp + 1)

            step(0, 0)
            step(0, 1)
            with sp.Fori(1, HP - 1) as hp:
                step(hp, 0)
                step(hp, 1)
            tail_sp(sp)

        @block.tensor
        def _(pe):
            def transposes_x():
                pe.wait_ge(s_const, 5)
                pe.wait_ge(s_ln, LN)
                for c in range(NC):
                    for t in range(NT):
                        mm = pe.transpose(ps[:, MX + c, t * P:(t + 1) * P],
                                          xn[:, t, c * P:(c + 1) * P], ident[:, :])
                    mm.then_inc(s_xt, 1)

            def transposes_ctx(n):
                pe.wait_ge(s_ctx[n % 2], 16 * (n // 2 + 1))
                for c in range(NC):
                    for half in range(2):
                        g = 4 * n + 2 * c + half
                        if g >= 4:
                            pe.wait_ge(s_tl, g - 3)
                        for t in range(4):
                            mm = pe.transpose(ps[:, g % 4, t * P:(t + 1) * P],
                                              stage[:, n % 2, 4 * half + t, c * P:(c + 1) * P],
                                              ident[:, :])
                        mm.then_inc(s_tp, 1)

            def event(kind, i, n, par):
                if kind == "q":
                    at_least(pe, s_vc, n * KCH)
                    pe.wait_ge(s_w[par], par_count(n, par))
                    for c in range(NC):
                        mm = pe.matmul(ps[:, PJ, 0:TQ], w_raw[:, par, 0, c, :],
                                       xnT[:, c, par * TQ:(par + 1) * TQ],
                                       start=(c == 0), stop=(c == NC - 1))
                    mm.then_inc(s_q, 1)
                elif kind == "k":
                    if i == 0:
                        pe.wait_ge(s_ql, n + 1)
                        pe.wait_ge(s_wl, n + 1)
                    else:
                        wait_pj(("k", i), n)
                    cols = slice(512 * i, 512 * (i + 1))
                    k = 0
                    for c in range(NC):
                        for w, y in ((w_hi, ctx_hi), (w_hi, ctx_lo), (w_lo, ctx_hi)):
                            mm = pe.matmul(ps[:, PJ, :], w[:, par, 0, c, :], y[:, c, par, cols],
                                           start=(k == 0), stop=(k == 5))
                            k += 1
                    mm.then_inc(s_k, 1)
                elif kind == "v":
                    wait_pj(("v", i), n)
                    for t in range(4):
                        toks = slice((4 * i + t) * P, (4 * i + t + 1) * P)
                        k = 0
                        for c in range(NC):
                            for y, w in ((ctx_hi, w_hi), (ctx_hi, w_lo), (ctx_lo, w_hi)):
                                mm = pe.matmul(ps[:, PJ, t * P:(t + 1) * P], y[:, c, par, toks],
                                               w[:, par, 1, c, :], start=(k == 0), stop=(k == 5))
                                k += 1
                    mm.then_inc(s_v, 1)
                elif kind == "m":
                    wait_pj(("m", 0), n)
                    pe.wait_ge(s_mn, n + 1)
                    for t in range(2):
                        mm = pe.matmul(ps[:, PJ, t * P:(t + 1) * P], m_neg[:, t, :], ident_b[:, :],
                                       start=True, stop=True)
                    mm.then_inc(s_mt, 1)

            def par_count(n, par):
                return (n - par) * 24 + 48

            ORDER = []
            for s in range(SLOTS):
                for table in (EARLY, LATE):
                    if s in table and table[s][0] != "sum":
                        ORDER.append(table[s])
            HAS_SUM_BEFORE = LATE[2]

            def wait_pj(ev, n):
                kind, i = ORDER[ORDER.index(ev) - 1]
                if kind == "k":
                    pe.wait_ge(s_kl, n * KCH + i + 1)
                elif kind == "v":
                    pe.wait_ge(s_vc, n * KCH + i + 1)
                elif kind == "m":
                    pe.wait_ge(s_mr, n + 1)

            def sums(n, par, wait):
                wait()
                pe.wait_ge(s_ps, summed(n, SLOTS - 1))
                for k in range(2):
                    for h in range(2):
                        mm = pe.matmul(ps[64 * h:64 * h + 64, PJ, 0:TQ], sixteen[:, :],
                                       psums[:, par, h, k, :], start=(k == 0), stop=(k == 1))
                mm.then_inc(s_sum, 1)

            def maxima(u, n, par):
                j, t = divmod(u, 2)
                at_least(pe, s_red, n * NU + u)
                pe.wait_ge(s_kh, n * KCH + j + 1)
                pe.wait_ge(s_qh, n + 1)
                for h in range(2):
                    rows = slice(64 * h, 64 * h + 64)
                    mm = pe.matmul(ps[:, MX + h, :], q_hi[rows, par, t * P:(t + 1) * P],
                                   k_hi[rows, par, 512 * j:512 * (j + 1)], start=True, stop=True)
                mm.then_inc(s_mx, 1)

            def scores(g, s, n, par):
                at_least(pe, s_exp, g - 1)
                if s == 0:
                    pe.wait_ge(s_mr, n + 1)
                    pe.wait_ge(s_kl, n * KCH + KCH)
                for k in range(2):
                    keys = slice((2 * s + k) * P, (2 * s + k + 1) * P)
                    for i in range(4):
                        for h in range(2):
                            rows = slice(64 * h, 64 * h + 64)
                            left, right = (
                                (k_hi[rows, par, keys], q_hi[rows, par, :]),
                                (k_lo[rows, par, keys], q_hi[rows, par, :]),
                                (k_hi[rows, par, keys], q_lo[rows, par, :]),
                                (ones_b[rows, :], m_row[rows, par, :]))[i]
                            mm = pe.matmul(ps[:, SC[s % 2] + h, k * TQ:(k + 1) * TQ], left, right,
                                           start=(i == 0), stop=(i == 3))
                mm.then_inc(s_sc, 1)

            def pv(g, s, n, par):
                pe.wait_ge(s_exp, g + 1)
                if s == 0:
                    at_least(pe, s_or, n)
                    pe.wait_ge(s_vc, n * KCH + KCH)
                for k in range(2):
                    for h in range(2):
                        mm = pe.matmul(ps[64 * h:64 * h + 64, ACC, 0:TQ],
                                       v_sb[:, par, 2 * s + k, 64 * h:64 * h + 64],
                                       probs[:, s % NP, h, k, :],
                                       start=(s == 0 and k == 0), stop=(s == SLOTS - 1 and k == 1))
                mm.then_inc(s_pv, 1)

            def step(hp, b):
                n, more = step_of(hp, b), prepares(hp, b)
                for s in range(SLOTS):
                    if s in EARLY and EARLY[s][0] == "sum":
                        if not first_step(hp, b):
                            sums(n - 1, 1 - b,
                                 (lambda: pe.wait_ge(s_kl, (n + 1) * KCH + LATE[s - 1][1] + 1))
                                 if more else (lambda: None))
                    elif s in EARLY and more:
                        event(*EARLY[s], n + 1, 1 - b)
                    scores(slot_of(hp, b, s), s, n, b)
                    if s in MAX_A and more:
                        maxima(MAX_A[s], n + 1, 1 - b)
                    if s >= 1:
                        pv(slot_of(hp, b, s - 1), s - 1, n, b)
                    elif not first_step(hp, b):
                        pv(slot_of(hp, b, s - 1), SLOTS - 1, n - 1, 1 - b)
                    if s in LATE and more:
                        if LATE[s] == HAS_SUM_BEFORE and not first_step(hp, b):
                            pe.wait_ge(s_rs, n)
                        event(*LATE[s], n + 1, 1 - b)
                    if s in MAX_B and more:
                        maxima(MAX_B[s], n + 1, 1 - b)

            transposes_x()
            for n in range(4):
                transposes_ctx(n)
            pe.wait_ge(s_xc, NC)
            pe.wait_ge(s_tl, 16)
            for s in range(SLOTS):
                if s in EARLY and EARLY[s][0] != "sum":
                    event(*EARLY[s], 0, 0)
                if s in MAX_A:
                    maxima(MAX_A[s], 0, 0)
                event(*LATE[s], 0, 0)
                if s in MAX_B:
                    maxima(MAX_B[s], 0, 0)
            for n in range(4, 8):
                transposes_ctx(n)
            pe.wait_ge(s_tl, 32)
            step(0, 0)
            step(0, 1)
            with pe.Fori(1, HP - 1) as hp:
                step(hp, 0)
                step(hp, 1)
            step(HP - 1, 0)
            step(HP - 1, 1)
            pv(STEPS * SLOTS - 1, SLOTS - 1, STEPS - 1, 1)
            sums(STEPS - 1, 1, lambda: pe.wait_ge(s_rs, STEPS - 1))
            tail_pe(pe)

        @block.scalar
        def _(act):
            def split_weights(n, par, count):
                act.wait_ge(s_w[par], count)
                at_least(act, s_v, (n - 1) * KCH)
                nc.scalar.activation(w_hi[:, par, :, :, :], w_raw[:, par, 1:3, :, :], ACT.Copy,
                                     scale=WS).then_inc(s_wh, 1)

            def event(kind, i, n, par):
                if kind == "q":
                    act.wait_ge(s_q, n + 1)
                    nc.scalar.activation(q_hi[:, par, :], ps[:, PJ, 0:TQ], ACT.Copy).then_inc(s_qh, 1)
                elif kind == "k":
                    act.wait_ge(s_k, n * KCH + i + 1)
                    nc.scalar.activation(k_hi[:, par, 512 * i:512 * (i + 1)], ps[:, PJ, :],
                                         ACT.Copy).then_inc(s_kh, 1)
                elif kind == "v":
                    act.wait_ge(s_v, n * KCH + i + 1)
                    nc.scalar.activation(v_sb[:, par, 4 * i:4 * (i + 1), :],
                                         ps[:, PJ, :].rearrange("p (t n) -> p t n", t=4),
                                         ACT.Copy).then_inc(s_vc, 1)
                elif kind == "m":
                    act.wait_ge(s_mt, n + 1)
                    nc.scalar.activation(m_row[:, par, :], ps[:, PJ, 0:TQ], ACT.Copy).then_inc(s_mr, 1)

            def context(n):
                for g in range(4 * n, 4 * n + 4):
                    c, half = divmod(g % 4, 2)
                    act.wait_ge(s_tp, g + 1)
                    keys = slice(1024 * (n % 4) + 512 * half, 1024 * (n % 4) + 512 * half + 512)
                    nc.scalar.activation(ctx_hi[:, c, n // 4, keys], ps[:, g % 4, :], ACT.Copy) \
                        .then_inc(s_th, 1)

            def step(hp, b):
                n, more = step_of(hp, b), prepares(hp, b)
                for s in range(SLOTS):
                    if s in EARLY and more:
                        event(*EARLY[s], n + 1, 1 - b)
                    g = slot_of(hp, b, s)
                    act.wait_ge(s_sc, g + 1)
                    at_least(act, s_pv, g - NP + 1)
                    at_least(act, s_ps, summed(n, s - NP))
                    nc.scalar.activation(
                        probs[:, s % NP, :, :, :].rearrange("p h k q -> p h (k q)"),
                        ps[:, SC[s % 2]:SC[s % 2] + 2, :], ACT.Exp, scale=XSCALE).then_inc(s_exp, 1)
                    if s in LATE and more:
                        event(*LATE[s], n + 1, 1 - b)
                    if s == SPLIT_SLOT and not (isinstance(hp, int) and hp == HP - 1):
                        split_weights(n + 2, b, (n + 2 - b) * 24 + 48)

            root_of_variance(act, 0)
            act.wait_ge(s_xt, NC)
            for c in range(NC):
                nc.scalar.activation(xnT[:, c, :], ps[:, MX + c, :], ACT.Copy).then_inc(s_xc, 1)
            split_weights(0, 0, 48)
            for n in range(4):
                context(n)
            for s in range(SLOTS):
                if s in EARLY:
                    event(*EARLY[s], 0, 0)
                event(*LATE[s], 0, 0)
            split_weights(1, 1, 48)
            for n in range(4, 8):
                context(n)
            step(0, 0)
            step(0, 1)
            with act.Fori(1, HP - 1) as hp:
                step(hp, 0)
                step(hp, 1)
            step(HP - 1, 0)
            step(HP - 1, 1)
            tail_act(act)

        @block.vector
        def _(dve):
            def layernorm(part):
                done = [LN * part]

                def link(i):
                    done[0] += 1
                    i.then_inc(s_ln, 1)
                    dve.wait_ge(s_ln, done[0])

                for t in range(NT):
                    i = nc.vector.bn_stats(stats[:, t, :], x_sb[:, t, :])
                link(i)
                for t in range(NT):
                    i = nc.vector.bn_aggr(mv[:, t, :], stats[:, t, :])
                link(i)
                link(nc.vector.tensor_scalar(var[:, :], mv[:, :, 1], EPS, None, ALU.add))
                dve.wait_ge(s_sd, part + 1)
                link(nc.vector.reciprocal(rstd[:, :], rstd[:, :]))
                link(nc.vector.tensor_tensor(newton[:, :], rstd[:, :], rstd[:, :], ALU.mult))
                link(nc.vector.tensor_tensor(newton[:, :], newton[:, :], var[:, :], ALU.mult))
                link(nc.vector.tensor_scalar(newton[:, :], newton[:, :], -0.5, 1.5, ALU.mult, ALU.add))
                link(nc.vector.tensor_tensor(rstd[:, :], rstd[:, :], newton[:, :], ALU.mult))
                for t in range(NT):
                    i = nc.vector.tensor_scalar(xn[:, t, :], x_sb[:, t, :], mv[:, t, 0:1],
                                                rstd[:, t:t + 1], ALU.subtract, ALU.mult)
                i.then_inc(s_ln, 1)

            def split_weights(n, par):
                dve.wait_ge(s_wh, n + 1)
                nc.vector.scalar_tensor_tensor(
                    w_lo[:, par, :, :, :].rearrange("p a c n -> p (a c n)"),
                    w_raw[:, par, 1:3, :, :].rearrange("p a c n -> p (a c n)"), WS,
                    w_hi[:, par, :, :, :].rearrange("p a c n -> p (a c n)"),
                    ALU.mult, ALU.subtract).then_inc(s_wl, 1)

            def event(kind, i, n, par):
                if kind == "q":
                    dve.wait_ge(s_qh, n + 1)
                    nc.vector.tensor_tensor(q_lo[:, par, :], ps[:, PJ, 0:TQ], q_hi[:, par, :],
                                            ALU.subtract).then_inc(s_ql, 1)
                elif kind == "k":
                    dve.wait_ge(s_kh, n * KCH + i + 1)
                    cols = slice(512 * i, 512 * (i + 1))
                    nc.vector.tensor_tensor(k_lo[:, par, cols], ps[:, PJ, :], k_hi[:, par, cols],
                                            ALU.subtract).then_inc(s_kl, 1)
                elif kind == "m":
                    dve.wait_ge(s_red, n * NU + NU)
                    at_least(dve, s_mt, n)
                    nc.vector.tensor_reduce(m_neg[:, :, 0:P:64], m_part[:, :, :, :].rearrange(
                        "p j t h -> p t h j"), AX.X, ALU.max, negate=True).then_inc(s_mn, 1)

            def maxima(u, n):
                j, t = divmod(u, 2)
                dve.wait_ge(s_mx, n * NU + u + 1)
                if u == 0:
                    at_least(dve, s_mn, n)
                nc.vector.tensor_reduce(m_part[:, j, t, :], ps[:, MX:MX + 2, :], AX.X, ALU.max) \
                    .then_inc(s_red, 1)

            def context(n):
                for g in range(4 * n, 4 * n + 4):
                    c, half = divmod(g % 4, 2)
                    dve.wait_ge(s_th, g + 1)
                    keys = slice(1024 * (n % 4) + 512 * half, 1024 * (n % 4) + 512 * half + 512)
                    nc.vector.tensor_tensor(ctx_lo[:, c, n // 4, keys], ps[:, g % 4, :],
                                            ctx_hi[:, c, n // 4, keys], ALU.subtract) \
                        .then_inc(s_tl, 1)

            def take_output(n, g):
                dve.wait_ge(s_pv, g + 1)
                at_least(dve, s_on, n)
                nc.vector.tensor_copy(o_raw[:, :], ps[:, ACC, 0:TQ]).then_inc(s_or, 1)

            def normalise(n, hp, par):
                dve.wait_ge(s_sum, n + 1)
                nc.vector.reciprocal(o_rec[:, :], ps[:, PJ, 0:TQ]).then_inc(s_rs, 1)
                dve.wait_ge(s_or, n + 1)
                dve.wait_ge(s_rs, n + 1)
                nc.vector.tensor_tensor(o_all[:, hp, par * TQ:(par + 1) * TQ], o_raw[:, :],
                                        o_rec[:, :], ALU.mult).then_inc(s_on, 1)

            def step(hp, b):
                n, more = step_of(hp, b), prepares(hp, b)
                for s in range(SLOTS):
                    if s in EARLY and EARLY[s][0] == "sum":
                        if not first_step(hp, b):
                            normalise(n - 1, hp if b else hp - 1, 1 - b)
                    elif s in EARLY and EARLY[s][0] == "q" and more:
                        event(*EARLY[s], n + 1, 1 - b)
                    if s in MAX_A and more:
                        maxima(MAX_A[s], n + 1)
                    if s == 0 and not first_step(hp, b):
                        take_output(n - 1, slot_of(hp, b, -1))
                    if s in LATE and more:
                        event(*LATE[s], n + 1, 1 - b)
                    if s in MAX_B and more:
                        maxima(MAX_B[s], n + 1)
                    if s == max(MAX_B) and more:
                        event("m", 0, n + 1, 1 - b)
                    if s == SPLIT_SLOT and not (isinstance(hp, int) and hp == HP - 1):
                        split_weights(n + 2, b)

            dve.wait_ge(s_x, 16)
            layernorm(0)
            nc.vector.memset(m_neg[:, :, :], 0.0).then_inc(s_mf, 1)
            split_weights(0, 0)
            for n in range(4):
                context(n)
            dve.wait_ge(s_mf, 1)
            for s in range(SLOTS):
                if EARLY.get(s, "-")[0] == "q":
                    event("q", 0, 0, 0)
                if s in MAX_A:
                    maxima(MAX_A[s], 0)
                event(*LATE[s], 0, 0)
                if s in MAX_B:
                    maxima(MAX_B[s], 0)
                if s == max(MAX_B):
                    event("m", 0, 0, 0)
            split_weights(1, 1)
            for n in range(4, 8):
                context(n)
            step(0, 0)
            step(0, 1)
            with dve.Fori(1, HP - 1) as hp:
                step(hp, 0)
                step(hp, 1)
            step(HP - 1, 0)
            step(HP - 1, 1)
            take_output(STEPS - 1, STEPS * SLOTS - 1)
            normalise(STEPS - 1, HP - 1, 1)
            tail_dve(dve, layernorm)

        @block.gpsimd
        def _(pool):
            nc.gpsimd.memset(ident[:, :], 0.0).then_inc(s_const, 1)
            nc.gpsimd.memset(ones_b[:, :], 1.0).then_inc(s_const, 1)
            nc.gpsimd.memset(sixteen[:, :], WS).then_inc(s_const, 1)
            pool.wait_ge(s_const, 3)
            nc.gpsimd.affine_select(out=ident[:, :], in_=ident[:, :], compare_op=ALU.not_equal,
                                    fill=1.0, base=0, pattern=[[-1, P]], channel_multiplier=1) \
                .then_inc(s_const, 1)
            pool.wait_ge(s_const, 4)
            nc.gpsimd.tensor_copy(ident_b[:, :], ident[:, :]).then_inc(s_const, 1)

            def step(hp, b):
                n = step_of(hp, b)
                total = psums[:, b, :, :, :].rearrange("p h k q -> p (h k q)")
                parts = [probs[:, i, :, :, :].rearrange("p h k q -> p (h k q)") for i in range(NP)]
                for s in range(1, SLOTS):
                    pool.wait_ge(s_exp, slot_of(hp, b, s) + 1)
                    if s == 1:
                        at_least(pool, s_sum, n - 1)
                    else:
                        pool.wait_ge(s_ps, summed(n, s - 1))
                    nc.gpsimd.tensor_tensor(total, parts[0] if s == 1 else total, parts[s % NP],
                                            ALU.add).then_inc(s_ps, 1)

            step(0, 0)
            step(0, 1)
            with pool.Fori(1, HP - 1) as hp:
                step(hp, 0)
                step(hp, 1)
            step(HP - 1, 0)
            step(HP - 1, 1)
            tail_pool(pool)


_INS = ["x", "ctx_1024", "L0_xattn_w_q", "L0_xattn_w_k", "L0_xattn_w_v", "L0_xattn_w_o", "L0_attn_wq",
        "L0_attn_wk", "L0_attn_wv", "L0_attn_wo", "L0_ffn_Wg", "L0_ffn_bg", "L0_ffn_W1", "L0_ffn_b1",
        "L0_ffn_W2", "L0_ffn_b2"]


def kernel(**inputs):
    import numpy as _np
    import concourse.bacc as _bacc
    from concourse import mybir as _mybir
    from concourse.bass_utils import run_bass_kernel_spmd as _run

    nc = _bacc.Bacc("TRN2", target_bir_lowering=False, num_devices=1)
    arrays, args = {}, []
    for name in _INS:
        a = _np.ascontiguousarray(inputs[name])
        arrays[f"in_{name}_dram"] = a
        args.append(nc.dram_tensor(f"in_{name}_dram", a.shape, _mybir.dt.from_np(a.dtype),
                                   kind="ExternalInput").ap())
    args.append(nc.dram_tensor("out_0_dram", (B, TQ, D), FP32, kind="ExternalOutput").ap())
    perceiver(nc, *args)
    r = _run(nc, [arrays], core_ids=[0])
    return r.results[0]["out_0_dram"]
```

```python
from contextlib import ExitStack

import concourse.bass as bass
from concourse import mybir

FP32 = mybir.dt.float32
FP16 = mybir.dt.float16
BF16 = mybir.dt.bfloat16
ALU = mybir.AluOpType
ACT = mybir.ActivationFunctionType
AX = mybir.AxisListType

P = 128
B, TQ, TK, D = 2, 256, 4096, 256
T = B * TQ
NT = T // P
NC = D // P
XH, XD = 16, 64
HP = XH // 2
STEPS = HP * B
SLOTS = TK // P
KCH = TK // 512
CS = 512 // P
WS = 16.0
XSCALE = XD ** -0.5 / WS
MS = 256.0
SH, SD = 16, 16
E, F = 8, 256
EPS = 1e-5
IQ = 12
DV = 7
TC = 9
LN = 9

SC = 0
ACC = 2
MX = 3
PK = 5
PV = 6
TURNED = (2, 6)
PM = 7

K_AT = {1: 0, 4: 1, 8: 2, 11: 3, 14: 4, 17: 5, 20: 6, 23: 7}
V_AT = {2: 1, 6: 2, 10: 3, 14: 4, 18: 5, 22: 6, 26: 7, 30: 0}
MAX_AT = {3: 0, 5: 1, 6: 2, 7: 3, 10: 4, 11: 5, 13: 6, 15: 7, 16: 8, 18: 9, 19: 10, 21: 11, 22: 12,
          24: 13, 25: 14, 27: 15}
Q_AT, SUM_AT, Y_AT, M_AT = 0, 5, 9, 30
TURN_AT = {20: 0, 23: 1, 27: 2, 29: 3}
TURN_BANK = (MX, MX + 1, PK, MX)
SPLIT_K_AT, SPLIT_V_AT = 16, 12
NU = 2 * KCH
NP = 8
NV = 4


def perceiver(nc, x, ctx, wq, wk, wv, wo, aq, ak, av, ao, gw, gb, w1, b1, w2, b2, out):
    stack = ExitStack()

    def sb(name, shape, dt=FP32):
        return stack.enter_context(nc.sbuf_tensor(name, shape, dt))

    def sem(name):
        return stack.enter_context(nc.semaphore(name))

    with stack:
        ps = stack.enter_context(nc.psum_tensor("ps", [P, 8, 512], FP32))
        ctx_hi = sb("ctx_hi", [P, B, NC, TK], FP16)
        ctx_lo = sb("ctx_lo", [P, B, NC, TK], FP16)
        k1 = sb("k1", [P, B, 2, TK], FP16)
        k2 = sb("k2", [P, B, 2, TK], FP16)
        q1 = sb("q1", [P, B, 2, TQ], FP16)
        q2 = sb("q2", [P, B, 2, TQ], FP16)
        v_sb = sb("v_sb", [P, NV, CS, P])
        probs = sb("probs", [P, NP, 2, TQ])
        psums = sb("psums", [P, B, 2, 2, TQ])
        o_raw = sb("o_raw", [P, TQ])
        o_rec = sb("o_rec", [P, TQ])
        o_norm = sb("o_norm", [P, TQ])
        x_sb = sb("x_sb", [P, NT, D])
        xn = sb("xn", [P, NT, D])
        xnT = sb("xnT", [P, NC, T])
        wqk_raw = sb("wqk_raw", [P, B, 2, NC, P])
        wk_hi = sb("wk_hi", [P, B, NC, P], FP16)
        wk_lo = sb("wk_lo", [P, B, NC, P], FP16)
        wv_raw = sb("wv_raw", [P, B, NC, P])
        wv_hi = sb("wv_hi", [P, B, NC, P], FP16)
        wv_lo = sb("wv_lo", [P, B, NC, P], FP16)
        wo_raw = sb("wo_raw", [P, B, D])
        m_part = sb("m_part", [P, KCH, 2, 2])
        m_neg = sb("m_neg", [P, 2, P])
        ident = sb("ident", [P, P])
        sixteen = sb("sixteen", [P, XD])
        stats = sb("stats", [P, NT, 6])
        mv = sb("mv", [P, NT, 2])
        rstd = sb("rstd", [P, NT])
        var = sb("var", [P, NT])
        newton = sb("newton", [P, NT])

        stage = (probs[:, :, :, :].rearrange("p (n a) h q -> p n (a h q)", n=2)
                 .rearrange("p n (t c) -> p n t c", c=D),
                 k1[:, 1, :, :].rearrange("p h k -> p (h k)").bitcast(FP32)
                 .rearrange("p (n t c) -> p n t c", n=2, c=D))

        copies = psums[:, :, :, :, :].rearrange("p b k h q -> p (b k) (h q)")

        hi32 = ctx_hi[:, :, :, :].rearrange("p b c k -> p (b c k)").bitcast(FP32)
        lo32 = ctx_lo[:, :, :, :].rearrange("p b c k -> p (b c k)").bitcast(FP32)
        w1_sb = hi32[:, 0:4096].rearrange("p (e c n) -> p e c n", e=E, c=NC)
        w2_sb = hi32[:, 4096:8192].rearrange("p (e c n) -> p e c n", e=E, c=NC)
        a_raw = lo32[:, 0:2048].rearrange("p (w t n) -> p w t n", w=4, t=NC)
        aqk_T = lo32[:, 2048:4096].rearrange("p (w c h d) -> p w c h d", w=2, c=NC, h=SH)
        avo_T = lo32[:, 4096:5120].rearrange("p (w c n) -> p w c n", w=2, c=NC)
        k1_32 = k1[:, :, :, :].rearrange("p b h k -> p (b h k)").bitcast(FP32)
        k2_32 = k2[:, :, :, :].rearrange("p b h k -> p (b h k)").bitcast(FP32)
        qx = k1_32[:, 0:2048].rearrange("p (g t) -> p g t", g=4)
        kx = k1_32[:, 2048:4096].rearrange("p (g t) -> p g t", g=4)
        rq = k1_32[:, 4096:5120].bitcast(BF16).rearrange("p (g t) -> p g t", g=4)
        rk = k1_32[:, 5120:6144].bitcast(BF16).rearrange("p (g t) -> p g t", g=4)
        square = lo32[:, 5120:6144].rearrange("p (n t) -> p n t", n=2)
        inv = lo32[:, 6144:6656]
        inv_t = lo32[:, 6656:7168]
        inv_p = lo32[:, 7168:7936].bitcast(BF16).rearrange("p (i t) -> p i t", i=3)
        p32 = probs[:, :, :, :].rearrange("p n h q -> p (n h q)")
        ratio = lo32[:, 0:4096].rearrange("p (n k h q) -> p n k h q", n=2, k=2, h=4)
        root = p32[:, 0:4096].rearrange("p (n k h q) -> p n k h q", n=2, k=2, h=4)
        weight = k2_32[:, 0:8192].rearrange("p (g k h q) -> p g k h q", g=4, k=2, h=4)
        o_T = lo32[:, 5120:5632].rearrange("p (n q) -> p n q", n=2)
        place = k2_32[:, 0:1536].bitcast(BF16).rearrange("p (w i g n) -> p w i g n", w=2, i=3, g=4)
        hid = k2_32[:, 0:1024].rearrange("p (n t) -> p n t", n=2)
        hid_m = k2_32[:, 1024:2048].rearrange("p (n t) -> p n t", n=2)
        s32 = psums[:, :, :, :, :].rearrange("p b h k q -> p (b h k q)")
        vx = s32[:, 0:2048].rearrange("p (t h d) -> p t h d", t=NT, h=SH)
        orec = sb("orec", [P, B, 2, SH])
        sel = sb("sel", [P, 2, P])
        head_rows = sb("head_rows", [P, 4])
        gather = sb("gather", [P, 240])
        vecs = sb("vecs", [P, 6])
        rvec = sb("rvec", [P, 10])
        ones1 = sb("ones1", [1, P])
        rank = sb("rank", [P, NT, E])
        gw_sb = sb("gw_sb", [P, NC, E])
        gb_sb = sb("gb_sb", [1, E])
        b1_T = sb("b1_T", [P, E * NC])
        lg = sb("lg", [P, NT, E])
        ge = sb("ge", [P, NT, E])
        best = sb("best", [P, NT, E])
        sel_b = sb("sel_b", [E, E, P], BF16)
        gs = sb("gs", [P, 4, NT])
        v32 = v_sb[:, :, :, :].rearrange("p n s d -> p (n s d)")
        best_T = v32[0:E, 0:T]
        best_b = v32[0:E, T:T + T // 2].bitcast(BF16)
        b2_sb = v32[0:E, 768:768 + D]
        b1_raw = v32[0:E * NC, 1024:1024 + P]

        s_const = sem("s_const")
        s_x = sem("s_x")
        s_ctx = [sem(f"s_ctx{i}") for i in range(4)]
        s_wqk = [sem("s_wqk0"), sem("s_wqk1")]
        s_wv = [sem("s_wv0"), sem("s_wv1")]
        s_wo = [sem("s_wo0"), sem("s_wo1")]
        s_k2 = [sem("s_k2a"), sem("s_k2b")]
        s_ln = sem("s_ln")
        s_sd = sem("s_sd")
        s_xt = sem("s_xt")
        s_xc = sem("s_xc")
        s_tp = sem("s_tp")
        s_th = sem("s_th")
        s_tl = [sem("s_tl0"), sem("s_tl1")]
        s_wkh = sem("s_wkh")
        s_wkl = sem("s_wkl")
        s_wvh = sem("s_wvh")
        s_wvl = sem("s_wvl")
        s_q = sem("s_q")
        s_k = sem("s_k")
        s_v = sem("s_v")
        s_mx = sem("s_mx")
        s_mt = sem("s_mt")
        s_sc = sem("s_sc")
        s_pv = sem("s_pv")
        s_sum = sem("s_sum")
        s_qh = sem("s_qh")
        s_kh = sem("s_kh")
        s_vc = sem("s_vc")
        s_mr = sem("s_mr")
        s_exp = sem("s_exp")
        s_ql = sem("s_ql")
        s_kl = sem("s_kl")
        s_red = sem("s_red")
        s_mn = sem("s_mn")
        s_mz = sem("s_mz")
        s_or = sem("s_or")
        s_rs = sem("s_rs")
        s_on = sem("s_on")
        s_yx = sem("s_yx")
        s_ya = sem("s_ya")
        s_ps = sem("s_ps")
        s_aw = sem("s_aw")
        s_ew = sem("s_ew")
        s_small = sem("s_small")
        s_out = sem("s_out")
        s_tc = sem("s_tc")
        s_vec = sem("s_vec")
        s_vone = sem("s_vone")
        s_at = sem("s_at")
        s_ac = sem("s_ac")
        s_y = sem("s_y")
        s_x1 = sem("s_x1")
        s_qk = sem("s_qk")
        s_sq = sem("s_sq")
        s_nm = sem("s_nm")
        s_qx = sem("s_qx")
        s_sl = sem("s_sl")
        s_iq = sem("s_iq")
        s_pl = sem("s_pl")
        s_pq = sem("s_pq")
        s_pk = sem("s_pk")
        s_vp = sem("s_vp")
        s_vx = sem("s_vx")
        s_dd = sem("s_dd")
        s_rt = sem("s_rt")
        s_r2 = sem("s_r2")
        s_ra = sem("s_ra")
        s_lg = sem("s_lg")
        s_wt = sem("s_wt")
        s_o = sem("s_o")
        s_oe = sem("s_oe")
        s_ot = sem("s_ot")
        s_on2 = sem("s_on2")
        s_gl = sem("s_gl")
        s_g = sem("s_g")
        s_ge = sem("s_ge")
        s_bt = sem("s_bt")
        s_bc = sem("s_bc")
        s_h = sem("s_h")
        s_hg = sem("s_hg")
        s_hm = sem("s_hm")
        s_dv = sem("s_dv")

        def at_least(eng, semaphore, count):
            if not (isinstance(count, int) and count <= 0):
                eng.wait_ge(semaphore, count)

        def context_pair(u):
            j, b = divmod(u, 2)
            return b, j // 2, j % 2, slice(512 * j, 512 * (j + 1))

        def slot_of(hp, b, s):
            return hp * (B * SLOTS) + (b * SLOTS + s)

        def step_of(hp, b):
            return hp * B + b

        def load_count(n, par, each):
            return (n - par) * (each // 2) + each

        def summed(n, s):
            if s < 0:
                return summed(n - 1, s + SLOTS)
            return n * (SLOTS // 2 - 1) + max(s // 2, 1)

        def first_step(hp, b):
            return isinstance(hp, int) and hp == 0 and b == 0

        def prepares(hp, b):
            return not (isinstance(hp, int) and hp == HP - 1 and b == B - 1)

        def attn_units():
            return [(((b * 4 + g) * 2 + kt) * 2 + jj, b * 4 + g, b, g, kt, jj) for b in range(B)
                    for g in range(4) for kt in range(2) for jj in range(2)]

        def tail_sp(sp):
            sp.dma_start(gw_sb[:, :, :], gw.rearrange("(c p) e -> p c e", p=P)).then_inc(s_small, 16)
            sp.dma_start(gb_sb[:, :], gb.rearrange("(a e) -> a e", a=1)).then_inc(s_small, 16)
            sp.wait_ge(s_v, (STEPS - 1) * KCH)
            for i, w in enumerate((aq, ak, av, ao)):
                sp.dma_start(a_raw[:, i, :, :], w.rearrange("(t p) n -> p t n", p=P)).then_inc(s_aw, 16)
            sp.dma_start(w1_sb.rearrange("p e c n -> p (e c) n"),
                         w1.rearrange("e (c p) n -> p (e c) n", p=P)).then_inc(s_ew, 16)
            sp.wait_ge(s_v, STEPS * KCH)
            sp.dma_start(w2_sb.rearrange("p e c n -> p (e c) n"),
                         w2.rearrange("e (c p) n -> p (e c) n", p=P)).then_inc(s_ew, 16)
            sp.wait_ge(s_sum, STEPS)
            sp.dma_start(b1_raw[:, :], b1.rearrange("e (i p) -> (e i) p", p=P)).then_inc(s_small, 16)
            sp.dma_start(b2_sb[:, :], b2).then_inc(s_small, 16)
            sp.wait_ge(s_x1, 2 * NT)
            sp.dma_start(out.rearrange("b (t p) c -> p (b t) c", p=P), x_sb[:, :, :]).then_inc(s_out, 16)
            sp.wait_ge(s_out, 16)

        def tail_constants(pool):
            for i, tile in enumerate((sel[:, :, :], sel_b[:, :, :], gather[:, :])):
                nc.gpsimd.memset(tile, 0.0).then_inc(s_tc, 1)
                pool.wait_ge(s_tc, i + 1)
            nc.gpsimd.memset(ones1[:, :], 1.0).then_inc(s_tc, 1)
            done = 4

            nc.gpsimd.memset(head_rows[:, :], 1.0).then_inc(s_tc, 1)
            for base, step, mult in ((0, -32, 1), (15, 32, -1)):
                done += 1
                pool.wait_ge(s_tc, done)
                nc.gpsimd.affine_select(out=head_rows[:, :], in_=head_rows[:, :],
                                        compare_op=ALU.is_ge, fill=0.0, base=base,
                                        pattern=[[step, 4]], channel_multiplier=mult) \
                    .then_inc(s_tc, 1)
            pool.wait_ge(s_tc, done + 1)
            for i, r in enumerate((16, 17)):
                nc.gpsimd.tensor_copy(sel[:, i, r:P:32], head_rows[:, :])
            nc.gpsimd.tensor_copy(gather[:, 112:128].rearrange("p (j r) -> p j r", r=4),
                                  head_rows[:, :].unsqueeze(2).to_broadcast([P, 4, 4]))
            nc.gpsimd.affine_select(out=sel_b[:, :, :], in_=sel_b[:, :, :], compare_op=ALU.not_equal,
                                    fill=1.0, base=0, pattern=[[-1, E], [0, P]],
                                    channel_multiplier=1).then_inc(s_tc, 1)
            pool.wait_ge(s_tc, done + 2)
            for e in range(E):
                i = nc.gpsimd.memset(rank[:, :, e], float(E - e))
            i.then_inc(s_tc, 1)

        def zero_rows(pool):
            pool.wait_ge(s_v, (STEPS - 1) * KCH)
            for w in range(2):
                for c in range(NC):
                    i = nc.gpsimd.memset(aqk_T[:, w, c, :, SD:32], 0.0)
            i.then_inc(s_vone, 1)

        def tail_pool(pool):
            pool.wait_ge(s_sc, STEPS * SLOTS)
            nc.gpsimd.memset(place, 0.0).then_inc(s_tc, 1)
            pool.wait_ge(s_tc, TC + 1)
            for product, parts in enumerate(((0, 0), (0, 1), (1, 0), (0, 2), (1, 1), (2, 0))):
                for w, part in enumerate(parts):
                    i = nc.gpsimd.tensor_copy(
                        place[:, w, part, :, :].rearrange("p g (j n) -> p g j n", j=4)
                        [:, :, :, 4 * product:4 * product + 4],
                        ident[:, 64 * w:64 * w + 64].rearrange("p (g j r) -> p g j r", g=4, j=4))
            i.then_inc(s_tc, 1)
            pool.wait_ge(s_sum, STEPS)
            for t in range(NT):
                nc.gpsimd.memset(vx[:, t, :, SD:SD + 1], 1.0)
                i = nc.gpsimd.memset(vx[:, t, :, SD + 1:32], 0.0)
            i.then_inc(s_vone, 1)
            for gg in range(8):
                pool.wait_ge(s_r2, gg + 1)
                if gg >= 4:
                    pool.wait_ge(s_o, gg - 3)
                nc.gpsimd.tensor_tensor(
                    weight[:, gg % 4, :, :, :].rearrange("p k h q -> p (k h q)"),
                    root[:, gg % 2, :, :, :].rearrange("p k h q -> p (k h q)"),
                    ratio[:, gg % 2, :, :, :].rearrange("p k h q -> p (k h q)"),
                    ALU.add).then_inc(s_ra, 1)

        def turn_weights(pe, w):
            if w == 0:
                pe.wait_ge(s_aw, 4 * 16)
                pe.wait_ge(s_red, STEPS * NU)
            if w == 3:
                pe.wait_ge(s_ac, 1)
            for c in range(NC):
                for t in range(NC):
                    mm = pe.transpose(ps[:, TURN_BANK[w], (NC * c + t) * P:(NC * c + t + 1) * P],
                                      a_raw[:, w, t, c * P:(c + 1) * P], ident[:, :])
            mm.then_inc(s_at, 1)

        def take_turned(act, w):
            act.wait_ge(s_at, w + 1)
            if w < 2:
                if w == 0:
                    act.wait_ge(s_vone, 1)
                nc.scalar.activation(
                    aqk_T[:, w, :, :, 0:SD].rearrange("p c h d -> p (c h) d"),
                    ps[:, TURN_BANK[w], :].rearrange("p (h d) -> p h d", d=SD),
                    ACT.Copy).then_inc(s_ac, 1)
            else:
                if w == 2:
                    act.wait_ge(s_v, STEPS * KCH)
                nc.scalar.activation(avo_T[:, w - 2, :, :].rearrange("p c n -> p (c n)"),
                                     ps[:, TURN_BANK[w], :], ACT.Copy).then_inc(s_ac, 1)

        def tail_pe(pe):
            def transposes(src, bank):
                for c in range(NC):
                    for t in range(NT):
                        mm = pe.transpose(ps[:, bank + c, t * P:(t + 1) * P],
                                          src[:, t, c * P:(c + 1) * P], ident[:, :])
                    mm.then_inc(s_xt, 1)

            pe.wait_ge(s_ln, 2 * LN)
            pe.wait_ge(s_ac, 4)
            pe.wait_ge(s_or, STEPS)
            transposes(xn, 4)
            pe.wait_ge(s_xc, 2 * NC)
            for t in range(NT):
                for c in range(NC):
                    mm = pe.matmul(ps[:, t, 0:D], xnT[:, c, t * P:(t + 1) * P], avo_T[:, 0, c, :],
                                   start=(c == 0), stop=(c == NC - 1))
                mm.then_inc(s_vp, 1)
            pe.wait_ge(s_tc, TC)

            def qk(i):
                w, g = divmod(i, 4)
                bank = 4 + i % 2
                if i >= 2:
                    pe.wait_ge(s_qx, i - 1)
                for c in range(NC):
                    mm = pe.matmul(ps[:, bank, :],
                                   aqk_T[:, w, c, 4 * g:4 * g + 4, :].rearrange("p h d -> p (h d)"),
                                   xnT[:, c, :], start=(c == 0), stop=(c == NC - 1))
                mm.then_inc(s_qk, 1)

            def lengths(i):
                w, g = divmod(i, 4)
                pe.wait_ge(s_sq, i + 1)
                pe.matmul(ps[:, 4 + i % 2, :], sel[:, w, :], square[:, i % 2, :],
                          start=False, stop=True, skip_group_check=True).then_inc(s_nm, 1)
                mm = pe.matmul(ps[:, 6, :], gather[:, 112 - 16 * i:240 - 16 * i], square[:, i % 2, :],
                               start=(i == 0), stop=(i == 7))
                mm.then_inc(s_sl, 1)

            for i in range(9):
                if i < 8:
                    qk(i)
                if i >= 1:
                    lengths(i - 1)
            pe.wait_ge(s_iq, IQ)
            pe.wait_ge(s_tc, TC + 2)
            pe.wait_ge(s_qx, 8)
            for g in range(4):
                for w in range(2):
                    if g >= 1:
                        pe.wait_ge((s_pq, s_pk)[w], g)
                    rows = slice(64 * w, 64 * w + 64)
                    for i in range(3):
                        mm = pe.matmul(ps[:, 4 + w, :], place[rows, w, i, g, :], inv_p[rows, i, :],
                                       start=(i == 0), stop=(i == 2))
                    mm.then_inc(s_pl, 1)
            pe.wait_ge(s_vx, NT)

            def distances(m, b, g, kt, jj):
                if m == 0:
                    pe.wait_ge(s_pq, 4)
                    pe.wait_ge(s_pk, 4)
                if m >= 2:
                    pe.wait_ge(s_rt, 2 * (m - 1))
                keys = slice((2 * b + kt) * P, (2 * b + kt + 1) * P)
                for half, left, right in ((0, kx, qx), (1, rk, rq)):
                    for j in (2 * jj, 2 * jj + 1):
                        mm = pe.matmul(ps[:, j, half * TQ:(half + 1) * TQ],
                                       left[32 * j:32 * j + 32, g, keys],
                                       right[32 * j:32 * j + 32, g, b * TQ:(b + 1) * TQ],
                                       start=True, stop=True)
                mm.then_inc(s_dd, 1)

            def average(gg, b, g):
                pe.wait_ge(s_wt, gg + 1)
                if gg >= 2:
                    pe.wait_ge(s_oe, gg - 1)
                for kt in range(2):
                    for j in range(4):
                        mm = pe.matmul(ps[32 * j:32 * j + 32, 4 + gg % 2, 0:TQ],
                                       vx[:, 2 * b + kt, 4 * g + j, :], weight[:, g, kt, j, :],
                                       start=(kt == 0), stop=(kt == 1))
                mm.then_inc(s_o, 1)

            def turn_average(gg, b, g):
                pe.wait_ge(s_oe, gg + 1)
                if gg == 4:
                    pe.wait_ge(s_on2, 1)
                for t in range(2):
                    mm = pe.transpose(ps[:, 6 + t, g * P:(g + 1) * P], o_T[:, gg % 2, t * P:(t + 1) * P],
                                      ident[:, :])
                mm.then_inc(s_ot, 1)

            for m, gg, b, g, kt, jj in attn_units():
                distances(m, b, g, kt, jj)
                if (b, g, kt, jj) == (1, 1, 1, 1):
                    for done in range(4):
                        average(done, 0, done)
                        if done >= 1:
                            turn_average(done - 1, 0, done - 1)
                    turn_average(3, 0, 3)
            for g in range(4):
                average(4 + g, 1, g)
                if g >= 1:
                    turn_average(3 + g, 1, g - 1)
            turn_average(7, 1, 3)
            pe.wait_ge(s_on2, B)
            transposes(xn, 0)
            pe.wait_ge(s_xc, 3 * NC)
            for t in range(NT):
                for c in range(NC):
                    mm = pe.matmul(ps[:, t, 0:D], xnT[:, c, t * P:(t + 1) * P], avo_T[:, 1, c, :],
                                   start=(c == 0), stop=(c == NC - 1))
                mm.then_inc(s_y, 1)

            pe.wait_ge(s_small, 64)
            pe.transpose(ps[:, 7, 0:E * NC], b1_raw[:, :], ident[0:E * NC, 0:E * NC]).then_inc(s_bt, 1)
            pe.wait_ge(s_ln, 3 * LN)
            transposes(xn, 4)
            pe.wait_ge(s_xc, 4 * NC)
            for t in range(NT):
                for c in range(NC):
                    pe.matmul(ps[:, 6, t * E:(t + 1) * E], xnT[:, c, t * P:(t + 1) * P],
                              gw_sb[:, c, :], start=(c == 0), stop=False)
                mm = pe.matmul(ps[:, 6, t * E:(t + 1) * E], ones1[:, :], gb_sb[:, :],
                               start=False, stop=True)
            mm.then_inc(s_gl, 1)
            pe.wait_ge(s_ew, 32)
            pe.wait_ge(s_x1, NT)
            pe.wait_ge(s_bc, 1)

            def hidden(i):
                e, it = divmod(i, NC)
                if i >= 2:
                    pe.wait_ge(s_hg, i - 1)
                for c in range(NC):
                    mm = pe.matmul(ps[:, 4 + i % 2, :], w1_sb[:, e, c, it * P:(it + 1) * P],
                                   xnT[:, c, :], start=(c == 0), stop=(c == NC - 1))
                mm.then_inc(s_h, 1)
                if it == 0:
                    if e >= 2:
                        pe.wait_ge(s_hm, NC * (e - 1))
                    pe.matmul(ps[:, 6 + e % 2, :], sel_b[:, e, :], best_b[:, :],
                              start=True, stop=True).then_inc(s_bt, 1)

            def outer(i):
                e, it = divmod(i, NC)
                pe.wait_ge(s_hm, i + 1)
                for t in range(NT):
                    mm = pe.matmul(ps[:, t, 0:D], hid_m[:, i % 2, t * P:(t + 1) * P],
                                   w2_sb[:, e, it, :], start=False, stop=(i == E * NC - 1))
                mm.then_inc(s_y, 1)

            pe.wait_ge(s_g, 10)
            for t in range(NT):
                mm = pe.transpose(ps[0:E, 7, t * P:(t + 1) * P], best[:, t, :], ident[:, :])
            mm.then_inc(s_bt, 1)
            pe.wait_ge(s_bc, 3)
            for t in range(NT):
                pe.matmul(ps[:, t, 0:D], best_T[:, t * P:(t + 1) * P], b2_sb[:, :],
                          start=True, stop=False)
            for i in range(E * NC + 1):
                if i < E * NC:
                    hidden(i)
                if i >= 1:
                    outer(i - 1)

        def root_of_variance(act, part):
            act.wait_ge(s_ln, LN * part + 3)
            nc.scalar.activation(rstd[:, :], var[:, :], ACT.Sqrt).then_inc(s_sd, 1)

        def tail_act(act):
            def take_xnT(base, bank):
                act.wait_ge(s_xt, base + NC)
                for c in range(NC):
                    nc.scalar.activation(xnT[:, c, :], ps[:, bank + c, :], ACT.Copy).then_inc(s_xc, 1)

            root_of_variance(act, 1)
            take_xnT(NC, 4)
            act.wait_ge(s_vp, NT)
            act.wait_ge(s_vone, 2)
            for t in range(NT):
                nc.scalar.activation(vx[:, t, :, 0:SD],
                                     ps[:, t, 0:D].rearrange("p (h d) -> p h d", d=SD),
                                     ACT.Copy).then_inc(s_vx, 1)

            def squares(i):
                act.wait_ge(s_qk, i + 1)
                if i >= 2:
                    act.wait_ge(s_nm, i - 1)
                nc.scalar.activation(square[:, i % 2, :], ps[:, 4 + i % 2, :], ACT.Square) \
                    .then_inc(s_sq, 1)

            def rows(i):
                w, g = divmod(i, 4)
                act.wait_ge(s_nm, i + 1)
                if w == 0:
                    nc.scalar.activation(qx[:, g, :], ps[:, 4 + i % 2, :], ACT.Identity,
                                         bias=vecs[:, 1:2]).then_inc(s_qx, 1)
                else:
                    nc.scalar.activation(kx[:, g, :], ps[:, 4 + i % 2, :], ACT.Identity,
                                         bias=vecs[:, 0:1], scale=vecs[:, 4:5]).then_inc(s_qx, 1)

            for i in range(9):
                if i < 8:
                    squares(i)
                if i >= 1:
                    rows(i - 1)

            for g in range(4):
                act.wait_ge(s_pl, 2 * g + 1)
                nc.scalar.activation(rq[:, g, :], ps[:, 4, :], ACT.Copy).then_inc(s_pq, 1)

            def flat(v):
                return v.rearrange("p k h q -> p (k h q)")

            def roots(gg):
                act.wait_ge(s_rt, 8 * (gg + 1))
                if gg >= 2:
                    act.wait_ge(s_ra, gg - 1)
                nc.scalar.activation(flat(root[:, gg % 2, :, :, :]), flat(ratio[:, gg % 2, :, :, :]),
                                     ACT.Sqrt, scale=2.0)
                nc.scalar.activation(flat(ratio[:, gg % 2, :, :, :]), flat(ratio[:, gg % 2, :, :, :]),
                                     ACT.Sqrt, scale=2.0, bias=vecs[:, 5:6]).then_inc(s_r2, 1)

            def logarithms(gg, g):
                act.wait_ge(s_ra, gg + 1)
                nc.scalar.activation(flat(weight[:, g, :, :, :]), flat(weight[:, g, :, :, :]),
                                     ACT.Ln).then_inc(s_lg, 1)

            def weights(gg, g):
                act.wait_ge(s_lg, gg + 1)
                nc.scalar.activation(flat(weight[:, g, :, :, :]), flat(weight[:, g, :, :, :]),
                                     ACT.Exp, scale=-2.0).then_inc(s_wt, 1)

            for b in range(B):
                for g in range(4):
                    roots(4 * b + g)
                for g in range(4):
                    logarithms(4 * b + g, g)
                for g in range(4):
                    weights(4 * b + g, g)
            take_xnT(2 * NC, 0)
            root_of_variance(act, 2)

            act.wait_ge(s_bt, 1)
            nc.scalar.activation(b1_T[:, :], ps[:, 7, 0:E * NC], ACT.Copy).then_inc(s_bc, 1)
            take_xnT(3 * NC, 4)
            act.wait_ge(s_g, 2)
            nc.scalar.activation(ge[:, :, :], lg[:, :, :], ACT.Exp).then_inc(s_ge, 1)
            act.wait_ge(s_bt, 2)
            nc.scalar.activation(best_T[:, :], ps[0:E, 7, :], ACT.Copy).then_inc(s_bc, 1)
            nc.scalar.activation(best_b[:, :], ps[0:E, 7, :], ACT.Copy).then_inc(s_bc, 1)
            act.wait_ge(s_bc, 1)
            for i in range(E * NC):
                act.wait_ge(s_h, i + 1)
                if i >= 2:
                    act.wait_ge(s_hm, i - 1)
                nc.scalar.activation(hid[:, i % 2, :], ps[:, 4 + i % 2, :], ACT.Gelu,
                                     bias=b1_T[:, i:i + 1]).then_inc(s_hg, 1)

        def row_vectors(dve):
            done = [0]

            def link(i):
                done[0] += 1
                i.then_inc(s_dv, 1)
                dve.wait_ge(s_dv, done[0])

            def ones_at(out, columns):
                return nc.vector.tensor_reduce(out, columns, AX.XY if len(columns.shape) > 2 else AX.X,
                                               ALU.add)

            for i, r in enumerate((16, 17)):
                ones_at(vecs[:, i:i + 1], ident[:, r:P:32])
            ones_at(vecs[:, 3:4], ident[:, :].rearrange("p (j d) -> p j d", d=32)[:, :, 0:SD])
            nc.vector.memset(vecs[:, 5:6], 2.0)
            for r in range(4):
                ones_at(rvec[:, r:r + 1], ident[:, r:P:4])
            ones_at(rvec[:, 4:5], ident[:, 0:64])
            link(ones_at(rvec[:, 5:6], ident[:, 64:P]))
            nc.vector.tensor_scalar(vecs[:, 4:5], vecs[:, 3:4], -3.0, 1.0, ALU.mult, ALU.add)
            r0, r1, r2, r3, rq_, rk_ = (rvec[:, i:i + 1] for i in range(6))
            sign, value, first, temp = (rvec[:, i:i + 1] for i in range(6, 10))
            nc.vector.tensor_tensor(first, r0, r1, ALU.add)
            link(nc.vector.tensor_tensor(temp, r2, r3, ALU.add))
            nc.vector.tensor_scalar(value, rk_, 1e6, rq_, ALU.mult, ALU.add).then_inc(s_vec, 1)
            dve.wait_ge(s_vec, 1)
            link(nc.vector.tensor_tensor(value, value, temp, ALU.mult))
            link(nc.vector.tensor_tensor(temp, r2, r3, ALU.subtract))
            link(nc.vector.tensor_tensor(sign, rk_, rq_, ALU.subtract))
            link(nc.vector.tensor_tensor(temp, temp, sign, ALU.mult))
            link(nc.vector.tensor_tensor(sign, r0, r1, ALU.subtract))
            nc.vector.tensor_tensor(sign, sign, temp, ALU.add).then_inc(s_vec, 1)
            assert done[0] == DV

        def tail_dve(dve, layernorm):
            def residual(part, count):
                for t in range(NT):
                    dve.wait_ge(s_y, count(t))
                    nc.vector.tensor_tensor(x_sb[:, t, :], x_sb[:, t, :], ps[:, t, 0:D], ALU.add) \
                        .then_inc(s_x1, 1)
                dve.wait_ge(s_x1, NT * (part + 1))

            layernorm(1)
            done = [0]

            def link(i):
                done[0] += 1
                i.then_inc(s_iq, 1)
                dve.wait_ge(s_iq, done[0])

            dve.wait_ge(s_sl, 8)
            link(nc.vector.tensor_scalar(inv, ps[:, 6, :], -1.0, 1.0, ALU.mult, ALU.add))
            link(nc.vector.tensor_scalar(inv_t, inv, 0.0, 1e-18, ALU.is_equal, ALU.mult))
            link(nc.vector.tensor_tensor(inv, inv, inv_t, ALU.add))
            link(nc.vector.reciprocal(inv, inv))
            link(nc.vector.tensor_scalar(inv, inv, rvec[:, 6:7], 0.0, ALU.mult, ALU.max))
            link(nc.vector.tensor_scalar(inv_t, inv, 0.0, rvec[:, 7:8], ALU.is_gt, ALU.mult))
            link(nc.vector.scalar_tensor_tensor(inv, inv, rvec[:, 8:9], inv_t, ALU.mult, ALU.add))
            for i in range(3):
                link(nc.vector.tensor_copy(inv_p[:, i, :], inv))
                if i < 2:
                    link(nc.vector.tensor_tensor(inv, inv, inv_p[:, i, :], ALU.subtract))
            for g in range(4):
                dve.wait_ge(s_pl, 2 * g + 2)
                nc.vector.tensor_copy(rk[:, g, :], ps[:, 5, :]).then_inc(s_pk, 1)

            def ratios(m, gg, kt, jj):
                dve.wait_ge(s_dd, m + 1)
                if kt == 0 and jj == 0 and gg >= 2:
                    dve.wait_ge(s_ra, gg - 1)
                heads = slice(2 * jj, 2 * jj + 2)
                part = ratio[:, gg % 2, kt, heads, :]
                nc.vector.tensor_scalar(part, ps[:, heads, 0:TQ], 0.0, None, ALU.max) \
                    .then_inc(s_rt, 1)
                dve.wait_ge(s_rt, 2 * m + 1)
                nc.vector.scalar_tensor_tensor(part, ps[:, heads, TQ:2 * TQ], 1e6, part,
                                               ALU.min, ALU.mult).then_inc(s_rt, 1)

            def take_average(gg):
                dve.wait_ge(s_o, gg + 1)
                if gg >= 2:
                    dve.wait_ge(s_ot, gg - 1)
                nc.vector.tensor_copy(o_T[:, gg % 2, :], ps[:, 4 + gg % 2, 0:TQ]).then_inc(s_oe, 1)

            def normalise(b):
                dve.wait_ge(s_ot, 4 * (b + 1))
                o = ps[:, 6:8, :].rearrange("p t (h d) -> p t h d", h=SH)
                for t in range(2):
                    i = nc.vector.reciprocal(orec[:, b, t, :], o[:, t, :, SD])
                i.then_inc(s_dv, 1)
                dve.wait_ge(s_dv, DV + b + 1)
                for t in range(2):
                    i = nc.vector.tensor_tensor(
                        xn[:, 2 * b + t, :].rearrange("p (h d) -> p h d", h=SH), o[:, t, :, 0:SD],
                        orec[:, b, t, :].unsqueeze(2).to_broadcast([P, SH, SD]), ALU.mult)
                i.then_inc(s_on2, 1)

            for m, gg, b, g, kt, jj in attn_units():
                ratios(m, gg, kt, jj)
                if (b, g, kt, jj) == (1, 1, 1, 1):
                    for done in range(4):
                        take_average(done)
                    normalise(0)
            for gg in range(4, 8):
                take_average(gg)
            normalise(1)
            residual(0, lambda t: t + 1)
            layernorm(2)

            def per_token(v):
                return v.unsqueeze(2).to_broadcast([P, NT, E])

            dve.wait_ge(s_gl, 1)
            logits = ps[:, 6, 0:NT * E].rearrange("p (t e) -> p t e", e=E)
            nc.vector.tensor_reduce(gs[:, 0, :], logits, AX.X, ALU.max).then_inc(s_g, 1)
            dve.wait_ge(s_g, 1)
            nc.vector.tensor_tensor(lg[:, :, :], logits, per_token(gs[:, 0, :]), ALU.subtract) \
                .then_inc(s_g, 1)
            dve.wait_ge(s_ge, 1)
            nc.vector.tensor_reduce(gs[:, 1, :], ge[:, :, :], AX.X, ALU.add).then_inc(s_g, 1)
            dve.wait_ge(s_g, 3)
            nc.vector.reciprocal(gs[:, 1, :], gs[:, 1, :]).then_inc(s_g, 1)
            dve.wait_ge(s_g, 4)
            nc.vector.tensor_tensor(lg[:, :, :], ge[:, :, :], per_token(gs[:, 1, :]), ALU.mult) \
                .then_inc(s_g, 1)
            dve.wait_ge(s_g, 5)
            nc.vector.tensor_reduce(gs[:, 2, :], lg[:, :, :], AX.X, ALU.max).then_inc(s_g, 1)
            dve.wait_ge(s_g, 6)
            nc.vector.tensor_tensor(best[:, :, :], lg[:, :, :], per_token(gs[:, 2, :]), ALU.is_equal) \
                .then_inc(s_g, 1)
            dve.wait_ge(s_g, 7)
            dve.wait_ge(s_tc, TC)
            nc.vector.tensor_tensor(best[:, :, :], best[:, :, :], rank[:, :, :], ALU.mult) \
                .then_inc(s_g, 1)
            dve.wait_ge(s_g, 8)
            nc.vector.tensor_reduce(gs[:, 3, :], best[:, :, :], AX.X, ALU.max).then_inc(s_g, 1)
            dve.wait_ge(s_g, 9)
            nc.vector.tensor_tensor(best[:, :, :], best[:, :, :], per_token(gs[:, 3, :]),
                                    ALU.is_equal).then_inc(s_g, 1)
            for i in range(E * NC):
                e, it = divmod(i, NC)
                dve.wait_ge(s_hg, i + 1)
                dve.wait_ge(s_bt, 3 + e)
                if i >= 2:
                    dve.wait_ge(s_y, NT + i - 1)
                nc.vector.tensor_tensor(hid_m[:, i % 2, :], hid[:, i % 2, :], ps[:, 6 + e % 2, :],
                                        ALU.mult).then_inc(s_hm, 1)
            residual(1, lambda t: NT + E * NC)

        block = stack.enter_context(nc.Block())

        @block.sync
        def _(sp):
            wqk_cols = [w.rearrange("(c p) n -> p c n", p=P) for w in (wq, wk)]
            wv_cols = wv.rearrange("(c p) n -> p c n", p=P)

            def load_wqk(par, hp):
                for i, w in enumerate(wqk_cols):
                    sp.dma_start(wqk_raw[:, par, i, :, :], w[:, :, bass.ds(hp * P, P)]) \
                        .then_inc(s_wqk[par], 16)

            def load_wv(par, hp):
                sp.dma_start(wv_raw[:, par, :, :], wv_cols[:, :, bass.ds(hp * P, P)]) \
                    .then_inc(s_wv[par], 16)

            def load_wo(par, hp):
                sp.dma_start(wo_raw[:, par, :], wo[bass.ds(hp * P, P), :]).then_inc(s_wo[par], 16)

            def copy_k2(n, par):
                for half in range(2):
                    sp.wait_ge(s_kh, n * (2 * KCH) + KCH * (half + 1))
                    keys = slice(half * (TK // 2), (half + 1) * (TK // 2))
                    for h in range(2):
                        rows = slice(64 * h, 64 * h + 64)
                        sp.dma_start(k2[rows, par, h, keys], k1[rows, par, h, keys]) \
                            .then_inc(s_k2[half], 16)

            sp.dma_start(x_sb[:, :, :], x.rearrange("b (t p) c -> p (b t) c", p=P)).then_inc(s_x, 16)
            chunks = ctx.rearrange("b (n p t) c -> b n p t c", p=P, t=8)
            for n in range(4):
                for b in range(B):
                    if n >= 2:
                        sp.wait_ge(s_tp, 2 * (2 * (2 * n - 3) + b) + 2)
                    sp.dma_start(stage[b][:, n % 2, :, :], chunks[b, n, :, :, :]) \
                        .then_inc(s_ctx[2 * b + n % 2], 16)
                    if (n, b) == (0, 0):
                        load_wqk(0, 0)
                if n == 1:
                    load_wv(0, 0)
                    load_wqk(1, 0)
            copy_k2(0, 0)

            def step(hp, b):
                n = step_of(hp, b)
                last_pair = isinstance(hp, int) and hp == HP - 1
                if not last_pair:
                    sp.wait_ge(s_q, n + 1)
                    sp.wait_ge(s_wkl, n + 1)
                    load_wqk(b, hp + 1)
                if prepares(hp, b):
                    at_least(sp, s_wvl, n)
                    load_wv(1 - b, hp + b)
                at_least(sp, s_yx, n - 1)
                load_wo(b, hp)
                if prepares(hp, b):
                    copy_k2(n + 1, 1 - b)

            step(0, 0)
            step(0, 1)
            with sp.Fori(1, HP - 1) as hp:
                step(hp, 0)
                step(hp, 1)
            step(HP - 1, 0)
            step(HP - 1, 1)
            tail_sp(sp)

        @block.tensor
        def _(pe):
            def transposes_x():
                pe.wait_ge(s_ln, LN)
                for c in range(NC):
                    for t in range(NT):
                        mm = pe.transpose(ps[:, MX + c, t * P:(t + 1) * P],
                                          xn[:, t, c * P:(c + 1) * P], ident[:, :])
                    mm.then_inc(s_xt, 1)

            def transposes_ctx(u):
                b, n, half, _ = context_pair(u)
                pe.wait_ge(s_ctx[2 * b + n % 2], 16 * (n // 2 + 1))
                for c in range(NC):
                    if u >= 1:
                        pe.wait_ge((s_tl[0], s_th)[c], (1, 2)[c] * u)
                    for t in range(4):
                        mm = pe.transpose(ps[:, TURNED[c], t * P:(t + 1) * P],
                                          stage[b][:, n % 2, 4 * half + t, c * P:(c + 1) * P],
                                          ident[:, :])
                    mm.then_inc(s_tp, 1)

            def project_q(n, par):
                at_least(pe, s_mr, n)
                pe.wait_ge(s_wqk[par], load_count(n, par, 32))
                for c in range(NC):
                    mm = pe.matmul(ps[:, PM, 0:TQ], wqk_raw[:, par, 0, c, :],
                                   xnT[:, c, par * TQ:(par + 1) * TQ],
                                   start=(c == 0), stop=(c == NC - 1))
                mm.then_inc(s_q, 1)

            def project_k(j, n, par):
                at_least(pe, s_kl, n * KCH + j)
                if j == 0:
                    pe.wait_ge(s_wkl, n + 1)
                keys = slice(512 * j, 512 * (j + 1))
                k = 0
                for c in range(NC):
                    for w, y in ((wk_hi, ctx_hi), (wk_hi, ctx_lo), (wk_lo, ctx_hi)):
                        mm = pe.matmul(ps[:, PK, :], w[:, par, c, :], y[:, par, c, keys],
                                       start=(k == 0), stop=(k == 5))
                        k += 1
                mm.then_inc(s_k, 1)

            def project_v(j, n, par):
                at_least(pe, s_vc, n * KCH + j)
                if j == 0:
                    pe.wait_ge(s_wvl, n + 1)
                for t in range(CS):
                    toks = slice((CS * j + t) * P, (CS * j + t + 1) * P)
                    k = 0
                    for c in range(NC):
                        for y, w in ((ctx_hi, wv_hi), (ctx_hi, wv_lo), (ctx_lo, wv_hi)):
                            mm = pe.matmul(ps[:, PV, t * P:(t + 1) * P], y[:, par, c, toks],
                                           w[:, par, c, :], start=(k == 0), stop=(k == 5))
                            k += 1
                mm.then_inc(s_v, 1)

            def maxima(u, n, par):
                j, t = divmod(u, 2)
                bank = MX
                if isinstance(n, int) and n == 0:
                    bank = (MX, SC)[u % 2]
                    at_least(pe, s_red, u - 1)
                else:
                    pe.wait_ge(s_red, n * NU + u)
                pe.wait_ge(s_kh, n * (2 * KCH) + 2 * (j + 1))
                if u == 0:
                    pe.wait_ge(s_qh, n + 1)
                for h in range(2):
                    rows = slice(64 * h, 64 * h + 64)
                    mm = pe.matmul(ps[:, bank + 1 - h, :], q1[rows, par, h, t * P:(t + 1) * P],
                                   k1[rows, par, h, 512 * j:512 * (j + 1)], start=True, stop=True)
                mm.then_inc(s_mx, 1)

            def max_rows(n, earlier):
                pe.wait_ge(s_ql, n + 1)
                at_least(pe, s_ya, n - 1 if earlier else 0)
                pe.wait_ge(s_mn, n + 1)
                for t in range(2):
                    mm = pe.transpose(ps[:, PM, t * P:(t + 1) * P], m_neg[:, t, :], ident[:, :])
                mm.then_inc(s_mt, 1)

            def sums(n, par, q_step):
                if q_step is not None:
                    pe.wait_ge(s_ql, q_step + 1)
                pe.wait_ge(s_ps, summed(n, SLOTS - 1))
                for k in range(2):
                    for h in range(2):
                        mm = pe.matmul(ps[64 * h:64 * h + 64, PM, 0:TQ], sixteen[:, :],
                                       psums[:, par, k, h, :], start=(k == 0), stop=(k == 1))
                mm.then_inc(s_sum, 1)

            def project_o(n, par):
                pe.wait_ge(s_on, n + 1)
                pe.wait_ge(s_wo[par], load_count(n, par, 16))
                for t in range(2):
                    mm = pe.matmul(ps[:, PM, t * TQ:(t + 1) * TQ], o_norm[:, t * P:(t + 1) * P],
                                   wo_raw[:, par, :], start=True, stop=True)
                mm.then_inc(s_yx, 1)

            def scores(g, s, n, par):
                at_least(pe, s_exp, g - 1)
                if s == 0:
                    pe.wait_ge(s_mr, n + 1)
                    pe.wait_ge(s_kl, n * KCH + KCH)
                if s % (SLOTS // 2) == 0:
                    pe.wait_ge(s_k2[2 * s // SLOTS], (n + 1) * 32)
                keys = slice(s * P, (s + 1) * P)
                for h in range(2):
                    cols = slice(h * TQ, (h + 1) * TQ)
                    pe.matmul(ps[:, SC + s % 2, cols], k1[:, par, h, keys], q1[:, par, h, :],
                              start=True, stop=False)
                    mm = pe.matmul(ps[:, SC + s % 2, cols], k2[:, par, h, keys], q2[:, par, h, :],
                                   start=False, stop=True)
                mm.then_inc(s_sc, 1)

            def pv(g, s, n):
                pe.wait_ge(s_exp, g + 1)
                if s == 0:
                    at_least(pe, s_or, n)
                if s % CS == 0:
                    pe.wait_ge(s_vc, n * KCH + s // CS + 1)
                for h in range(2):
                    mm = pe.matmul(ps[64 * h:64 * h + 64, ACC, 0:TQ],
                                   v_sb[:, s // CS % NV, s % CS, 64 * h:64 * h + 64],
                                   probs[:, s % NP, h, :], start=(s == 0), stop=(s == SLOTS - 1))
                mm.then_inc(s_pv, 1)

            def step(hp, b):
                n, more, first = step_of(hp, b), prepares(hp, b), first_step(hp, b)
                for s in range(SLOTS):
                    scores(slot_of(hp, b, s), s, n, b)
                    if s in MAX_AT and more:
                        maxima(MAX_AT[s], n + 1, 1 - b)
                    if s == M_AT and more:
                        max_rows(n + 1, not first)
                    if s >= 1:
                        pv(slot_of(hp, b, s - 1), s - 1, n)
                    elif not first:
                        pv(slot_of(hp, b, s - 1), SLOTS - 1, n - 1)
                    if s == Q_AT and more:
                        project_q(n + 1, 1 - b)
                    if s in K_AT and more:
                        project_k(K_AT[s], n + 1, 1 - b)
                    if s in V_AT and V_AT[s]:
                        project_v(V_AT[s], n, b)
                    elif s in V_AT and more:
                        project_v(0, n + 1, 1 - b)
                    if s == SUM_AT and not first:
                        sums(n - 1, 1 - b, n + 1 if more else None)
                    if s == Y_AT and not first:
                        project_o(n - 1, 1 - b)
                    if s in TURN_AT and not more:
                        turn_weights(pe, TURN_AT[s])

            pe.wait_ge(s_const, 3)
            for j in range(KCH + 2):
                if j < KCH:
                    transposes_ctx(2 * j)
                if j == 0:
                    transposes_x()
                    pe.wait_ge(s_xc, NC)
                    project_q(0, 0)
                if j == KCH:
                    pe.wait_ge(s_th, 4 * KCH)
                    project_v(0, 0, 0)
                if 1 <= j <= KCH:
                    for c in range(NC):
                        pe.wait_ge(s_tl[c], 2 * (j - 1) + 1)
                    project_k(j - 1, 0, 0)
                if j >= 2:
                    maxima(2 * (j - 2), 0, 0)
                if j < KCH:
                    transposes_ctx(2 * j + 1)
                if j >= 2:
                    maxima(2 * (j - 2) + 1, 0, 0)
            max_rows(0, False)
            pe.wait_ge(s_const, 5)
            for c in range(NC):
                pe.wait_ge(s_tl[c], 2 * KCH)
            pe.wait_ge(s_red, NU)
            step(0, 0)
            step(0, 1)
            with pe.Fori(1, HP - 1) as hp:
                step(hp, 0)
                step(hp, 1)
            step(HP - 1, 0)
            step(HP - 1, 1)
            pv(STEPS * SLOTS - 1, SLOTS - 1, STEPS - 1)
            pe.wait_ge(s_ya, STEPS - 1)
            sums(STEPS - 1, 1, None)
            project_o(STEPS - 1, 1)
            tail_pe(pe)

        @block.scalar
        def _(act):
            def split_k(n, par):
                act.wait_ge(s_wqk[par], load_count(n, par, 32))
                at_least(act, s_k, (n - 1) * KCH)
                nc.scalar.activation(wk_hi[:, par, :, :], wqk_raw[:, par, 1, :, :], ACT.Copy,
                                     scale=WS).then_inc(s_wkh, 1)

            def split_v(n, par):
                act.wait_ge(s_wv[par], load_count(n, par, 16))
                at_least(act, s_v, (n - 1) * KCH)
                nc.scalar.activation(wv_hi[:, par, :, :], wv_raw[:, par, :, :], ACT.Copy,
                                     scale=WS).then_inc(s_wvh, 1)

            def take_q(n, par):
                act.wait_ge(s_q, n + 1)
                for h in range(2):
                    for half in range(2):
                        i = nc.scalar.activation(q1[64 * half:64 * half + 64, par, h, :],
                                                 ps[64 * h:64 * h + 64, PM, 0:TQ], ACT.Copy)
                i.then_inc(s_qh, 1)

            def take_k(j, n, par):
                act.wait_ge(s_k, n * KCH + j + 1)
                for h in range(2):
                    rows = slice(64 * h, 64 * h + 64)
                    nc.scalar.activation(k1[rows, par, h, 512 * j:512 * (j + 1)], ps[rows, PK, :],
                                         ACT.Copy).then_inc(s_kh, 1)

            def take_v(j, n):
                act.wait_ge(s_v, n * KCH + j + 1)
                nc.scalar.activation(v_sb[:, j % NV, :, :],
                                     ps[:, PV, :].rearrange("p (t n) -> p t n", t=CS),
                                     ACT.Copy).then_inc(s_vc, 1)

            def take_max(n, par):
                act.wait_ge(s_mt, n + 1)
                nc.scalar.activation(q2[64:P, par, 0, :], ps[64:P, PM, 0:TQ], ACT.Copy,
                                     scale=1.0 / MS)
                nc.scalar.activation(q2[0:64, par, 1, :], ps[0:64, PM, 0:TQ], ACT.Copy,
                                     scale=1.0 / MS).then_inc(s_mr, 1)

            def context(u):
                b, _, _, keys = context_pair(u)
                for c in range(NC):
                    act.wait_ge(s_tp, 2 * u + c + 1)
                    i = nc.scalar.activation(ctx_hi[:, b, c, keys], ps[:, TURNED[c], :], ACT.Copy)
                    if c == 1:
                        if u >= 4:
                            act.wait_ge(s_tl[1], u - 3)
                        i = nc.scalar.activation(copies[:, u % 4, :], ps[:, TURNED[c], :], ACT.Copy)
                    i.then_inc(s_th, 1)

            def step(hp, b):
                n, more = step_of(hp, b), prepares(hp, b)
                for s in range(SLOTS):
                    g = slot_of(hp, b, s)
                    act.wait_ge(s_sc, g + 1)
                    at_least(act, s_pv, g - NP + 1)
                    if s % 2 == 0 and not (first_step(hp, b) and s < NP):
                        act.wait_ge(s_ps, summed(n, s - NP))
                    nc.scalar.activation(probs[:, s % NP, :, :],
                                         ps[:, SC + s % 2, :].rearrange("p (h q) -> p h q", h=2),
                                         ACT.Exp, scale=XSCALE).then_inc(s_exp, 1)
                    if s == M_AT and more:
                        take_max(n + 1, 1 - b)
                    if s == Q_AT and more:
                        take_q(n + 1, 1 - b)
                    if s in K_AT and more:
                        take_k(K_AT[s], n + 1, 1 - b)
                    if s in V_AT and V_AT[s]:
                        take_v(V_AT[s], n)
                    elif s in V_AT and more:
                        take_v(0, n + 1)
                    if s == SPLIT_K_AT and not (isinstance(hp, int) and hp == HP - 1):
                        split_k(n + 2, b)
                    if s == SPLIT_V_AT and more:
                        split_v(n + 1, 1 - b)
                    if s in TURN_AT and not more:
                        take_turned(act, TURN_AT[s])

            root_of_variance(act, 0)
            for j in range(KCH + 1):
                if j < KCH:
                    context(2 * j)
                if j == 0:
                    act.wait_ge(s_xt, NC)
                    for c in range(NC):
                        nc.scalar.activation(xnT[:, c, :], ps[:, MX + c, :], ACT.Copy) \
                            .then_inc(s_xc, 1)
                    take_q(0, 0)
                    split_k(0, 0)
                if j == 3:
                    split_v(0, 0)
                if j == 4:
                    split_k(1, 1)
                if j == KCH:
                    take_v(0, 0)
                if j >= 1:
                    take_k(j - 1, 0, 0)
                if j < KCH:
                    context(2 * j + 1)
            take_max(0, 0)
            step(0, 0)
            step(0, 1)
            with act.Fori(1, HP - 1) as hp:
                step(hp, 0)
                step(hp, 1)
            step(HP - 1, 0)
            step(HP - 1, 1)
            tail_act(act)

        @block.vector
        def _(dve):
            def layernorm(part):
                done = [LN * part]

                def link(i):
                    done[0] += 1
                    i.then_inc(s_ln, 1)
                    dve.wait_ge(s_ln, done[0])

                for t in range(NT):
                    i = nc.vector.bn_stats(stats[:, t, :], x_sb[:, t, :])
                link(i)
                for t in range(NT):
                    i = nc.vector.bn_aggr(mv[:, t, :], stats[:, t, :])
                link(i)
                link(nc.vector.tensor_scalar(var[:, :], mv[:, :, 1], EPS, None, ALU.add))
                dve.wait_ge(s_sd, part + 1)
                link(nc.vector.reciprocal(rstd[:, :], rstd[:, :]))
                link(nc.vector.tensor_tensor(newton[:, :], rstd[:, :], rstd[:, :], ALU.mult))
                link(nc.vector.tensor_tensor(newton[:, :], newton[:, :], var[:, :], ALU.mult))
                link(nc.vector.tensor_scalar(newton[:, :], newton[:, :], -0.5, 1.5, ALU.mult, ALU.add))
                link(nc.vector.tensor_tensor(rstd[:, :], rstd[:, :], newton[:, :], ALU.mult))
                for t in range(NT):
                    i = nc.vector.tensor_scalar(xn[:, t, :], x_sb[:, t, :], mv[:, t, 0:1],
                                                rstd[:, t:t + 1], ALU.subtract, ALU.mult)
                i.then_inc(s_ln, 1)

            def low_part(lo, raw, hi):
                return nc.vector.scalar_tensor_tensor(
                    lo.rearrange("p c n -> p (c n)"), raw.rearrange("p c n -> p (c n)"), WS,
                    hi.rearrange("p c n -> p (c n)"), ALU.mult, ALU.subtract)

            def split_k(n, par):
                dve.wait_ge(s_wkh, n + 1)
                low_part(wk_lo[:, par, :, :], wqk_raw[:, par, 1, :, :], wk_hi[:, par, :, :]) \
                    .then_inc(s_wkl, 1)

            def split_v(n, par):
                dve.wait_ge(s_wvh, n + 1)
                low_part(wv_lo[:, par, :, :], wv_raw[:, par, :, :], wv_hi[:, par, :, :]) \
                    .then_inc(s_wvl, 1)

            def take_q(n, par):
                dve.wait_ge(s_qh, n + 1)
                for h in range(2):
                    rows = slice(64 * h, 64 * h + 64)
                    i = nc.vector.tensor_tensor(q2[rows, par, h, :], ps[rows, PM, 0:TQ],
                                                q1[rows, par, h, :], ALU.subtract)
                i.then_inc(s_ql, 1)

            def take_k(j, n, par):
                keys = slice(512 * j, 512 * (j + 1))
                for h in range(2):
                    dve.wait_ge(s_kh, n * (2 * KCH) + 2 * j + h + 1)
                    rows, other = slice(64 * h, 64 * h + 64), slice(64 - 64 * h, P - 64 * h)
                    i = nc.vector.tensor_tensor(k1[other, par, h, keys], ps[rows, PK, :],
                                                k1[rows, par, h, keys], ALU.subtract)
                i.then_inc(s_kl, 1)

            def maxima(u, n):
                j, t = divmod(u, 2)
                dve.wait_ge(s_mx, n * NU + u + 1)
                if u == 0:
                    at_least(dve, s_mn, n)
                bank = SC if isinstance(n, int) and n == 0 and t == 1 else MX
                nc.vector.tensor_reduce(m_part[:, j, t, :], ps[:, bank:bank + 2, :], AX.X, ALU.max) \
                    .then_inc(s_red, 1)

            def take_max(n):
                dve.wait_ge(s_red, n * NU + NU)
                at_least(dve, s_mt, n)
                nc.vector.tensor_reduce(m_neg[:, :, 0:P:64], m_part[:, :, :, :].rearrange(
                    "p j t h -> p t h j"), AX.X, ALU.max, negate=True).then_inc(s_mn, 1)

            def context(u):
                b, _, _, keys = context_pair(u)
                dve.wait_ge(s_th, 2 * u + 1)
                nc.vector.tensor_tensor(ctx_lo[:, b, 0, keys], ps[:, TURNED[0], :],
                                        ctx_hi[:, b, 0, keys], ALU.subtract).then_inc(s_tl[0], 1)

            def take_output(n, g):
                dve.wait_ge(s_pv, g + 1)
                at_least(dve, s_on, n)
                nc.vector.tensor_copy(o_raw[:, :], ps[:, ACC, 0:TQ]).then_inc(s_or, 1)

            def normalise(n):
                dve.wait_ge(s_sum, n + 1)
                nc.vector.reciprocal(o_rec[:, :], ps[:, PM, 0:TQ]).then_inc(s_rs, 1)
                dve.wait_ge(s_or, n + 1)
                dve.wait_ge(s_rs, n + 1)
                at_least(dve, s_yx, n)
                nc.vector.tensor_tensor(o_norm[:, :], o_raw[:, :], o_rec[:, :], ALU.mult) \
                    .then_inc(s_on, 1)

            def add_output(n, par):
                dve.wait_ge(s_yx, n + 1)
                at_least(dve, s_ya, n - 1)
                rows = x_sb[:, 2 * par:2 * par + 2, :].rearrange("p t c -> p (t c)")
                nc.vector.tensor_tensor(rows, rows, ps[:, PM, :], ALU.add).then_inc(s_ya, 1)

            def step(hp, b):
                n, more, first = step_of(hp, b), prepares(hp, b), first_step(hp, b)
                for s in range(SLOTS):
                    if s in MAX_AT and more:
                        maxima(MAX_AT[s], n + 1)
                    if s == max(MAX_AT) and more:
                        take_max(n + 1)
                    if s == 0 and not first:
                        take_output(n - 1, slot_of(hp, b, -1))
                    if s == Q_AT and more:
                        take_q(n + 1, 1 - b)
                    if s in K_AT and more:
                        take_k(K_AT[s], n + 1, 1 - b)
                    if s == SUM_AT and not first:
                        normalise(n - 1)
                    if s == Y_AT and not first:
                        add_output(n - 1, 1 - b)
                    if s == SPLIT_K_AT and not (isinstance(hp, int) and hp == HP - 1):
                        split_k(n + 2, b)
                    if s == SPLIT_V_AT and more:
                        split_v(n + 1, 1 - b)

            dve.wait_ge(s_x, 16)
            layernorm(0)
            nc.vector.memset(m_neg[:, :, :], 0.0).then_inc(s_mz, 1)
            dve.wait_ge(s_mz, 1)
            for j in range(KCH + 2):
                if j < KCH:
                    context(2 * j)
                if j == 0:
                    take_q(0, 0)
                    split_k(0, 0)
                if j == 3:
                    split_v(0, 0)
                if j == 4:
                    split_k(1, 1)
                if 1 <= j <= KCH:
                    take_k(j - 1, 0, 0)
                if j >= 2:
                    maxima(2 * (j - 2), 0)
                if j < KCH:
                    context(2 * j + 1)
                if j >= 2:
                    maxima(2 * (j - 2) + 1, 0)
            take_max(0)
            dve.wait_ge(s_const, 5)
            row_vectors(dve)
            step(0, 0)
            step(0, 1)
            with dve.Fori(1, HP - 1) as hp:
                step(hp, 0)
                step(hp, 1)
            step(HP - 1, 0)
            step(HP - 1, 1)
            take_output(STEPS - 1, STEPS * SLOTS - 1)
            normalise(STEPS - 1)
            add_output(STEPS - 1, 1)
            dve.wait_ge(s_ya, STEPS)
            tail_dve(dve, layernorm)

        @block.gpsimd
        def _(pool):
            nc.gpsimd.memset(ident[:, :], 0.0).then_inc(s_const, 1)
            nc.gpsimd.memset(sixteen[:, :], WS).then_inc(s_const, 1)
            pool.wait_ge(s_const, 2)
            nc.gpsimd.affine_select(out=ident[:, :], in_=ident[:, :], compare_op=ALU.not_equal,
                                    fill=1.0, base=0, pattern=[[-1, P]], channel_multiplier=1) \
                .then_inc(s_const, 1)
            for u in range(2 * KCH):
                b, _, _, keys = context_pair(u)
                pool.wait_ge(s_th, 2 * u + 2)
                nc.gpsimd.tensor_tensor(ctx_lo[:, b, 1, keys], copies[:, u % 4, :],
                                        ctx_hi[:, b, 1, keys], ALU.subtract).then_inc(s_tl[1], 1)
                if u in (7, 11):
                    h = (u - 7) // 4
                    pool.wait_ge(s_tl[1], u + 1)
                    nc.gpsimd.memset(k2[64 - 64 * h:P - 64 * h, :, h, :], MS).then_inc(s_const, 1)
                    pool.wait_ge(s_const, 4 + h)
            pool.wait_ge(s_tl[1], 2 * KCH)
            tail_constants(pool)

            def step(hp, b):
                n = step_of(hp, b)
                total = psums[:, b, :, :, :].rearrange("p k h q -> p (k h q)")
                pairs = [probs[:, i:i + 2, :, :].rearrange("p k h q -> p (k h q)")
                         for i in range(0, NP, 2)]
                for s in range(3, SLOTS, 2):
                    if s == 5 and not prepares(hp, b):
                        zero_rows(pool)
                    pool.wait_ge(s_exp, slot_of(hp, b, s) + 1)
                    if s == 3:
                        at_least(pool, s_sum, n - 1)
                    else:
                        pool.wait_ge(s_ps, summed(n, s - 2))
                    nc.gpsimd.tensor_tensor(total, pairs[0] if s == 3 else total,
                                            pairs[s // 2 % (NP // 2)], ALU.add).then_inc(s_ps, 1)

            step(0, 0)
            step(0, 1)
            with pool.Fori(1, HP - 1) as hp:
                step(hp, 0)
                step(hp, 1)
            step(HP - 1, 0)
            step(HP - 1, 1)
            tail_pool(pool)


_INS = ["x", "ctx_1024", "L0_xattn_w_q", "L0_xattn_w_k", "L0_xattn_w_v", "L0_xattn_w_o", "L0_attn_wq",
        "L0_attn_wk", "L0_attn_wv", "L0_attn_wo", "L0_ffn_Wg", "L0_ffn_bg", "L0_ffn_W1", "L0_ffn_b1",
        "L0_ffn_W2", "L0_ffn_b2"]


def kernel(**inputs):
    import numpy as _np
    import concourse.bacc as _bacc
    from concourse import mybir as _mybir
    from concourse.bass_utils import run_bass_kernel_spmd as _run

    nc = _bacc.Bacc("TRN2", target_bir_lowering=False, num_devices=1)
    arrays, args = {}, []
    for name in _INS:
        a = _np.ascontiguousarray(inputs[name])
        arrays[f"in_{name}_dram"] = a
        args.append(nc.dram_tensor(f"in_{name}_dram", a.shape, _mybir.dt.from_np(a.dtype),
                                   kind="ExternalInput").ap())
    args.append(nc.dram_tensor("out_0_dram", (B, TQ, D), FP32, kind="ExternalOutput").ap())
    perceiver(nc, *args)
    r = _run(nc, [arrays], core_ids=[0])
    return r.results[0]["out_0_dram"]
```

```python
from contextlib import ExitStack

import concourse.bass as bass
from concourse import mybir

FP32 = mybir.dt.float32
FP16 = mybir.dt.float16
BF16 = mybir.dt.bfloat16
ALU = mybir.AluOpType
ACT = mybir.ActivationFunctionType
AX = mybir.AxisListType

P = 128
B, TQ, TK, D = 2, 256, 4096, 256
T = B * TQ
NT = T // P
NC = D // P
XH, XD = 16, 64
HP = XH // 2
STEPS = HP * B
SLOTS = TK // P
KCH = TK // 512
CS = 512 // P
WS = 16.0
XSCALE = XD ** -0.5 / WS
MS = 256.0
SH, SD = 16, 16
E, F = 8, 256
EPS = 1e-5
ES = 256.0
IQ = 12
DV = 7
TC = 9
LN = 9

SC = 0
ACC = 2
MX = 3
PK = 5
PV = 6
TURNED = (2, 6)
PM = 7

K_AT = {1: 0, 4: 1, 8: 2, 11: 3, 14: 4, 17: 5, 20: 6, 23: 7}
V_AT = {2: 1, 6: 2, 10: 3, 14: 4, 18: 5, 22: 6, 26: 7, 30: 0}
MAX_AT = {3: 0, 5: 1, 7: 2, 9: 3, 11: 4, 13: 5, 14: 6, 16: 7, 17: 8, 18: 9, 20: 10, 22: 11,
          23: 12, 25: 13, 26: 14, 28: 15}
Q_AT, SUM_AT, Y_AT, M_AT = 0, 5, 9, 30
TURN_AT = {20: 0, 23: 1, 27: 2, 29: 3}
TURN_BANK = (MX, MX + 1, PK, MX)
TURN_X = (PK, MX)
RATIO = (0, 1, 3, 0, 1, 0, 2, 1)
EXPERTS_AT = (13, 15, 18, 21, 27, 28, 30, 31)
OUT_BANKS = ((6, 7), (0, 1))
XN_BANK, GATE_BANK = 2, 3
AVERAGE_AT = (24, 27)
PLACE_BANKS = ((0, 1), (4, 5))
ROWS_AHEAD = 3
LN_AT, ROOT_AT, XT_AT = 10, 12, 17
SPLIT_K_AT, SPLIT_V_AT = 16, 12
NU = 2 * KCH
NP = 8
NV = 4


def perceiver(nc, x, ctx, wq, wk, wv, wo, aq, ak, av, ao, gw, gb, w1, b1, w2, b2, out):
    stack = ExitStack()

    def sb(name, shape, dt=FP32):
        return stack.enter_context(nc.sbuf_tensor(name, shape, dt))

    def sem(name):
        return stack.enter_context(nc.semaphore(name))

    with stack:
        ps = stack.enter_context(nc.psum_tensor("ps", [P, 8, 512], FP32))
        ctx_hi = sb("ctx_hi", [P, B, NC, TK], FP16)
        ctx_lo = sb("ctx_lo", [P, B, NC, TK], FP16)
        k1 = sb("k1", [P, B, 2, TK], FP16)
        k2 = sb("k2", [P, B, 2, TK], FP16)
        q1 = sb("q1", [P, B, 2, TQ], FP16)
        q2 = sb("q2", [P, B, 2, TQ], FP16)
        v_sb = sb("v_sb", [P, NV, CS, P])
        probs = sb("probs", [P, NP, 2, TQ])
        psums = sb("psums", [P, B, 2, 2, TQ])
        o_raw = sb("o_raw", [P, TQ])
        o_rec = sb("o_rec", [P, TQ])
        o_norm = sb("o_norm", [P, TQ])
        x_sb = sb("x_sb", [P, NT, D])
        xn = sb("xn", [P, NT, D])
        xnT = sb("xnT", [P, NC, T])
        wqk_raw = sb("wqk_raw", [P, B, 2, NC, P])
        wk_hi = sb("wk_hi", [P, B, NC, P], FP16)
        wk_lo = sb("wk_lo", [P, B, NC, P], FP16)
        wv_raw = sb("wv_raw", [P, B, NC, P])
        wv_hi = sb("wv_hi", [P, B, NC, P], FP16)
        wv_lo = sb("wv_lo", [P, B, NC, P], FP16)
        wo_raw = sb("wo_raw", [P, B, D])
        m_part = sb("m_part", [P, KCH, 2, 2])
        m_neg = sb("m_neg", [P, 2, P])
        ident = sb("ident", [P, P])
        sixteen = sb("sixteen", [P, XD])
        stats = sb("stats", [P, NT, 6])
        mv = sb("mv", [P, NT, 2])
        rstd = sb("rstd", [P, NT])
        var = sb("var", [P, NT])
        newton = sb("newton", [P, NT])

        stage = (probs[:, :, :, :].rearrange("p (n a) h q -> p n (a h q)", n=2)
                 .rearrange("p n (t c) -> p n t c", c=D),
                 k1[:, 1, :, :].rearrange("p h k -> p (h k)").bitcast(FP32)
                 .rearrange("p (n t c) -> p n t c", n=2, c=D))

        copies = psums[:, :, :, :, :].rearrange("p b k h q -> p (b k) (h q)")

        hi32 = ctx_hi[:, :, :, :].rearrange("p b c k -> p (b c k)").bitcast(FP32)
        lo32 = ctx_lo[:, :, :, :].rearrange("p b c k -> p (b c k)").bitcast(FP32)
        w2_p, w1_p = (hi32[:, i:i + 4096].bitcast(FP16).rearrange(
            "p (i e c n) -> p i e c n", i=2, e=E, c=NC)
                      for i in (0, 4096))
        a_raw = lo32[:, 0:2048].rearrange("p (w t n) -> p w t n", w=4, t=NC)
        aqk_T = lo32[:, 2048:4096].rearrange("p (w c h d) -> p w c h d", w=2, c=NC, h=SH)
        avo_T = lo32[:, 4096:5120].rearrange("p (w c n) -> p w c n", w=2, c=NC)
        k1_32 = k1[:, :, :, :].rearrange("p b h k -> p (b h k)").bitcast(FP32)
        k2_32 = k2[:, :, :, :].rearrange("p b h k -> p (b h k)").bitcast(FP32)
        w1_raw = k1_32[:, 0:4096]
        w2_raw = k2_32[:, 0:4096]
        qkx = k1_32[:, 0:4096].bitcast(FP16).rearrange("p (w i g t) -> p w i g t", w=2, i=2, g=4)
        v32 = v_sb[:, :, :, :].rearrange("p n s d -> p (n s d)")
        rq = k1_32[:, 4096:5120].bitcast(BF16).rearrange("p (g t) -> p g t", g=4)
        rk = k1_32[:, 5120:6144].bitcast(BF16).rearrange("p (g t) -> p g t", g=4)
        square = lo32[:, 5120:6144].rearrange("p (n t) -> p n t", n=2)
        inv = lo32[:, 6144:6656]
        inv_t = lo32[:, 6656:7168]
        inv_p = lo32[:, 7168:7936].bitcast(BF16).rearrange("p (i t) -> p i t", i=3)
        p32 = probs[:, :, :, :].rearrange("p n h q -> p (n h q)")
        ratio = [m.rearrange("p (k h q) -> p k h q", k=2, h=4)
                 for m in (k1_32[:, 6144:8192], lo32[:, 0:2048], v32[:, 0:2048],
                           k2_32[:, 6144:8192])]
        root = p32[:, 0:4096].rearrange("p (n k h q) -> p n k h q", n=2, k=2, h=4)
        weight = k2_32[:, 0:8192].rearrange("p (g k h q) -> p g k h q", g=4, k=2, h=4)
        o_T = lo32[:, 5120:5632].rearrange("p (n q) -> p n q", n=2)
        place = v32[:, 0:1536].bitcast(BF16).rearrange("p (w i g n) -> p w i g n", w=2, i=3, g=4)
        hid = k2_32[:, 0:1024].rearrange("p (n t) -> p n t", n=2)
        hid_m = k2_32[:, 1024:2048].rearrange("p (n t) -> p n t", n=2)
        hid_p = k2_32[:, 2048:4096].bitcast(FP16).rearrange("p (n i t) -> p n i t", n=4, i=2)
        xnT_p = k1_32[:, 4096:5120].bitcast(FP16).rearrange("p (i c t) -> p i c t", i=2, c=NC)
        s32 = psums[:, :, :, :, :].rearrange("p b h k q -> p (b h k q)")
        vx = s32[:, 0:2048].rearrange("p (t h d) -> p t h d", t=NT, h=SH)
        orec = sb("orec", [P, B, 2, SH])
        sel = sb("sel", [P, 2, P])
        head_rows = sb("head_rows", [P, 4])
        gather = sb("gather", [P, 240])
        vecs = sb("vecs", [P, 3])
        rvec = sb("rvec", [P, 10])
        ones1 = sb("ones1", [1, P])
        rank = sb("rank", [P, NT, E])
        gw_sb = sb("gw_sb", [P, NC, E])
        gb_sb = sb("gb_sb", [1, E])
        b1_T = sb("b1_T", [P, E * NC])
        lg = sb("lg", [P, NT, E])
        ge = sb("ge", [P, NT, E])
        best = sb("best", [P, NT, E])
        sel_b = sb("sel_b", [E, E, P], BF16)
        gs = sb("gs", [P, 4, NT])
        best_T = p32[0:E, 0:T]
        best_b = p32[0:E, T:T + T // 2].bitcast(BF16)
        b2_sb = o_raw[0:E, :]
        b1_raw = o_norm[0:E * NC, 0:P]

        s_const = sem("s_const")
        s_x = sem("s_x")
        s_ctx = [sem(f"s_ctx{i}") for i in range(4)]
        s_wqk = [sem("s_wqk0"), sem("s_wqk1")]
        s_wv = [sem("s_wv0"), sem("s_wv1")]
        s_wo = [sem("s_wo0"), sem("s_wo1")]
        s_k2 = [sem("s_k2a"), sem("s_k2b")]
        s_ln = sem("s_ln")
        s_sd = sem("s_sd")
        s_xt = sem("s_xt")
        s_xc = sem("s_xc")
        s_tp = sem("s_tp")
        s_th = sem("s_th")
        s_tl = [sem("s_tl0"), sem("s_tl1")]
        s_wkh = sem("s_wkh")
        s_wkl = sem("s_wkl")
        s_wvh = sem("s_wvh")
        s_wvl = sem("s_wvl")
        s_q = sem("s_q")
        s_k = sem("s_k")
        s_v = sem("s_v")
        s_mx = sem("s_mx")
        s_mt = sem("s_mt")
        s_sc = sem("s_sc")
        s_pv = sem("s_pv")
        s_sum = sem("s_sum")
        s_qh = sem("s_qh")
        s_kh = sem("s_kh")
        s_vc = sem("s_vc")
        s_mr = sem("s_mr")
        s_exp = sem("s_exp")
        s_ql = sem("s_ql")
        s_kl = sem("s_kl")
        s_red = sem("s_red")
        s_mn = sem("s_mn")
        s_mz = sem("s_mz")
        s_or = sem("s_or")
        s_rs = sem("s_rs")
        s_on = sem("s_on")
        s_yx = sem("s_yx")
        s_ya = sem("s_ya")
        s_ps = sem("s_ps")
        s_aw = sem("s_aw")
        s_ew = sem("s_ew")
        s_eh = sem("s_eh")
        s_el = sem("s_el")
        s_xl = sem("s_xl")
        s_hh = sem("s_hh")
        s_hl = sem("s_hl")
        s_small = sem("s_small")
        s_out = sem("s_out")
        s_tc = sem("s_tc")
        s_vec = sem("s_vec")
        s_vone = sem("s_vone")
        s_at = sem("s_at")
        s_ac = sem("s_ac")
        s_y = sem("s_y")
        s_x1 = sem("s_x1")
        s_qk = sem("s_qk")
        s_sq = sem("s_sq")
        s_nm = sem("s_nm")
        s_qx = sem("s_qx")
        s_lx = sem("s_lx")
        s_sl = sem("s_sl")
        s_iq = sem("s_iq")
        s_pl = sem("s_pl")
        s_pq = sem("s_pq")
        s_pk = sem("s_pk")
        s_vp = sem("s_vp")
        s_vx = sem("s_vx")
        s_dd = sem("s_dd")
        s_rt = sem("s_rt")
        s_r2 = sem("s_r2")
        s_ra = sem("s_ra")
        s_lg = sem("s_lg")
        s_wt = sem("s_wt")
        s_o = sem("s_o")
        s_oe = sem("s_oe")
        s_ot = sem("s_ot")
        s_on2 = sem("s_on2")
        s_gl = sem("s_gl")
        s_g = sem("s_g")
        s_ge = sem("s_ge")
        s_bt = sem("s_bt")
        s_bc = sem("s_bc")
        s_h = sem("s_h")
        s_hg = sem("s_hg")
        s_hm = sem("s_hm")
        s_dv = sem("s_dv")

        def at_least(eng, semaphore, count):
            if not (isinstance(count, int) and count <= 0):
                eng.wait_ge(semaphore, count)

        def context_pair(u):
            j, b = divmod(u, 2)
            return b, j // 2, j % 2, slice(512 * j, 512 * (j + 1))

        def slot_of(hp, b, s):
            return hp * (B * SLOTS) + (b * SLOTS + s)

        def step_of(hp, b):
            return hp * B + b

        def load_count(n, par, each):
            return (n - par) * (each // 2) + each

        def summed(n, s):
            if s < 0:
                return summed(n - 1, s + SLOTS)
            return n * (SLOTS // 2 - 1) + max(s // 2, 1)

        def first_step(hp, b):
            return isinstance(hp, int) and hp == 0 and b == 0

        def prepares(hp, b):
            return not (isinstance(hp, int) and hp == HP - 1 and b == B - 1)

        def row_bank(i, b):
            return (4, 5, PM)[(8 * b + i) % 3]

        def attn_units():
            return [(((b * 4 + g) * 2 + kt) * 2 + jj, b * 4 + g, b, g, kt, jj) for b in range(B)
                    for g in range(4) for kt in range(2) for jj in range(2)]

        def tail_sp(sp):
            sp.dma_start(gw_sb[:, :, :], gw.rearrange("(c p) e -> p c e", p=P)).then_inc(s_small, 16)
            sp.dma_start(gb_sb[:, :], gb.rearrange("(a e) -> a e", a=1)).then_inc(s_small, 16)
            sp.wait_ge(s_v, (STEPS - 1) * KCH)
            for i, w in enumerate((aq, ak, av, ao)):
                sp.dma_start(a_raw[:, i, :, :], w.rearrange("(t p) n -> p t n", p=P)).then_inc(s_aw, 16)
            sp.wait_ge(s_sc, (STEPS - 1) * SLOTS)
            for raw, w in ((w2_raw, w2), (w1_raw, w1)):
                sp.dma_start(raw.rearrange("p (m n) -> p m n", n=F),
                             w.rearrange("e (c p) n -> p (e c) n", p=P)).then_inc(s_ew, 16)
            sp.wait_ge(s_yx, STEPS)
            sp.dma_start(b1_raw[:, :], b1.rearrange("e (i p) -> (e i) p", p=P)).then_inc(s_small, 16)
            sp.dma_start(b2_sb[:, :], b2).then_inc(s_small, 16)
            for b in range(B):
                sp.wait_ge(s_x1, B + 2 * (b + 1))
                sp.dma_start(out.rearrange("b (t p) c -> b p t c", p=P)[b, :, :, :],
                             x_sb[:, 2 * b:2 * b + 2, :]).then_inc(s_out, 16)
            sp.wait_ge(s_out, B * 16)

        def tail_constants(pool):
            for i, tile in enumerate((sel[:, :, :], sel_b[:, :, :], gather[:, :])):
                nc.gpsimd.memset(tile, 0.0).then_inc(s_tc, 1)
                pool.wait_ge(s_tc, i + 1)
            nc.gpsimd.memset(ones1[:, :], 1.0).then_inc(s_tc, 1)
            done = 4

            nc.gpsimd.memset(head_rows[:, :], 1.0).then_inc(s_tc, 1)
            for base, step, mult in ((0, -32, 1), (15, 32, -1)):
                done += 1
                pool.wait_ge(s_tc, done)
                nc.gpsimd.affine_select(out=head_rows[:, :], in_=head_rows[:, :],
                                        compare_op=ALU.is_ge, fill=0.0, base=base,
                                        pattern=[[step, 4]], channel_multiplier=mult) \
                    .then_inc(s_tc, 1)
            pool.wait_ge(s_tc, done + 1)
            for i, r in enumerate((16, 17)):
                nc.gpsimd.tensor_copy(sel[:, i, r:P:32], head_rows[:, :])
            nc.gpsimd.tensor_copy(gather[:, 112:128].rearrange("p (j r) -> p j r", r=4),
                                  head_rows[:, :].unsqueeze(2).to_broadcast([P, 4, 4]))
            nc.gpsimd.affine_select(out=sel_b[:, :, :], in_=sel_b[:, :, :], compare_op=ALU.not_equal,
                                    fill=1.0, base=0, pattern=[[-1, E], [0, P]],
                                    channel_multiplier=1).then_inc(s_tc, 1)
            pool.wait_ge(s_tc, done + 2)
            for e in range(E):
                i = nc.gpsimd.memset(rank[:, :, e], float(E - e))
            i.then_inc(s_tc, 1)

        def zero_rows(pool):
            pool.wait_ge(s_v, (STEPS - 1) * KCH)
            for w in range(2):
                for c in range(NC):
                    i = nc.gpsimd.memset(aqk_T[:, w, c, :, SD:32], 0.0)
            i.then_inc(s_vone, 1)

        def tail_pool(pool):
            pool.wait_ge(s_pv, STEPS * SLOTS)
            nc.gpsimd.memset(place, 0.0).then_inc(s_tc, 1)
            pool.wait_ge(s_tc, TC + 1)
            for product, parts in enumerate(((0, 0), (0, 1), (1, 0), (0, 2), (1, 1), (2, 0))):
                for w, part in enumerate(parts):
                    i = nc.gpsimd.tensor_copy(
                        place[:, w, part, :, :].rearrange("p g (j n) -> p g j n", j=4)
                        [:, :, :, 4 * product:4 * product + 4],
                        ident[:, 64 * w:64 * w + 64].rearrange("p (g j r) -> p g j r", g=4, j=4))
            i.then_inc(s_tc, 1)
            pool.wait_ge(s_sum, STEPS)
            for t in range(NT):
                nc.gpsimd.memset(vx[:, t, :, SD:SD + 1], 1.0)
                i = nc.gpsimd.memset(vx[:, t, :, SD + 1:32], 0.0)
            i.then_inc(s_vone, 1)
            for gg in range(8):
                pool.wait_ge(s_r2, gg + 1)
                if gg == 3:
                    pool.wait_ge(s_ra, 3)
                if gg >= 4:
                    pool.wait_ge(s_o, gg - 3)
                nc.gpsimd.tensor_tensor(
                    weight[:, gg % 4, :, :, :].rearrange("p k h q -> p (k h q)"),
                    root[:, gg % 2, :, :, :].rearrange("p k h q -> p (k h q)"),
                    ratio[RATIO[gg]].rearrange("p k h q -> p (k h q)"),
                    ALU.add).then_inc(s_ra, 1)
            for i in range(E * NC):
                pool.wait_ge(s_hh, i + 1)
                nc.gpsimd.tensor_tensor(hid_p[:, i % 4, 1, :], hid_m[:, i % 2, :],
                                        hid_p[:, i % 4, 0, :], ALU.subtract).then_inc(s_hl, 1)

        def turn_weights(pe, w):
            if w == 0:
                pe.wait_ge(s_aw, 4 * 16)
                pe.wait_ge(s_red, STEPS * NU)
            if w == 2:
                pe.wait_ge(s_xc, NC + 1)
            if w == 3:
                pe.wait_ge(s_ac, 1)
            for c in range(NC):
                for t in range(NC):
                    mm = pe.transpose(ps[:, TURN_BANK[w], (NC * c + t) * P:(NC * c + t + 1) * P],
                                      a_raw[:, w, t, c * P:(c + 1) * P], ident[:, :])
            mm.then_inc(s_at, 1)

        def take_turned(act, w):
            act.wait_ge(s_at, w + 1)
            if w < 2:
                if w == 0:
                    act.wait_ge(s_vone, 1)
                nc.scalar.activation(
                    aqk_T[:, w, :, :, 0:SD].rearrange("p c h d -> p (c h) d"),
                    ps[:, TURN_BANK[w], :].rearrange("p (h d) -> p h d", d=SD),
                    ACT.Copy, scale=(1.0, -2.0)[w]).then_inc(s_ac, 1)
            else:
                if w == 2:
                    act.wait_ge(s_v, STEPS * KCH)
                nc.scalar.activation(avo_T[:, w - 2, :, :].rearrange("p c n -> p (c n)"),
                                     ps[:, TURN_BANK[w], :], ACT.Copy).then_inc(s_ac, 1)

        def transposes_batch(pe, b):
            if b == 1:
                pe.wait_ge(s_ac, 4)
            pe.wait_ge(s_ln, (2 + b) * LN)
            for c in range(NC):
                for t in range(2):
                    mm = pe.transpose(ps[:, TURN_X[b], (2 * c + t) * P:(2 * c + t + 1) * P],
                                      xn[:, 2 * b + t, c * P:(c + 1) * P], ident[:, :])
            mm.then_inc(s_xt, 1)

        def take_batch(act, b):
            act.wait_ge(s_xt, NC + b + 1)
            nc.scalar.activation(xnT[:, :, b * TQ:(b + 1) * TQ],
                                 ps[:, TURN_X[b], :].rearrange("p (c t) -> p c t", c=NC), ACT.Copy) \
                .then_inc(s_xc, 1)

        def tail_pe(pe, last_output):
            def turn(b, bank):
                for c in range(NC):
                    for t in range(2):
                        mm = pe.transpose(ps[:, bank, (2 * c + t) * P:(2 * c + t + 1) * P],
                                          xn[:, 2 * b + t, c * P:(c + 1) * P], ident[:, :])
                mm.then_inc(s_xt, 1)

            def turn_output(b):
                pe.wait_ge(s_on2, b + 1)
                turn(b, OUT_BANKS[b][0])

            def project_output(b):
                pe.wait_ge(s_xc, NC + B + b + 1)
                for t in (2 * b, 2 * b + 1):
                    cols = slice(t % 2 * D, (t % 2 + 1) * D)
                    for c in range(NC):
                        mm = pe.matmul(ps[:, OUT_BANKS[b][1], cols], xnT[:, c, t * P:(t + 1) * P],
                                       avo_T[:, 1, c, :], start=(c == 0), stop=(c == NC - 1))
                mm.then_inc(s_y, 1)

            def turn_normalised(b):
                pe.wait_ge(s_ln, (4 + b) * LN)
                if b == 1:
                    pe.wait_ge(s_xl, 1)
                turn(b, XN_BANK)

            def logits(b):
                pe.wait_ge(s_xc, NC + 2 * B + b + 1)
                for t in (2 * b, 2 * b + 1):
                    for c in range(NC):
                        pe.matmul(ps[:, GATE_BANK, t * E:(t + 1) * E], xnT[:, c, t * P:(t + 1) * P],
                                  gw_sb[:, c, :], start=(c == 0), stop=False)
                    mm = pe.matmul(ps[:, GATE_BANK, t * E:(t + 1) * E], ones1[:, :], gb_sb[:, :],
                                   start=False, stop=True)
                mm.then_inc(s_gl, 1)

            def values(b):
                pe.wait_ge(s_xc, NC + b + 1)
                for t in (2 * b, 2 * b + 1):
                    for c in range(NC):
                        mm = pe.matmul(ps[:, t, 0:D], xnT[:, c, t * P:(t + 1) * P],
                                       avo_T[:, 0, c, :], start=(c == 0), stop=(c == NC - 1))
                    mm.then_inc(s_vp, 1)

            def qk(i, b):
                w, g = divmod(i, 4)
                n = 8 * b + i
                if n == 2:
                    pe.wait_ge(s_ya, STEPS)
                if n >= 3:
                    pe.wait_ge(s_lx, n - 2)
                for c in range(NC):
                    mm = pe.matmul(ps[:, row_bank(i, b), 0:TQ],
                                   aqk_T[:, w, c, 4 * g:4 * g + 4, :].rearrange("p h d -> p (h d)"),
                                   xnT[:, c, b * TQ:(b + 1) * TQ],
                                   start=(c == 0), stop=(c == NC - 1))
                mm.then_inc(s_qk, 1)

            def lengths(i, b):
                w = i // 4
                pe.wait_ge(s_sq, 8 * b + i + 1)
                pe.matmul(ps[:, row_bank(i, b), 0:TQ], sel[:, w, :], square[:, i % 2, 0:TQ],
                          start=False, stop=True, skip_group_check=True).then_inc(s_nm, 1)
                if (i, b) == (0, 1):
                    pe.wait_ge(s_iq, 1)
                pe.matmul(ps[:, 6, b * TQ:(b + 1) * TQ], gather[:, 112 - 16 * i:240 - 16 * i],
                          square[:, i % 2, 0:TQ], start=(i == 0), stop=(i == 7)).then_inc(s_sl, 1)

            def rows_step(i, b):
                if i < 8:
                    qk(i, b)
                if i >= 1:
                    lengths(i - 1, b)

            def place_rows(b):
                pe.wait_ge(s_iq, IQ * (b + 1))
                if b == 0:
                    pe.wait_ge(s_vx, 2)
                else:
                    pe.wait_ge(s_lx, 8 * (b + 1))
                for g in range(4):
                    for w in range(2):
                        if g >= 1:
                            pe.wait_ge((s_pq, s_pk)[w], 4 * b + g)
                        rows = slice(64 * w, 64 * w + 64)
                        for i in range(3):
                            mm = pe.matmul(ps[:, PLACE_BANKS[b][w], 0:TQ], place[rows, w, i, g, :],
                                           inv_p[rows, i, b * TQ:(b + 1) * TQ],
                                           start=(i == 0), stop=(i == 2))
                        mm.then_inc(s_pl, 1)

            pe.wait_ge(s_ac, 4)
            values(0)
            last_output()
            pe.wait_ge(s_tc, TC)
            for i in range(9):
                rows_step(i, 0)
            transposes_batch(pe, 1)
            pe.wait_ge(s_or, STEPS)
            values(1)
            for i in range(ROWS_AHEAD):
                rows_step(i, 1)
            pe.wait_ge(s_tc, TC + 2)
            place_rows(0)
            pe.wait_ge(s_vx, NT)

            def distances(m, b, g, kt, jj):
                if (g, kt, jj) == (0, 0, 0):
                    pe.wait_ge(s_pq, 4 * (b + 1))
                    pe.wait_ge(s_pk, 4 * (b + 1))
                if m >= 2:
                    pe.wait_ge(s_rt, 2 * (m - 1))
                keys = slice((2 * b + kt) * P, (2 * b + kt + 1) * P)
                queries = slice(b * TQ, (b + 1) * TQ)
                for j in (2 * jj, 2 * jj + 1):
                    rows = slice(32 * j, 32 * j + 32)
                    for i, (k_part, q_part) in enumerate(((0, 0), (0, 1), (1, 0))):
                        pe.matmul(ps[:, j, 0:TQ], qkx[rows, 1, k_part, g, keys],
                                  qkx[rows, 0, q_part, g, queries], start=(i == 0), stop=(i == 2))
                    mm = pe.matmul(ps[:, j, TQ:2 * TQ], rk[rows, g, keys], rq[rows, g, queries],
                                   start=True, stop=True)
                mm.then_inc(s_dd, 1)

            def average(gg, b, g):
                pe.wait_ge(s_wt, gg + 1)
                if gg >= 2:
                    pe.wait_ge(s_oe, gg - 1)
                for kt in range(2):
                    for j in range(4):
                        mm = pe.matmul(ps[32 * j:32 * j + 32, 4 + gg % 2, 0:TQ],
                                       vx[:, 2 * b + kt, 4 * g + j, :], weight[:, g, kt, j, :],
                                       start=(kt == 0), stop=(kt == 1))
                mm.then_inc(s_o, 1)

            def turn_average(gg, b, g):
                pe.wait_ge(s_oe, gg + 1)
                if gg == 4:
                    pe.wait_ge(s_x1, 1)
                for t in range(2):
                    mm = pe.transpose(ps[:, 6 + t, g * P:(g + 1) * P], o_T[:, gg % 2, t * P:(t + 1) * P],
                                      ident[:, :])
                mm.then_inc(s_ot, 1)

            for m, gg, b, g, kt, jj in attn_units():
                if m == 16:
                    place_rows(1)
                distances(m, b, g, kt, jj)
                if ROWS_AHEAD + m < 9:
                    rows_step(ROWS_AHEAD + m, 1)
                if m in AVERAGE_AT:
                    average(AVERAGE_AT.index(m), 0, AVERAGE_AT.index(m))
            turn_average(0, 0, 0)
            for g in range(2, 4):
                average(g, 0, g)
                turn_average(g - 1, 0, g - 1)
            turn_average(3, 0, 3)
            turn_output(0)
            project_output(0)
            pe.wait_ge(s_rt, 2 * 32)
            for g in range(4):
                average(4 + g, 1, g)
                if g >= 1:
                    turn_average(3 + g, 1, g - 1)
            turn_average(7, 1, 3)
            turn_output(1)
            turn_normalised(0)
            project_output(1)
            pe.wait_ge(s_small, 64)
            pe.transpose(ps[:, 7, 0:E * NC], b1_raw[:, :], ident[0:E * NC, 0:E * NC]).then_inc(s_bt, 1)
            logits(0)
            turn_normalised(1)
            logits(1)

            def hidden(i):
                e, it = divmod(i, NC)
                if i >= 2:
                    pe.wait_ge(s_hg, i - 1)
                k = 0
                for c in range(NC):
                    for w_part, x_part in ((0, 0), (0, 1), (1, 0)):
                        mm = pe.matmul(ps[:, 4 + i % 2, :],
                                       w1_p[:, w_part, e, c, it * P:(it + 1) * P],
                                       xnT_p[:, x_part, c, :], start=(k == 0), stop=(k == 5))
                        k += 1
                mm.then_inc(s_h, 1)

            def mask(e):
                if e >= 2:
                    pe.wait_ge(s_hm, NC * (e - 1))
                pe.matmul(ps[:, 6 + e % 2, :], sel_b[:, e, :], best_b[:, :],
                          start=True, stop=True).then_inc(s_bt, 1)

            def outer(i):
                e, it = divmod(i, NC)
                pe.wait_ge(s_hl, i + 1)
                for t in range(NT):
                    for h_part, w_part in ((0, 0), (0, 1), (1, 0)):
                        mm = pe.matmul(ps[:, t, 0:D], hid_p[:, i % 4, h_part, t * P:(t + 1) * P],
                                       w2_p[:, w_part, e, it, :], start=False,
                                       stop=(i == E * NC - 1 and h_part == 1))
                    if i == E * NC - 1 or t == NT - 1:
                        mm.then_inc(s_y, 1)

            pe.wait_ge(s_el, 8)
            pe.wait_ge(s_xl, B)
            hidden(0)
            hidden(1)
            pe.wait_ge(s_bc, 1)
            pe.wait_ge(s_g, 10)
            for t in range(NT):
                mm = pe.transpose(ps[0:E, 7, t * P:(t + 1) * P], best[:, t, :], ident[:, :])
            mm.then_inc(s_bt, 1)
            pe.wait_ge(s_bc, 3)
            mask(0)
            mask(1)
            for t in range(NT):
                pe.matmul(ps[:, t, 0:D], best_T[:, t * P:(t + 1) * P], b2_sb[:, :],
                          start=True, stop=False)
            for i in range(2, E * NC + 2):
                if i < E * NC:
                    hidden(i)
                    if i % NC == 0 and i >= 2 * NC:
                        mask(i // NC)
                outer(i - 2)

        def root_of_variance(act, i, tiles):
            act.wait_ge(s_ln, LN * i + 3)
            nc.scalar.activation(rstd[:, tiles], var[:, tiles], ACT.Sqrt).then_inc(s_sd, 1)

        def expert_quarter(k):
            raw, parts = ((w2_raw, w2_p), (w1_raw, w1_p))[k // 4]
            experts = slice(k % 4 * (E // 4), (k % 4 + 1) * (E // 4))
            return [raw[:, k % 4 * 1024:(k % 4 + 1) * 1024]] + \
                [parts[:, i, experts, :, :].rearrange("p e c n -> p (e c n)") for i in range(2)]

        def split_experts_high(act, k):
            if k == 0:
                act.wait_ge(s_ew, 32)
                act.wait_ge(s_v, (STEPS - 1) * KCH)
            if k == 4:
                act.wait_ge(s_v, STEPS * KCH)
            raw, high, _ = expert_quarter(k)
            nc.scalar.activation(high, raw, ACT.Copy, scale=ES).then_inc(s_eh, 1)

        def split_experts_low(dve, k):
            dve.wait_ge(s_eh, k + 1)
            raw, high, low = expert_quarter(k)
            nc.vector.scalar_tensor_tensor(low, raw, ES, high, ALU.mult, ALU.subtract) \
                .then_inc(s_el, 1)

        def tail_act(act):
            def take_values(b):
                act.wait_ge(s_vp, 2 * b + 2)
                for t in (2 * b, 2 * b + 1):
                    nc.scalar.activation(vx[:, t, :, 0:SD],
                                         ps[:, t, 0:D].rearrange("p (h d) -> p h d", d=SD),
                                         ACT.Copy).then_inc(s_vx, 1)

            def squares(i, b):
                act.wait_ge(s_qk, 8 * b + i + 1)
                if 8 * b + i >= 2:
                    act.wait_ge(s_sl, 8 * b + i - 1)
                nc.scalar.activation(square[:, i % 2, 0:TQ], ps[:, row_bank(i, b), 0:TQ], ACT.Square,
                                     scale=(1.0, 0.5)[i // 4]) \
                    .then_inc(s_sq, 1)

            def rows(i, b):
                w, g = divmod(i, 4)
                tokens = slice(b * TQ, (b + 1) * TQ)
                act.wait_ge(s_nm, 8 * b + i + 1)
                nc.scalar.activation(qkx[:, w, 0, g, tokens], ps[:, row_bank(i, b), 0:TQ], ACT.Identity,
                                     bias=vecs[:, 1 - w:2 - w]).then_inc(s_qx, 1)

            def rows_step(i, b):
                if i < 8:
                    squares(i, b)
                if i >= 1:
                    rows(i - 1, b)

            def take_placed(b, g):
                act.wait_ge(s_pl, 8 * b + 2 * g + 1)
                nc.scalar.activation(rq[:, g, b * TQ:(b + 1) * TQ], ps[:, PLACE_BANKS[b][0], 0:TQ],
                                     ACT.Copy).then_inc(s_pq, 1)

            act.wait_ge(s_vone, 2)
            take_values(0)
            for i in range(9):
                rows_step(i, 0)
                if i == 3:
                    root_of_variance(act, 2, slice(2, NT))
            take_batch(act, 1)
            take_values(1)
            for i in range(ROWS_AHEAD):
                rows_step(i, 1)
            for g in range(4):
                take_placed(0, g)

            def flat(v):
                return v.rearrange("p k h q -> p (k h q)")

            def roots(gg):
                act.wait_ge(s_rt, 8 * (gg + 1))
                if gg >= 2:
                    act.wait_ge(s_ra, gg - 1)
                nc.scalar.activation(flat(root[:, gg % 2, :, :, :]), flat(ratio[RATIO[gg]]),
                                     ACT.Sqrt, scale=2.0)
                nc.scalar.activation(flat(ratio[RATIO[gg]]), flat(ratio[RATIO[gg]]),
                                     ACT.Sqrt, scale=2.0, bias=vecs[:, 2:3]).then_inc(s_r2, 1)

            def logarithms(gg, g):
                act.wait_ge(s_ra, gg + 1)
                nc.scalar.activation(flat(weight[:, g, :, :, :]), flat(weight[:, g, :, :, :]),
                                     ACT.Ln).then_inc(s_lg, 1)

            def weights(gg, g):
                act.wait_ge(s_lg, gg + 1)
                nc.scalar.activation(flat(weight[:, g, :, :, :]), flat(weight[:, g, :, :, :]),
                                     ACT.Exp, scale=-2.0).then_inc(s_wt, 1)

            def take_turned_xn(n, b, bank):
                act.wait_ge(s_xt, NC + B + n)
                nc.scalar.activation(xnT[:, :, b * TQ:(b + 1) * TQ],
                                     ps[:, bank, :].rearrange("p (c t) -> p c t", c=NC), ACT.Copy) \
                    .then_inc(s_xc, 1)

            def take_normalised(b):
                act.wait_ge(s_xt, NC + 2 * B + b + 1)
                nc.scalar.activation(xnT_p[:, 0, :, b * TQ:(b + 1) * TQ],
                                     ps[:, XN_BANK, :].rearrange("p (c t) -> p c t", c=NC), ACT.Copy)
                take_turned_xn(B + b + 1, b, XN_BANK)

            for b in range(B):
                for g in range(4):
                    if (b, g) == (0, 0):
                        for i in range(ROWS_AHEAD, 9):
                            rows_step(i, 1)
                    roots(4 * b + g)
                for g in range(4):
                    logarithms(4 * b + g, g)
                    if b == 0:
                        take_placed(1, g)
                    if (b, g) == (1, 2):
                        take_turned_xn(1, 0, OUT_BANKS[0][0])
                for g in range(4):
                    weights(4 * b + g, g)
            root_of_variance(act, 3, slice(0, 2))
            take_turned_xn(2, 1, OUT_BANKS[1][0])
            take_normalised(0)
            root_of_variance(act, 4, slice(2, NT))

            act.wait_ge(s_bt, 1)
            nc.scalar.activation(b1_T[:, :], ps[:, 7, 0:E * NC], ACT.Copy).then_inc(s_bc, 1)
            take_normalised(1)
            act.wait_ge(s_g, 2)
            nc.scalar.activation(ge[:, :, :], lg[:, :, :], ACT.Exp).then_inc(s_ge, 1)
            for i in range(E * NC + 1):
                if i < E * NC:
                    act.wait_ge(s_h, i + 1)
                    if i >= 2:
                        act.wait_ge(s_hm, i - 1)
                    nc.scalar.activation(hid[:, i % 2, :], ps[:, 4 + i % 2, :], ACT.Gelu,
                                         bias=b1_T[:, i:i + 1], scale=1.0 / ES).then_inc(s_hg, 1)
                if i == 1:
                    act.wait_ge(s_bt, 2)
                    nc.scalar.activation(best_T[:, :], ps[0:E, 7, :], ACT.Copy, scale=ES) \
                        .then_inc(s_bc, 1)
                    nc.scalar.activation(best_b[:, :], ps[0:E, 7, :], ACT.Copy).then_inc(s_bc, 1)
                if i >= 1:
                    act.wait_ge(s_hm, i)
                    if i >= 5:
                        act.wait_ge(s_y, B + i - 4)
                    nc.scalar.activation(hid_p[:, (i - 1) % 4, 0, :], hid_m[:, (i - 1) % 2, :],
                                         ACT.Copy).then_inc(s_hh, 1)

        def row_vectors(dve):
            done = [0]

            def link(i):
                done[0] += 1
                i.then_inc(s_dv, 1)
                dve.wait_ge(s_dv, done[0])

            def ones_at(out, columns):
                return nc.vector.tensor_reduce(out, columns, AX.XY if len(columns.shape) > 2 else AX.X,
                                               ALU.add)

            for i, r in enumerate((16, 17)):
                ones_at(vecs[:, i:i + 1], ident[:, r:P:32])
            nc.vector.memset(vecs[:, 2:3], 2.0)
            for r in range(4):
                ones_at(rvec[:, r:r + 1], ident[:, r:P:4])
            ones_at(rvec[:, 4:5], ident[:, 0:64])
            link(ones_at(rvec[:, 5:6], ident[:, 64:P]))
            r0, r1, r2, r3, rq_, rk_ = (rvec[:, i:i + 1] for i in range(6))
            sign, value, first, temp = (rvec[:, i:i + 1] for i in range(6, 10))
            nc.vector.tensor_tensor(first, r0, r1, ALU.add)
            link(nc.vector.tensor_tensor(temp, r2, r3, ALU.add))
            nc.vector.tensor_scalar(value, rk_, 1e6, rq_, ALU.mult, ALU.add).then_inc(s_vec, 1)
            dve.wait_ge(s_vec, 1)
            link(nc.vector.tensor_tensor(value, value, temp, ALU.mult))
            link(nc.vector.tensor_tensor(temp, r2, r3, ALU.subtract))
            link(nc.vector.tensor_tensor(sign, rk_, rq_, ALU.subtract))
            link(nc.vector.tensor_tensor(temp, temp, sign, ALU.mult))
            link(nc.vector.tensor_tensor(sign, r0, r1, ALU.subtract))
            nc.vector.tensor_tensor(sign, sign, temp, ALU.add).then_inc(s_vec, 1)
            assert done[0] == DV

        def tail_dve(dve, variance, normalised):
            def residual(b):
                dve.wait_ge(s_y, b + 1)
                rows = x_sb[:, 2 * b:2 * b + 2, :].rearrange("p t c -> p (t c)")
                nc.vector.tensor_tensor(rows, rows, ps[:, OUT_BANKS[b][1], :], ALU.add) \
                    .then_inc(s_x1, 1)
                dve.wait_ge(s_x1, b + 1)

            def low_xnT(b):
                dve.wait_ge(s_xc, NC + 2 * B + b + 1)
                cols = slice(b * TQ, (b + 1) * TQ)
                nc.vector.tensor_tensor(xnT_p[:, 1, :, cols],
                                        ps[:, XN_BANK, :].rearrange("p (c t) -> p c t", c=NC),
                                        xnT_p[:, 0, :, cols], ALU.subtract).then_inc(s_xl, 1)

            def low_rows(i, b):
                w, g = divmod(i, 4)
                tokens = slice(b * TQ, (b + 1) * TQ)
                dve.wait_ge(s_qx, 8 * b + i + 1)
                nc.vector.scalar_tensor_tensor(
                    qkx[:, w, 1, g, tokens], ps[:, row_bank(i, b), 0:TQ], vecs[:, 1 - w:2 - w],
                    qkx[:, w, 0, g, tokens], ALU.add, ALU.subtract).then_inc(s_lx, 1)

            for i in range(3):
                low_rows(i, 0)
            variance(2, slice(2, NT))
            normalised(2, slice(2, NT))
            for i in range(3, 8):
                low_rows(i, 0)

            def inverses(b, k):
                cols = slice(b * TQ, (b + 1) * TQ)
                v, t, tt, ts = inv[:, cols], inv_t[:, cols], nc.vector.tensor_tensor, \
                    nc.vector.tensor_scalar
                if k == 0:
                    dve.wait_ge(s_sl, 8 * (b + 1))
                    i = ts(v, ps[:, 6, cols], -1.0, 1.0, ALU.mult, ALU.add)
                elif k == 1:
                    i = ts(t, v, 0.0, 1e-18, ALU.is_equal, ALU.mult)
                elif k == 2:
                    i = tt(v, v, t, ALU.add)
                elif k == 3:
                    i = nc.vector.reciprocal(v, v)
                elif k == 4:
                    i = ts(v, v, rvec[:, 6:7], 0.0, ALU.mult, ALU.max)
                elif k == 5:
                    i = ts(t, v, 0.0, rvec[:, 7:8], ALU.is_gt, ALU.mult)
                elif k == 6:
                    i = nc.vector.scalar_tensor_tensor(v, v, rvec[:, 8:9], t, ALU.mult, ALU.add)
                elif k % 2 == 1:
                    i = nc.vector.tensor_copy(inv_p[:, (k - 7) // 2, cols], v)
                else:
                    i = tt(v, v, inv_p[:, (k - 8) // 2, cols], ALU.subtract)
                i.then_inc(s_iq, 1)
                dve.wait_ge(s_iq, IQ * b + k + 1)

            def take_placed(b):
                for g in range(4):
                    dve.wait_ge(s_pl, 8 * b + 2 * g + 2)
                    nc.vector.tensor_copy(rk[:, g, b * TQ:(b + 1) * TQ], ps[:, PLACE_BANKS[b][1], 0:TQ]) \
                        .then_inc(s_pk, 1)

            for k in range(IQ):
                inverses(0, k)
            for i in range(ROWS_AHEAD - 1):
                low_rows(i, 1)
            take_placed(0)

            def ratios(m, gg, kt, jj):
                dve.wait_ge(s_dd, m + 1)
                if kt == 0 and jj == 0 and RATIO[gg] in RATIO[:gg]:
                    dve.wait_ge(s_ra, max(i for i in range(gg) if RATIO[i] == RATIO[gg]) + 1)
                heads = slice(2 * jj, 2 * jj + 2)
                part = ratio[RATIO[gg]][:, kt, heads, :]
                nc.vector.tensor_scalar(part, ps[:, heads, 0:TQ], 0.0, None, ALU.max) \
                    .then_inc(s_rt, 1)
                dve.wait_ge(s_rt, 2 * m + 1)
                nc.vector.scalar_tensor_tensor(part, ps[:, heads, TQ:2 * TQ], 1e6, part,
                                               ALU.min, ALU.mult).then_inc(s_rt, 1)

            def take_average(gg):
                dve.wait_ge(s_o, gg + 1)
                if gg >= 2:
                    dve.wait_ge(s_ot, gg - 1)
                nc.vector.tensor_copy(o_T[:, gg % 2, :], ps[:, 4 + gg % 2, 0:TQ]).then_inc(s_oe, 1)

            def normalise(b):
                dve.wait_ge(s_ot, 4 * (b + 1))
                o = ps[:, 6:8, :].rearrange("p t (h d) -> p t h d", h=SH)
                for t in range(2):
                    i = nc.vector.reciprocal(orec[:, b, t, :], o[:, t, :, SD])
                i.then_inc(s_dv, 1)
                dve.wait_ge(s_dv, DV + b + 1)
                for t in range(2):
                    i = nc.vector.tensor_tensor(
                        xn[:, 2 * b + t, :].rearrange("p (h d) -> p h d", h=SH), o[:, t, :, 0:SD],
                        orec[:, b, t, :].unsqueeze(2).to_broadcast([P, SH, SD]), ALU.mult)
                i.then_inc(s_on2, 1)

            for m, gg, b, g, kt, jj in attn_units():
                ratios(m, gg, kt, jj)
                if ROWS_AHEAD + m < 9:
                    low_rows(ROWS_AHEAD + m - 1, 1)
                k = m - 9 + ROWS_AHEAD
                if 0 <= k <= 15 - 9 + ROWS_AHEAD:
                    inverses(1, k)
                if m == 15:
                    for k in range(15 - 9 + ROWS_AHEAD + 1, IQ):
                        inverses(1, k)
                    take_placed(1)
                if m in AVERAGE_AT:
                    take_average(AVERAGE_AT.index(m))
            take_average(2)
            take_average(3)
            normalise(0)
            residual(0)
            variance(3, slice(0, 2))
            for gg in range(4, 8):
                take_average(gg)
            normalise(1)
            normalised(3, slice(0, 2))
            residual(1)
            variance(4, slice(2, NT))
            normalised(4, slice(2, NT))
            low_xnT(0)
            low_xnT(1)

            def per_token(v):
                return v.unsqueeze(2).to_broadcast([P, NT, E])

            dve.wait_ge(s_gl, B)
            logits = ps[:, GATE_BANK, 0:NT * E].rearrange("p (t e) -> p t e", e=E)
            nc.vector.tensor_reduce(gs[:, 0, :], logits, AX.X, ALU.max).then_inc(s_g, 1)
            dve.wait_ge(s_g, 1)
            nc.vector.tensor_tensor(lg[:, :, :], logits, per_token(gs[:, 0, :]), ALU.subtract) \
                .then_inc(s_g, 1)
            dve.wait_ge(s_ge, 1)
            nc.vector.tensor_reduce(gs[:, 1, :], ge[:, :, :], AX.X, ALU.add).then_inc(s_g, 1)
            dve.wait_ge(s_g, 3)
            nc.vector.reciprocal(gs[:, 1, :], gs[:, 1, :]).then_inc(s_g, 1)
            dve.wait_ge(s_g, 4)
            nc.vector.tensor_tensor(lg[:, :, :], ge[:, :, :], per_token(gs[:, 1, :]), ALU.mult) \
                .then_inc(s_g, 1)
            dve.wait_ge(s_g, 5)
            nc.vector.tensor_reduce(gs[:, 2, :], lg[:, :, :], AX.X, ALU.max).then_inc(s_g, 1)
            dve.wait_ge(s_g, 6)
            nc.vector.tensor_tensor(best[:, :, :], lg[:, :, :], per_token(gs[:, 2, :]), ALU.is_equal) \
                .then_inc(s_g, 1)
            dve.wait_ge(s_g, 7)
            dve.wait_ge(s_tc, TC)
            nc.vector.tensor_tensor(best[:, :, :], best[:, :, :], rank[:, :, :], ALU.mult) \
                .then_inc(s_g, 1)
            dve.wait_ge(s_g, 8)
            nc.vector.tensor_reduce(gs[:, 3, :], best[:, :, :], AX.X, ALU.max).then_inc(s_g, 1)
            dve.wait_ge(s_g, 9)
            nc.vector.tensor_tensor(best[:, :, :], best[:, :, :], per_token(gs[:, 3, :]),
                                    ALU.is_equal).then_inc(s_g, 1)
            for i in range(E * NC):
                e, it = divmod(i, NC)
                dve.wait_ge(s_hg, i + 1)
                dve.wait_ge(s_bt, 3 + e)
                if i >= 2:
                    dve.wait_ge(s_hl, i - 1)
                nc.vector.tensor_tensor(hid_m[:, i % 2, :], hid[:, i % 2, :], ps[:, 6 + e % 2, :],
                                        ALU.mult).then_inc(s_hm, 1)
            for t in range(NT):
                dve.wait_ge(s_y, B + E * NC + t)
                nc.vector.scalar_tensor_tensor(x_sb[:, t, :], ps[:, t, 0:D], 1.0 / ES, x_sb[:, t, :],
                                               ALU.mult, ALU.add).then_inc(s_x1, 1)

        block = stack.enter_context(nc.Block())

        @block.sync
        def _(sp):
            wqk_cols = [w.rearrange("(c p) n -> p c n", p=P) for w in (wq, wk)]
            wv_cols = wv.rearrange("(c p) n -> p c n", p=P)

            def load_wqk(par, hp):
                for i, w in enumerate(wqk_cols):
                    sp.dma_start(wqk_raw[:, par, i, :, :], w[:, :, bass.ds(hp * P, P)]) \
                        .then_inc(s_wqk[par], 16)

            def load_wv(par, hp):
                sp.dma_start(wv_raw[:, par, :, :], wv_cols[:, :, bass.ds(hp * P, P)]) \
                    .then_inc(s_wv[par], 16)

            def load_wo(par, hp):
                sp.dma_start(wo_raw[:, par, :], wo[bass.ds(hp * P, P), :]).then_inc(s_wo[par], 16)

            def copy_k2(n, par):
                for half in range(2):
                    sp.wait_ge(s_kh, n * (2 * KCH) + KCH * (half + 1))
                    keys = slice(half * (TK // 2), (half + 1) * (TK // 2))
                    for h in range(2):
                        rows = slice(64 * h, 64 * h + 64)
                        sp.dma_start(k2[rows, par, h, keys], k1[rows, par, h, keys]) \
                            .then_inc(s_k2[half], 16)

            sp.dma_start(x_sb[:, :, :], x.rearrange("b (t p) c -> p (b t) c", p=P)).then_inc(s_x, 16)
            chunks = ctx.rearrange("b (n p t) c -> b n p t c", p=P, t=8)
            for n in range(4):
                for b in range(B):
                    if n >= 2:
                        sp.wait_ge(s_tp, 2 * (2 * (2 * n - 3) + b) + 2)
                    sp.dma_start(stage[b][:, n % 2, :, :], chunks[b, n, :, :, :]) \
                        .then_inc(s_ctx[2 * b + n % 2], 16)
                    if (n, b) == (0, 0):
                        load_wqk(0, 0)
                if n == 1:
                    load_wv(0, 0)
                    load_wqk(1, 0)
            copy_k2(0, 0)

            def step(hp, b):
                n = step_of(hp, b)
                last_pair = isinstance(hp, int) and hp == HP - 1
                if not last_pair:
                    sp.wait_ge(s_q, n + 1)
                    sp.wait_ge(s_wkl, n + 1)
                    load_wqk(b, hp + 1)
                if prepares(hp, b):
                    at_least(sp, s_wvl, n)
                    load_wv(1 - b, hp + b)
                at_least(sp, s_yx, n - 1)
                load_wo(b, hp)
                if prepares(hp, b):
                    copy_k2(n + 1, 1 - b)

            step(0, 0)
            step(0, 1)
            with sp.Fori(1, HP - 1) as hp:
                step(hp, 0)
                step(hp, 1)
            step(HP - 1, 0)
            step(HP - 1, 1)
            tail_sp(sp)

        @block.tensor
        def _(pe):
            def transposes_x():
                pe.wait_ge(s_ln, LN)
                for c in range(NC):
                    for t in range(NT):
                        mm = pe.transpose(ps[:, MX + c, t * P:(t + 1) * P],
                                          xn[:, t, c * P:(c + 1) * P], ident[:, :])
                    mm.then_inc(s_xt, 1)

            def transposes_ctx(u):
                b, n, half, _ = context_pair(u)
                pe.wait_ge(s_ctx[2 * b + n % 2], 16 * (n // 2 + 1))
                for c in range(NC):
                    if u >= 1:
                        pe.wait_ge((s_tl[0], s_th)[c], (1, 2)[c] * u)
                    for t in range(4):
                        mm = pe.transpose(ps[:, TURNED[c], t * P:(t + 1) * P],
                                          stage[b][:, n % 2, 4 * half + t, c * P:(c + 1) * P],
                                          ident[:, :])
                    mm.then_inc(s_tp, 1)

            def project_q(n, par):
                at_least(pe, s_mr, n)
                pe.wait_ge(s_wqk[par], load_count(n, par, 32))
                for c in range(NC):
                    mm = pe.matmul(ps[:, PM, 0:TQ], wqk_raw[:, par, 0, c, :],
                                   xnT[:, c, par * TQ:(par + 1) * TQ],
                                   start=(c == 0), stop=(c == NC - 1))
                mm.then_inc(s_q, 1)

            def project_k(j, n, par):
                at_least(pe, s_kl, n * KCH + j)
                if j == 0:
                    pe.wait_ge(s_wkl, n + 1)
                keys = slice(512 * j, 512 * (j + 1))
                k = 0
                for c in range(NC):
                    for w, y in ((wk_hi, ctx_hi), (wk_hi, ctx_lo), (wk_lo, ctx_hi)):
                        mm = pe.matmul(ps[:, PK, :], w[:, par, c, :], y[:, par, c, keys],
                                       start=(k == 0), stop=(k == 5))
                        k += 1
                mm.then_inc(s_k, 1)

            def project_v(j, n, par):
                at_least(pe, s_vc, n * KCH + j)
                if j == 0:
                    pe.wait_ge(s_wvl, n + 1)
                for t in range(CS):
                    toks = slice((CS * j + t) * P, (CS * j + t + 1) * P)
                    k = 0
                    for c in range(NC):
                        for y, w in ((ctx_hi, wv_hi), (ctx_hi, wv_lo), (ctx_lo, wv_hi)):
                            mm = pe.matmul(ps[:, PV, t * P:(t + 1) * P], y[:, par, c, toks],
                                           w[:, par, c, :], start=(k == 0), stop=(k == 5))
                            k += 1
                mm.then_inc(s_v, 1)

            def maxima(u, n, par):
                j, t = divmod(u, 2)
                bank = MX
                if isinstance(n, int) and n == 0:
                    bank = (MX, SC)[u % 2]
                    at_least(pe, s_red, u - 1)
                else:
                    pe.wait_ge(s_red, n * NU + u)
                pe.wait_ge(s_kh, n * (2 * KCH) + 2 * (j + 1))
                if u == 0:
                    pe.wait_ge(s_qh, n + 1)
                for h in range(2):
                    rows = slice(64 * h, 64 * h + 64)
                    mm = pe.matmul(ps[:, bank + 1 - h, :], q1[rows, par, h, t * P:(t + 1) * P],
                                   k1[rows, par, h, 512 * j:512 * (j + 1)], start=True, stop=True)
                mm.then_inc(s_mx, 1)

            def max_rows(n, earlier):
                pe.wait_ge(s_ql, n + 1)
                at_least(pe, s_ya, n - 1 if earlier else 0)
                pe.wait_ge(s_mn, n + 1)
                for t in range(2):
                    mm = pe.transpose(ps[:, PM, t * P:(t + 1) * P], m_neg[:, t, :], ident[:, :])
                mm.then_inc(s_mt, 1)

            def sums(n, par, q_step):
                if q_step is not None:
                    pe.wait_ge(s_ql, q_step + 1)
                pe.wait_ge(s_ps, summed(n, SLOTS - 1))
                for k in range(2):
                    for h in range(2):
                        mm = pe.matmul(ps[64 * h:64 * h + 64, PM, 0:TQ], sixteen[:, :],
                                       psums[:, par, k, h, :], start=(k == 0), stop=(k == 1))
                mm.then_inc(s_sum, 1)

            def project_o(n, par):
                pe.wait_ge(s_on, n + 1)
                pe.wait_ge(s_wo[par], load_count(n, par, 16))
                for t in range(2):
                    mm = pe.matmul(ps[:, PM, t * TQ:(t + 1) * TQ], o_norm[:, t * P:(t + 1) * P],
                                   wo_raw[:, par, :], start=True, stop=True)
                mm.then_inc(s_yx, 1)

            def scores(g, s, n, par):
                at_least(pe, s_exp, g - 1)
                if s == 0:
                    pe.wait_ge(s_mr, n + 1)
                    pe.wait_ge(s_kl, n * KCH + KCH)
                if s % (SLOTS // 2) == 0:
                    pe.wait_ge(s_k2[2 * s // SLOTS], (n + 1) * 32)
                keys = slice(s * P, (s + 1) * P)
                for h in range(2):
                    cols = slice(h * TQ, (h + 1) * TQ)
                    pe.matmul(ps[:, SC + s % 2, cols], k1[:, par, h, keys], q1[:, par, h, :],
                              start=True, stop=False)
                    mm = pe.matmul(ps[:, SC + s % 2, cols], k2[:, par, h, keys], q2[:, par, h, :],
                                   start=False, stop=True)
                mm.then_inc(s_sc, 1)

            def pv(g, s, n):
                pe.wait_ge(s_exp, g + 1)
                if s == 0:
                    at_least(pe, s_or, n)
                if s % CS == 0:
                    pe.wait_ge(s_vc, n * KCH + s // CS + 1)
                for h in range(2):
                    mm = pe.matmul(ps[64 * h:64 * h + 64, ACC, 0:TQ],
                                   v_sb[:, s // CS % NV, s % CS, 64 * h:64 * h + 64],
                                   probs[:, s % NP, h, :], start=(s == 0), stop=(s == SLOTS - 1))
                mm.then_inc(s_pv, 1)

            def step(hp, b):
                n, more, first = step_of(hp, b), prepares(hp, b), first_step(hp, b)
                for s in range(SLOTS):
                    scores(slot_of(hp, b, s), s, n, b)
                    if s in MAX_AT and more:
                        maxima(MAX_AT[s], n + 1, 1 - b)
                    if s == M_AT and more:
                        max_rows(n + 1, not first)
                    if s >= 1:
                        pv(slot_of(hp, b, s - 1), s - 1, n)
                    elif not first:
                        pv(slot_of(hp, b, s - 1), SLOTS - 1, n - 1)
                    if s == Q_AT and more:
                        project_q(n + 1, 1 - b)
                    if s in K_AT and more:
                        project_k(K_AT[s], n + 1, 1 - b)
                    if s in V_AT and V_AT[s]:
                        project_v(V_AT[s], n, b)
                    elif s in V_AT and more:
                        project_v(0, n + 1, 1 - b)
                    if s == SUM_AT and not first:
                        sums(n - 1, 1 - b, n + 1 if more else None)
                    if s == Y_AT and not first:
                        project_o(n - 1, 1 - b)
                    if s == XT_AT and not more:
                        transposes_batch(pe, 0)
                    if s in TURN_AT and not more:
                        turn_weights(pe, TURN_AT[s])

            pe.wait_ge(s_const, 3)
            for j in range(KCH + 2):
                if j < KCH:
                    transposes_ctx(2 * j)
                if j == 0:
                    transposes_x()
                    pe.wait_ge(s_xc, NC)
                    project_q(0, 0)
                if j == KCH:
                    pe.wait_ge(s_th, 4 * KCH)
                    project_v(0, 0, 0)
                if 1 <= j <= KCH:
                    for c in range(NC):
                        pe.wait_ge(s_tl[c], 2 * (j - 1) + 1)
                    project_k(j - 1, 0, 0)
                if j >= 2:
                    maxima(2 * (j - 2), 0, 0)
                if j < KCH:
                    transposes_ctx(2 * j + 1)
                if j >= 2:
                    maxima(2 * (j - 2) + 1, 0, 0)
            max_rows(0, False)
            pe.wait_ge(s_const, 5)
            for c in range(NC):
                pe.wait_ge(s_tl[c], 2 * KCH)
            pe.wait_ge(s_red, NU)
            step(0, 0)
            step(0, 1)
            with pe.Fori(1, HP - 1) as hp:
                step(hp, 0)
                step(hp, 1)
            step(HP - 1, 0)
            step(HP - 1, 1)
            pv(STEPS * SLOTS - 1, SLOTS - 1, STEPS - 1)
            pe.wait_ge(s_ya, STEPS - 1)
            sums(STEPS - 1, 1, None)
            tail_pe(pe, lambda: project_o(STEPS - 1, 1))

        @block.scalar
        def _(act):
            def split_k(n, par):
                act.wait_ge(s_wqk[par], load_count(n, par, 32))
                at_least(act, s_k, (n - 1) * KCH)
                nc.scalar.activation(wk_hi[:, par, :, :], wqk_raw[:, par, 1, :, :], ACT.Copy,
                                     scale=WS).then_inc(s_wkh, 1)

            def split_v(n, par):
                act.wait_ge(s_wv[par], load_count(n, par, 16))
                at_least(act, s_v, (n - 1) * KCH)
                nc.scalar.activation(wv_hi[:, par, :, :], wv_raw[:, par, :, :], ACT.Copy,
                                     scale=WS).then_inc(s_wvh, 1)

            def take_q(n, par):
                act.wait_ge(s_q, n + 1)
                for h in range(2):
                    for half in range(2):
                        i = nc.scalar.activation(q1[64 * half:64 * half + 64, par, h, :],
                                                 ps[64 * h:64 * h + 64, PM, 0:TQ], ACT.Copy)
                i.then_inc(s_qh, 1)

            def take_k(j, n, par):
                act.wait_ge(s_k, n * KCH + j + 1)
                for h in range(2):
                    rows = slice(64 * h, 64 * h + 64)
                    nc.scalar.activation(k1[rows, par, h, 512 * j:512 * (j + 1)], ps[rows, PK, :],
                                         ACT.Copy).then_inc(s_kh, 1)

            def take_v(j, n):
                act.wait_ge(s_v, n * KCH + j + 1)
                nc.scalar.activation(v_sb[:, j % NV, :, :],
                                     ps[:, PV, :].rearrange("p (t n) -> p t n", t=CS),
                                     ACT.Copy).then_inc(s_vc, 1)

            def take_max(n, par):
                act.wait_ge(s_mt, n + 1)
                nc.scalar.activation(q2[64:P, par, 0, :], ps[64:P, PM, 0:TQ], ACT.Copy,
                                     scale=1.0 / MS)
                nc.scalar.activation(q2[0:64, par, 1, :], ps[0:64, PM, 0:TQ], ACT.Copy,
                                     scale=1.0 / MS).then_inc(s_mr, 1)

            def context(u):
                b, _, _, keys = context_pair(u)
                for c in range(NC):
                    act.wait_ge(s_tp, 2 * u + c + 1)
                    i = nc.scalar.activation(ctx_hi[:, b, c, keys], ps[:, TURNED[c], :], ACT.Copy)
                    if c == 1:
                        if u >= 4:
                            act.wait_ge(s_tl[1], u - 3)
                        i = nc.scalar.activation(copies[:, u % 4, :], ps[:, TURNED[c], :], ACT.Copy)
                    i.then_inc(s_th, 1)

            def step(hp, b):
                n, more = step_of(hp, b), prepares(hp, b)
                for s in range(SLOTS):
                    g = slot_of(hp, b, s)
                    act.wait_ge(s_sc, g + 1)
                    at_least(act, s_pv, g - NP + 1)
                    if s % 2 == 0 and not (first_step(hp, b) and s < NP):
                        act.wait_ge(s_ps, summed(n, s - NP))
                    nc.scalar.activation(probs[:, s % NP, :, :],
                                         ps[:, SC + s % 2, :].rearrange("p (h q) -> p h q", h=2),
                                         ACT.Exp, scale=XSCALE).then_inc(s_exp, 1)
                    if s == M_AT and more:
                        take_max(n + 1, 1 - b)
                    if s == Q_AT and more:
                        take_q(n + 1, 1 - b)
                    if s in K_AT and more:
                        take_k(K_AT[s], n + 1, 1 - b)
                    if s in V_AT and V_AT[s]:
                        take_v(V_AT[s], n)
                    elif s in V_AT and more:
                        take_v(0, n + 1)
                    if s == SPLIT_K_AT and not (isinstance(hp, int) and hp == HP - 1):
                        split_k(n + 2, b)
                    if s == SPLIT_V_AT and more:
                        split_v(n + 1, 1 - b)
                    if s == ROOT_AT and not more:
                        root_of_variance(act, 1, slice(0, 2))
                    if s == XT_AT and not more:
                        take_batch(act, 0)
                    if s in TURN_AT and not more:
                        take_turned(act, TURN_AT[s])
                    if s in EXPERTS_AT and not more:
                        split_experts_high(act, EXPERTS_AT.index(s))

            root_of_variance(act, 0, slice(0, NT))
            for j in range(KCH + 1):
                if j < KCH:
                    context(2 * j)
                if j == 0:
                    act.wait_ge(s_xt, NC)
                    for c in range(NC):
                        nc.scalar.activation(xnT[:, c, :], ps[:, MX + c, :], ACT.Copy) \
                            .then_inc(s_xc, 1)
                    take_q(0, 0)
                    split_k(0, 0)
                if j == 3:
                    split_v(0, 0)
                if j == 4:
                    split_k(1, 1)
                if j == KCH:
                    take_v(0, 0)
                if j >= 1:
                    take_k(j - 1, 0, 0)
                if j < KCH:
                    context(2 * j + 1)
            take_max(0, 0)
            step(0, 0)
            step(0, 1)
            with act.Fori(1, HP - 1) as hp:
                step(hp, 0)
                step(hp, 1)
            step(HP - 1, 0)
            step(HP - 1, 1)
            tail_act(act)

        @block.vector
        def _(dve):
            def ln_link(instruction, count):
                instruction.then_inc(s_ln, 1)
                dve.wait_ge(s_ln, count)

            def variance(i, tiles):
                for t in range(NT)[tiles]:
                    last = nc.vector.bn_stats(stats[:, t, :], x_sb[:, t, :])
                ln_link(last, LN * i + 1)
                for t in range(NT)[tiles]:
                    last = nc.vector.bn_aggr(mv[:, t, :], stats[:, t, :])
                ln_link(last, LN * i + 2)
                nc.vector.tensor_scalar(var[:, tiles], mv[:, tiles, 1], EPS, None, ALU.add) \
                    .then_inc(s_ln, 1)

            def normalised(i, tiles):
                v, r, nw = var[:, tiles], rstd[:, tiles], newton[:, tiles]
                dve.wait_ge(s_ln, LN * i + 3)
                dve.wait_ge(s_sd, i + 1)
                ln_link(nc.vector.reciprocal(r, r), LN * i + 4)
                ln_link(nc.vector.tensor_tensor(nw, r, r, ALU.mult), LN * i + 5)
                ln_link(nc.vector.tensor_tensor(nw, nw, v, ALU.mult), LN * i + 6)
                ln_link(nc.vector.tensor_scalar(nw, nw, -0.5, 1.5, ALU.mult, ALU.add), LN * i + 7)
                ln_link(nc.vector.tensor_tensor(r, r, nw, ALU.mult), LN * i + 8)
                for t in range(NT)[tiles]:
                    last = nc.vector.tensor_scalar(xn[:, t, :], x_sb[:, t, :], mv[:, t, 0:1],
                                                   rstd[:, t:t + 1], ALU.subtract, ALU.mult)
                last.then_inc(s_ln, 1)

            def layernorm(i, tiles):
                variance(i, tiles)
                normalised(i, tiles)

            def low_part(lo, raw, hi):
                return nc.vector.scalar_tensor_tensor(
                    lo.rearrange("p c n -> p (c n)"), raw.rearrange("p c n -> p (c n)"), WS,
                    hi.rearrange("p c n -> p (c n)"), ALU.mult, ALU.subtract)

            def split_k(n, par):
                dve.wait_ge(s_wkh, n + 1)
                low_part(wk_lo[:, par, :, :], wqk_raw[:, par, 1, :, :], wk_hi[:, par, :, :]) \
                    .then_inc(s_wkl, 1)

            def split_v(n, par):
                dve.wait_ge(s_wvh, n + 1)
                low_part(wv_lo[:, par, :, :], wv_raw[:, par, :, :], wv_hi[:, par, :, :]) \
                    .then_inc(s_wvl, 1)

            def take_q(n, par):
                dve.wait_ge(s_qh, n + 1)
                for h in range(2):
                    rows = slice(64 * h, 64 * h + 64)
                    i = nc.vector.tensor_tensor(q2[rows, par, h, :], ps[rows, PM, 0:TQ],
                                                q1[rows, par, h, :], ALU.subtract)
                i.then_inc(s_ql, 1)

            def take_k(j, n, par):
                keys = slice(512 * j, 512 * (j + 1))
                for h in range(2):
                    dve.wait_ge(s_kh, n * (2 * KCH) + 2 * j + h + 1)
                    rows, other = slice(64 * h, 64 * h + 64), slice(64 - 64 * h, P - 64 * h)
                    i = nc.vector.tensor_tensor(k1[other, par, h, keys], ps[rows, PK, :],
                                                k1[rows, par, h, keys], ALU.subtract)
                i.then_inc(s_kl, 1)

            def maxima(u, n):
                j, t = divmod(u, 2)
                dve.wait_ge(s_mx, n * NU + u + 1)
                if u == 0:
                    at_least(dve, s_mn, n)
                bank = SC if isinstance(n, int) and n == 0 and t == 1 else MX
                nc.vector.tensor_reduce(m_part[:, j, t, :], ps[:, bank:bank + 2, :], AX.X, ALU.max) \
                    .then_inc(s_red, 1)

            def take_max(n):
                dve.wait_ge(s_red, n * NU + NU)
                at_least(dve, s_mt, n)
                nc.vector.tensor_reduce(m_neg[:, :, 0:P:64], m_part[:, :, :, :].rearrange(
                    "p j t h -> p t h j"), AX.X, ALU.max, negate=True).then_inc(s_mn, 1)

            def context(u):
                b, _, _, keys = context_pair(u)
                dve.wait_ge(s_th, 2 * u + 1)
                nc.vector.tensor_tensor(ctx_lo[:, b, 0, keys], ps[:, TURNED[0], :],
                                        ctx_hi[:, b, 0, keys], ALU.subtract).then_inc(s_tl[0], 1)

            def take_output(n, g):
                dve.wait_ge(s_pv, g + 1)
                at_least(dve, s_on, n)
                nc.vector.tensor_copy(o_raw[:, :], ps[:, ACC, 0:TQ]).then_inc(s_or, 1)

            def normalise(n):
                dve.wait_ge(s_sum, n + 1)
                nc.vector.reciprocal(o_rec[:, :], ps[:, PM, 0:TQ]).then_inc(s_rs, 1)
                dve.wait_ge(s_or, n + 1)
                dve.wait_ge(s_rs, n + 1)
                at_least(dve, s_yx, n)
                nc.vector.tensor_tensor(o_norm[:, :], o_raw[:, :], o_rec[:, :], ALU.mult) \
                    .then_inc(s_on, 1)

            def add_output(n, par):
                dve.wait_ge(s_yx, n + 1)
                at_least(dve, s_ya, n - 1)
                rows = x_sb[:, 2 * par:2 * par + 2, :].rearrange("p t c -> p (t c)")
                nc.vector.tensor_tensor(rows, rows, ps[:, PM, :], ALU.add).then_inc(s_ya, 1)

            def step(hp, b):
                n, more, first = step_of(hp, b), prepares(hp, b), first_step(hp, b)
                for s in range(SLOTS):
                    if s in MAX_AT and more:
                        maxima(MAX_AT[s], n + 1)
                    if s == max(MAX_AT) and more:
                        take_max(n + 1)
                    if s == 0 and not first:
                        take_output(n - 1, slot_of(hp, b, -1))
                    if s == Q_AT and more:
                        take_q(n + 1, 1 - b)
                    if s in K_AT and more:
                        take_k(K_AT[s], n + 1, 1 - b)
                    if s == SUM_AT and not first:
                        normalise(n - 1)
                    if s == Y_AT and not first:
                        add_output(n - 1, 1 - b)
                    if s == SPLIT_K_AT and not (isinstance(hp, int) and hp == HP - 1):
                        split_k(n + 2, b)
                    if s == SPLIT_V_AT and more:
                        split_v(n + 1, 1 - b)
                    if s == LN_AT and not more:
                        dve.wait_ge(s_ya, STEPS - 1)
                        layernorm(1, slice(0, 2))
                    if s in EXPERTS_AT and not more:
                        split_experts_low(dve, EXPERTS_AT.index(s))

            dve.wait_ge(s_x, 16)
            layernorm(0, slice(0, NT))
            nc.vector.memset(m_neg[:, :, :], 0.0).then_inc(s_mz, 1)
            dve.wait_ge(s_mz, 1)
            for j in range(KCH + 2):
                if j < KCH:
                    context(2 * j)
                if j == 0:
                    take_q(0, 0)
                    split_k(0, 0)
                if j == 3:
                    split_v(0, 0)
                if j == 4:
                    split_k(1, 1)
                if 1 <= j <= KCH:
                    take_k(j - 1, 0, 0)
                if j < KCH:
                    context(2 * j + 1)
                if j >= 2:
                    maxima(2 * (j - 2), 0)
                    maxima(2 * (j - 2) + 1, 0)
            take_max(0)
            dve.wait_ge(s_const, 5)
            row_vectors(dve)
            step(0, 0)
            step(0, 1)
            with dve.Fori(1, HP - 1) as hp:
                step(hp, 0)
                step(hp, 1)
            step(HP - 1, 0)
            step(HP - 1, 1)
            take_output(STEPS - 1, STEPS * SLOTS - 1)
            normalise(STEPS - 1)
            add_output(STEPS - 1, 1)
            dve.wait_ge(s_ya, STEPS)
            tail_dve(dve, variance, normalised)

        @block.gpsimd
        def _(pool):
            nc.gpsimd.memset(ident[:, :], 0.0).then_inc(s_const, 1)
            nc.gpsimd.memset(sixteen[:, :], WS).then_inc(s_const, 1)
            pool.wait_ge(s_const, 2)
            nc.gpsimd.affine_select(out=ident[:, :], in_=ident[:, :], compare_op=ALU.not_equal,
                                    fill=1.0, base=0, pattern=[[-1, P]], channel_multiplier=1) \
                .then_inc(s_const, 1)
            def rows_beside(h):
                nc.gpsimd.memset(k2[64 - 64 * h:P - 64 * h, :, h, :], MS).then_inc(s_const, 1)

            pool.wait_ge(s_const, 3)
            rows_beside(0)
            pool.wait_ge(s_const, 4)
            for u in range(2 * KCH):
                b, _, _, keys = context_pair(u)
                pool.wait_ge(s_th, 2 * u + 2)
                nc.gpsimd.tensor_tensor(ctx_lo[:, b, 1, keys], copies[:, u % 4, :],
                                        ctx_hi[:, b, 1, keys], ALU.subtract).then_inc(s_tl[1], 1)
            pool.wait_ge(s_tl[1], 2 * KCH)
            rows_beside(1)
            pool.wait_ge(s_const, 5)
            tail_constants(pool)

            def step(hp, b):
                n = step_of(hp, b)
                total = psums[:, b, :, :, :].rearrange("p k h q -> p (k h q)")
                pairs = [probs[:, i:i + 2, :, :].rearrange("p k h q -> p (k h q)")
                         for i in range(0, NP, 2)]
                for s in range(3, SLOTS, 2):
                    if s == 5 and not prepares(hp, b):
                        zero_rows(pool)
                    pool.wait_ge(s_exp, slot_of(hp, b, s) + 1)
                    if s == 3:
                        at_least(pool, s_sum, n - 1)
                    else:
                        pool.wait_ge(s_ps, summed(n, s - 2))
                    nc.gpsimd.tensor_tensor(total, pairs[0] if s == 3 else total,
                                            pairs[s // 2 % (NP // 2)], ALU.add).then_inc(s_ps, 1)

            step(0, 0)
            step(0, 1)
            with pool.Fori(1, HP - 1) as hp:
                step(hp, 0)
                step(hp, 1)
            step(HP - 1, 0)
            step(HP - 1, 1)
            tail_pool(pool)


_INS = ["x", "ctx_1024", "L0_xattn_w_q", "L0_xattn_w_k", "L0_xattn_w_v", "L0_xattn_w_o", "L0_attn_wq",
        "L0_attn_wk", "L0_attn_wv", "L0_attn_wo", "L0_ffn_Wg", "L0_ffn_bg", "L0_ffn_W1", "L0_ffn_b1",
        "L0_ffn_W2", "L0_ffn_b2"]


def kernel(**inputs):
    import numpy as _np
    import concourse.bacc as _bacc
    from concourse import mybir as _mybir
    from concourse.bass_utils import run_bass_kernel_spmd as _run

    nc = _bacc.Bacc("TRN2", target_bir_lowering=False, num_devices=1)
    arrays, args = {}, []
    for name in _INS:
        a = _np.ascontiguousarray(inputs[name])
        arrays[f"in_{name}_dram"] = a
        args.append(nc.dram_tensor(f"in_{name}_dram", a.shape, _mybir.dt.from_np(a.dtype),
                                   kind="ExternalInput").ap())
    args.append(nc.dram_tensor("out_0_dram", (B, TQ, D), FP32, kind="ExternalOutput").ap())
    perceiver(nc, *args)
    r = _run(nc, [arrays], core_ids=[0])
    return r.results[0]["out_0_dram"]
```
